# Optimizing a Trainium2 kernel written in Bass

```python
import numpy as np
import jax
import jax.numpy as jnp

def _softmax(x, axis=-1):
    return jax.nn.softmax(x, axis=axis)

def _gelu(x):
    return jax.nn.gelu(x, approximate=True)

def _silu(x):
    return jax.nn.silu(x)

def _sigmoid(x):
    return jax.nn.sigmoid(x)

def _layernorm(x, axis=-1, eps=1e-05):
    m = jnp.mean(x, axis=axis, keepdims=True)
    v = jnp.var(x, axis=axis, keepdims=True)
    return (x - m) / jnp.sqrt(v + eps)

def _scatter_add(tgt, idx, src, axis=0):
    return tgt.at[idx].add(src)

def _segment_sum(src, seg, n):
    return jax.ops.segment_sum(src, seg, n)
kernel_name = 'mk_audio_tower_d4_tok_audfeat256_r4_5cafc8'

def setup_inputs(seed: int=0):
    np.random.seed(seed)
    _w = jnp.asarray

    def _rec_inputs():
        import jax
        import jax.numpy as jnp
        _rk = jax.random.key(seed)
        x = -0.00040386 + 0.999972 * jax.random.normal(jax.random.fold_in(_rk, 1), (16, 1536, 64), jnp.float32)
        return x
    x = _rec_inputs()

    def _L0_tok_setup():
        import jax, jax.numpy as jnp
        import numpy as np
        LN_EPS = 1e-05
        key = jax.random.key(seed)
        ks = jax.random.split(key, 8)
        dim = 64
        b, n3 = (8, 1536)
        s = 0.02
        return {'x': jax.random.normal(ks[0], (b, n3, dim), jnp.float32), 'ln_g': jnp.ones((dim,), jnp.float32), 'ln_b': jnp.zeros((dim,), jnp.float32), 'Wq': jax.random.normal(ks[1], (dim, dim), jnp.float32) * s, 'bq': jax.random.normal(ks[2], (dim,), jnp.float32) * s, 'Wk': jax.random.normal(ks[3], (dim, dim), jnp.float32) * s, 'bk': jax.random.normal(ks[4], (dim,), jnp.float32) * s, 'Wv': jax.random.normal(ks[5], (dim, dim), jnp.float32) * s, 'bv': jax.random.normal(ks[6], (dim,), jnp.float32) * s, 'Wo': jax.random.normal(ks[7], (dim, dim), jnp.float32) * s, 'bo': jnp.zeros((dim,), jnp.float32), 'heads': 8}
    _L0_tok_all = _L0_tok_setup()
    _L0_tok_in = {k: v for k, v in _L0_tok_all.items() if k in ('ln_g', 'ln_b', 'Wq', 'bq', 'Wk', 'bk', 'Wv', 'bv', 'Wo', 'bo')}
    del _L0_tok_all

    def _L0_attn_setup():
        import jax, jax.numpy as jnp
        import numpy as np
        B_, L, D = (8, 512, 64)
        EXP, NST, DCONV = (128, 16, 4)
        SPARSITY = 0.3
        key = jax.random.key(seed)
        ks = jax.random.split(key, 16)
        r = lambda k, shape, s=0.02: jax.random.normal(k, shape, dtype=jnp.float32) * s
        return {'x': jax.random.normal(ks[0], (B_, L, D), dtype=jnp.float32), 'alpha': jnp.ones((1,), jnp.float32) * 0.5, 'dyt_w': jnp.ones((D,), jnp.float32), 'dyt_b': jnp.zeros((D,), jnp.float32), 'w_in': r(ks[1], (EXP, D)), 'b_in': r(ks[2], (EXP,)), 'w_q': r(ks[3], (1, EXP)), 'b_q': r(ks[4], (1,)), 'w_k': r(ks[5], (1, EXP)), 'b_k': r(ks[6], (1,)), 'A': r(ks[7], (NST, NST)), 'Bp': r(ks[8], (1, 1, NST)), 'Cp': r(ks[9], (EXP, NST)), 'conv_w': r(ks[10], (EXP, 1, DCONV)), 'w_out': r(ks[11], (D, EXP)), 'b_out': r(ks[12], (D,))}
    _L0_attn_all = _L0_attn_setup()
    _L0_attn_in = {k: v for k, v in _L0_attn_all.items() if k in ('alpha', 'dyt_w', 'dyt_b', 'w_in', 'b_in', 'w_q', 'b_q', 'w_k', 'b_k', 'A', 'Bp', 'Cp', 'conv_w', 'w_out', 'b_out')}
    del _L0_attn_all

    def _L0_ffn_setup():
        import jax, jax.numpy as jnp
        import numpy as np
        B, A = (1024, 8)
        IN, OUT = (64, 64)
        SH1, SH2 = (64, 128)
        EH1, EH2 = (128, 64)
        E, TOPK = (4, 2)

        def _shared_mlp(x, W1, b1, W2, b2, W3, b3):
            h = jax.nn.relu(x @ W1 + b1)
            h = jax.nn.relu(h @ W2 + b2)
            return h @ W3 + b3

        def _experts_mlp(x, eW1, eb1, eW2, eb2, eW3, eb3):
            h = jax.nn.relu(jnp.einsum('baf,efh->ebah', x, eW1) + eb1[:, None, None, :])
            h = jax.nn.relu(jnp.einsum('ebah,ehg->ebag', h, eW2) + eb2[:, None, None, :])
            o = jnp.einsum('ebag,ego->ebao', h, eW3) + eb3[:, None, None, :]
            return jnp.moveaxis(o, 0, -1)
        key = jax.random.key(seed)
        ks = jax.random.split(key, 16)
        s = 0.05
        return {'x': jax.random.normal(ks[0], (B, A, IN), jnp.float32), 'sW1': jax.random.normal(ks[1], (IN, SH1), jnp.float32) * s, 'sb1': jnp.zeros((SH1,), jnp.float32), 'sW2': jax.random.normal(ks[2], (SH1, SH2), jnp.float32) * s, 'sb2': jnp.zeros((SH2,), jnp.float32), 'sW3': jax.random.normal(ks[3], (SH2, OUT), jnp.float32) * s, 'sb3': jnp.zeros((OUT,), jnp.float32), 'eW1': jax.random.normal(ks[4], (E, IN, EH1), jnp.float32) * s, 'eb1': jnp.zeros((E, EH1), jnp.float32), 'eW2': jax.random.normal(ks[5], (E, EH1, EH2), jnp.float32) * s, 'eb2': jnp.zeros((E, EH2), jnp.float32), 'eW3': jax.random.normal(ks[6], (E, EH2, OUT), jnp.float32) * s, 'eb3': jnp.zeros((E, OUT), jnp.float32), 'gW': jax.random.normal(ks[7], (IN, E), jnp.float32) * s, 'gb': jnp.zeros((E,), jnp.float32)}
    _L0_ffn_all = _L0_ffn_setup()
    _L0_ffn_in = {k: v for k, v in _L0_ffn_all.items() if k in ('sW1', 'sb1', 'sW2', 'sb2', 'sW3', 'sb3', 'eW1', 'eb1', 'eW2', 'eb2', 'eW3', 'eb3', 'gW', 'gb')}
    del _L0_ffn_all

    def _L1_attn_setup():
        import jax, jax.numpy as jnp
        import numpy as np
        NUM_HEADS = 8
        DIM = 64
        key = jax.random.key(seed)
        k1, k2, k3, k4 = jax.random.split(key, 4)
        B, N, C = (2, 1024, DIM)
        x = jax.random.normal(k1, (B, N, C), dtype=jnp.float32)
        w_qkv = jax.random.normal(k2, (3 * C, C), dtype=jnp.float32) * C ** (-0.5)
        w_proj = jax.random.normal(k3, (C, C), dtype=jnp.float32) * C ** (-0.5)
        b_proj = jax.random.normal(k4, (C,), dtype=jnp.float32) * 0.01
        temperature = jnp.ones((1,), dtype=jnp.float32)
        return {'x': x, 'w_qkv': w_qkv, 'w_proj': w_proj, 'b_proj': b_proj, 'temperature': temperature}
    _L1_attn_all = _L1_attn_setup()
    _L1_attn_in = {k: v for k, v in _L1_attn_all.items() if k in ('w_qkv', 'w_proj', 'b_proj', 'temperature')}
    del _L1_attn_all

    def _L1_ffn_setup():
        import jax, jax.numpy as jnp
        import numpy as np
        E = 8
        K = 2
        D = 64
        H = 128
        DOUT = 64
        EPS = 1e-05
        key = jax.random.key(seed)
        ks = jax.random.split(key, 9)
        s = 0.02
        return {'x': jax.random.normal(ks[0], (4, 2048, D), jnp.float32), 'gamma': 1.0 + 0.05 * jax.random.normal(ks[1], (D,), jnp.float32), 'beta': 0.05 * jax.random.normal(ks[2], (D,), jnp.float32), 'Wr': 0.01 * jax.random.normal(ks[3], (D, E), jnp.float32), 'br': jnp.zeros((E,), jnp.float32), 'W1': s * jax.random.normal(ks[4], (E, D, H), jnp.float32), 'b1': s * jax.random.normal(ks[5], (E, H), jnp.float32), 'W2': s * jax.random.normal(ks[6], (E, H, DOUT), jnp.float32), 'b2': s * jax.random.normal(ks[7], (E, DOUT), jnp.float32)}
    _L1_ffn_all = _L1_ffn_setup()
    _L1_ffn_in = {k: v for k, v in _L1_ffn_all.items() if k in ('gamma', 'beta', 'Wr', 'br', 'W1', 'b1', 'W2', 'b2')}
    del _L1_ffn_all

    def _L2_attn_setup():
        import jax, jax.numpy as jnp
        import numpy as np
        import math
        DIM = 64
        key = jax.random.key(seed)
        kx, kq, kk, kv = jax.random.split(key, 4)
        B, N, D = (2, 2048, DIM)
        x = jax.random.normal(kx, (B, N, D), dtype=jnp.float32)
        s = 1.0 / math.sqrt(D)
        Wq = jax.random.uniform(kq, (D, D), dtype=jnp.float32, minval=-s, maxval=s)
        Wk = jax.random.uniform(kk, (D, D), dtype=jnp.float32, minval=-s, maxval=s)
        Wv = jax.random.uniform(kv, (D, D), dtype=jnp.float32, minval=-s, maxval=s)
        return {'x': x, 'Wq': Wq, 'Wk': Wk, 'Wv': Wv}
    _L2_attn_all = _L2_attn_setup()
    _L2_attn_in = {k: v for k, v in _L2_attn_all.items() if k in ('Wq', 'Wk', 'Wv')}
    del _L2_attn_all

    def _L2_ffn_setup():
        import jax, jax.numpy as jnp
        import numpy as np
        B, T, C = (64, 96, 64)
        NH, NKV = (4, 2)
        HD = C // NH
        NREP = NH // NKV
        NE, TOPK = (8, 2)
        HID = int(8 / 3 * C)
        EPS_RMS = 1e-06

        def _rope_tables(t_len):
            inv_freq = 1.0 / 10000.0 ** (np.arange(0, HD, 2, dtype=np.float32) / HD)
            t = np.arange(t_len, dtype=np.float32)
            freqs = np.outer(t, inv_freq)
            emb = np.concatenate([freqs, freqs], axis=-1)
            return (jnp.asarray(np.cos(emb)), jnp.asarray(np.sin(emb)))

        def _rotate_half(x):
            h = x.shape[-1] // 2
            return jnp.concatenate([-x[..., h:], x[..., :h]], axis=-1)

        def _rmsnorm(v, w):
            return v * jax.lax.rsqrt(jnp.mean(v * v, axis=-1, keepdims=True) + EPS_RMS) * w
        key = jax.random.key(seed)
        ks = jax.random.split(key, 10)
        s = lambda k, shape: jax.random.normal(k, shape, jnp.float32) * 0.02
        return {'x': jax.random.normal(ks[0], (B, T, C), jnp.float32), 'ln1_w': jnp.ones((C,), jnp.float32), 'ln2_w': jnp.ones((C,), jnp.float32), 'wq': s(ks[1], (NH * HD, C)), 'wk': s(ks[2], (NKV * HD, C)), 'wv': s(ks[3], (NKV * HD, C)), 'wo': s(ks[4], (C, C)), 'router_w': s(ks[5], (NE, C)), 'w1': s(ks[6], (NE, HID, C)), 'w2': s(ks[7], (NE, C, HID)), 'w3': s(ks[8], (NE, HID, C))}
    _L2_ffn_all = _L2_ffn_setup()
    _L2_ffn_in = {k: v for k, v in _L2_ffn_all.items() if k in ('ln1_w', 'ln2_w', 'wq', 'wk', 'wv', 'wo', 'router_w', 'w1', 'w2', 'w3')}
    del _L2_ffn_all

    def _L3_attn_setup():
        import jax, jax.numpy as jnp
        import numpy as np
        B, N, D = (4, 1024, 64)
        key = jax.random.key(seed)
        ks = jax.random.split(key, 7)

        def xavier(k, shape):
            fan_in, fan_out = (shape[1], shape[0])
            a = jnp.sqrt(6.0 / (fan_in + fan_out))
            return jax.random.uniform(k, shape, jnp.float32, -a, a)
        return {'x': jax.random.normal(ks[0], (B, N, D), jnp.float32), 'Wq': xavier(ks[1], (D, D)), 'bq': jnp.zeros((D,), jnp.float32), 'Wk': xavier(ks[2], (D, D)), 'bk': jnp.zeros((D,), jnp.float32), 'Wv': xavier(ks[3], (D, D)), 'bv': jnp.zeros((D,), jnp.float32), 'scale': jnp.asarray([jnp.sqrt(jnp.float32(D))])}
    _L3_attn_all = _L3_attn_setup()
    _L3_attn_in = {k: v for k, v in _L3_attn_all.items() if k in ('Wq', 'bq', 'Wk', 'bk', 'Wv', 'bv', 'scale')}
    del _L3_attn_all

    def _L3_ffn_setup():
        import jax, jax.numpy as jnp
        import numpy as np
        B, S, H, F, E, K = (8, 1024, 64, 128, 16, 2)
        EPS = 1e-05
        key = jax.random.key(seed)
        ks = jax.random.split(key, 9)
        sc = 0.02
        return {'x': jax.random.normal(ks[0], (B, S, H), dtype=jnp.float32), 'gate_w': jax.random.normal(ks[1], (H, E), dtype=jnp.float32) * sc, 'gate_b': jnp.zeros((E,), dtype=jnp.float32), 'w1': jax.random.normal(ks[2], (E, H, F), dtype=jnp.float32) * sc, 'b1': jnp.zeros((E, F), dtype=jnp.float32), 'w2': jax.random.normal(ks[3], (E, F, H), dtype=jnp.float32) * sc, 'b2': jnp.zeros((E, H), dtype=jnp.float32), 'gamma': jnp.ones((H,), dtype=jnp.float32), 'beta': jnp.zeros((H,), dtype=jnp.float32)}
    _L3_ffn_all = _L3_ffn_setup()
    _L3_ffn_in = {k: v for k, v in _L3_ffn_all.items() if k in ('gate_w', 'gate_b', 'w1', 'b1', 'w2', 'b2', 'gamma', 'beta')}
    del _L3_ffn_all
    return {'x': x, 'L0_tok_ln_g': _L0_tok_in['ln_g'], 'L0_tok_ln_b': _L0_tok_in['ln_b'], 'L0_tok_Wq': _L0_tok_in['Wq'], 'L0_tok_bq': _L0_tok_in['bq'], 'L0_tok_Wk': _L0_tok_in['Wk'], 'L0_tok_bk': _L0_tok_in['bk'], 'L0_tok_Wv': _L0_tok_in['Wv'], 'L0_tok_bv': _L0_tok_in['bv'], 'L0_tok_Wo': _L0_tok_in['Wo'], 'L0_tok_bo': _L0_tok_in['bo'], 'L0_attn_alpha': _L0_attn_in['alpha'], 'L0_attn_dyt_w': _L0_attn_in['dyt_w'], 'L0_attn_dyt_b': _L0_attn_in['dyt_b'], 'L0_attn_w_in': _L0_attn_in['w_in'], 'L0_attn_b_in': _L0_attn_in['b_in'], 'L0_attn_w_q': _L0_attn_in['w_q'], 'L0_attn_b_q': _L0_attn_in['b_q'], 'L0_attn_w_k': _L0_attn_in['w_k'], 'L0_attn_b_k': _L0_attn_in['b_k'], 'L0_attn_A': _L0_attn_in['A'], 'L0_attn_Bp': _L0_attn_in['Bp'], 'L0_attn_Cp': _L0_attn_in['Cp'], 'L0_attn_conv_w': _L0_attn_in['conv_w'], 'L0_attn_w_out': _L0_attn_in['w_out'], 'L0_attn_b_out': _L0_attn_in['b_out'], 'L0_ffn_sW1': _L0_ffn_in['sW1'], 'L0_ffn_sb1': _L0_ffn_in['sb1'], 'L0_ffn_sW2': _L0_ffn_in['sW2'], 'L0_ffn_sb2': _L0_ffn_in['sb2'], 'L0_ffn_sW3': _L0_ffn_in['sW3'], 'L0_ffn_sb3': _L0_ffn_in['sb3'], 'L0_ffn_eW1': _L0_ffn_in['eW1'], 'L0_ffn_eb1': _L0_ffn_in['eb1'], 'L0_ffn_eW2': _L0_ffn_in['eW2'], 'L0_ffn_eb2': _L0_ffn_in['eb2'], 'L0_ffn_eW3': _L0_ffn_in['eW3'], 'L0_ffn_eb3': _L0_ffn_in['eb3'], 'L0_ffn_gW': _L0_ffn_in['gW'], 'L0_ffn_gb': _L0_ffn_in['gb'], 'L1_attn_w_qkv': _L1_attn_in['w_qkv'], 'L1_attn_w_proj': _L1_attn_in['w_proj'], 'L1_attn_b_proj': _L1_attn_in['b_proj'], 'L1_attn_temperature': _L1_attn_in['temperature'], 'L1_ffn_gamma': _L1_ffn_in['gamma'], 'L1_ffn_beta': _L1_ffn_in['beta'], 'L1_ffn_Wr': _L1_ffn_in['Wr'], 'L1_ffn_br': _L1_ffn_in['br'], 'L1_ffn_W1': _L1_ffn_in['W1'], 'L1_ffn_b1': _L1_ffn_in['b1'], 'L1_ffn_W2': _L1_ffn_in['W2'], 'L1_ffn_b2': _L1_ffn_in['b2'], 'L2_attn_Wq': _L2_attn_in['Wq'], 'L2_attn_Wk': _L2_attn_in['Wk'], 'L2_attn_Wv': _L2_attn_in['Wv'], 'L2_ffn_ln1_w': _L2_ffn_in['ln1_w'], 'L2_ffn_ln2_w': _L2_ffn_in['ln2_w'], 'L2_ffn_wq': _L2_ffn_in['wq'], 'L2_ffn_wk': _L2_ffn_in['wk'], 'L2_ffn_wv': _L2_ffn_in['wv'], 'L2_ffn_wo': _L2_ffn_in['wo'], 'L2_ffn_router_w': _L2_ffn_in['router_w'], 'L2_ffn_w1': _L2_ffn_in['w1'], 'L2_ffn_w2': _L2_ffn_in['w2'], 'L2_ffn_w3': _L2_ffn_in['w3'], 'L3_attn_Wq': _L3_attn_in['Wq'], 'L3_attn_bq': _L3_attn_in['bq'], 'L3_attn_Wk': _L3_attn_in['Wk'], 'L3_attn_bk': _L3_attn_in['bk'], 'L3_attn_Wv': _L3_attn_in['Wv'], 'L3_attn_bv': _L3_attn_in['bv'], 'L3_attn_scale': _L3_attn_in['scale'], 'L3_ffn_gate_w': _L3_ffn_in['gate_w'], 'L3_ffn_gate_b': _L3_ffn_in['gate_b'], 'L3_ffn_w1': _L3_ffn_in['w1'], 'L3_ffn_b1': _L3_ffn_in['b1'], 'L3_ffn_w2': _L3_ffn_in['w2'], 'L3_ffn_b2': _L3_ffn_in['b2'], 'L3_ffn_gamma': _L3_ffn_in['gamma'], 'L3_ffn_beta': _L3_ffn_in['beta']}

def reference(x, L0_tok_ln_g, L0_tok_ln_b, L0_tok_Wq, L0_tok_bq, L0_tok_Wk, L0_tok_bk, L0_tok_Wv, L0_tok_bv, L0_tok_Wo, L0_tok_bo, L0_attn_alpha, L0_attn_dyt_w, L0_attn_dyt_b, L0_attn_w_in, L0_attn_b_in, L0_attn_w_q, L0_attn_b_q, L0_attn_w_k, L0_attn_b_k, L0_attn_A, L0_attn_Bp, L0_attn_Cp, L0_attn_conv_w, L0_attn_w_out, L0_attn_b_out, L0_ffn_sW1, L0_ffn_sb1, L0_ffn_sW2, L0_ffn_sb2, L0_ffn_sW3, L0_ffn_sb3, L0_ffn_eW1, L0_ffn_eb1, L0_ffn_eW2, L0_ffn_eb2, L0_ffn_eW3, L0_ffn_eb3, L0_ffn_gW, L0_ffn_gb, L1_attn_w_qkv, L1_attn_w_proj, L1_attn_b_proj, L1_attn_temperature, L1_ffn_gamma, L1_ffn_beta, L1_ffn_Wr, L1_ffn_br, L1_ffn_W1, L1_ffn_b1, L1_ffn_W2, L1_ffn_b2, L2_attn_Wq, L2_attn_Wk, L2_attn_Wv, L2_ffn_ln1_w, L2_ffn_ln2_w, L2_ffn_wq, L2_ffn_wk, L2_ffn_wv, L2_ffn_wo, L2_ffn_router_w, L2_ffn_w1, L2_ffn_w2, L2_ffn_w3, L3_attn_Wq, L3_attn_bq, L3_attn_Wk, L3_attn_bk, L3_attn_Wv, L3_attn_bv, L3_attn_scale, L3_ffn_gate_w, L3_ffn_gate_b, L3_ffn_w1, L3_ffn_b1, L3_ffn_w2, L3_ffn_b2, L3_ffn_gamma, L3_ffn_beta):
    import jax
    import jax.numpy as jnp

    def _L0_tok_ref(x, ln_g, ln_b, Wq, bq, Wk, bk, Wv, bv, Wo, bo, heads):
        import jax, jax.numpy as jnp
        import numpy as np
        LN_EPS = 1e-05
        dim = x.shape[-1]
        scale = dim ** (-0.5)
        d = dim // heads

        def cross_attn(xcat):
            mu = jnp.mean(xcat, axis=-1, keepdims=True)
            var = jnp.mean(jnp.square(xcat - mu), axis=-1, keepdims=True)
            xn = (xcat - mu) * jax.lax.rsqrt(var + LN_EPS) * ln_g + ln_b
            x1, x2 = jnp.split(xn, 2, axis=0)
            q = x1 @ Wq.T + bq
            k = x2 @ Wk.T + bk
            v = x2 @ Wv.T + bv
            b_, n_ = (q.shape[0], q.shape[1])
            q = q.reshape(b_, n_, heads, d).transpose(0, 2, 1, 3)
            k = k.reshape(b_, n_, heads, d).transpose(0, 2, 1, 3)
            v = v.reshape(b_, n_, heads, d).transpose(0, 2, 1, 3)
            dots = jnp.einsum('bhid,bhjd->bhij', q, k) * scale
            attn = jax.nn.softmax(dots, axis=-1)
            out = jnp.einsum('bhij,bhjd->bhid', attn, v)
            out = out.transpose(0, 2, 1, 3).reshape(b_, n_, dim)
            return out @ Wo.T + bo
        x_origin, x_emap, x_lbp = jnp.split(x, 3, axis=1)
        out_oe = cross_attn(jnp.concatenate((x_origin, x_emap), axis=0))
        out_ol = cross_attn(jnp.concatenate((x_origin, x_lbp), axis=0))
        return out_oe + out_ol

    def _L0_attn_ref(x, alpha, dyt_w, dyt_b, w_in, b_in, w_q, b_q, w_k, b_k, A, Bp, Cp, conv_w, w_out, b_out):
        import jax, jax.numpy as jnp
        import numpy as np
        B_, L, D = (8, 512, 64)
        EXP, NST, DCONV = (128, 16, 4)
        SPARSITY = 0.3
        B, Lx, Dx = x.shape
        residual = x
        xn = jnp.tanh(alpha * x) * dyt_w + dyt_b
        xp = xn @ w_in.T + b_in
        nrm = jnp.maximum(jnp.linalg.norm(xp, axis=-1, keepdims=True), 1e-12)
        xpn = xp / nrm
        Q = xpn @ w_q.T + b_q
        K = xpn @ w_k.T + b_k
        kd = w_q.shape[0]
        scores = jnp.einsum('blk,bmk->blm', Q, K) * kd ** (-0.5)
        aw = jax.nn.softmax(scores, axis=-1)
        imp = aw.mean(axis=1)
        k = max(1, int(Lx * SPARSITY))
        _, topk_idx = jax.lax.top_k(imp, k)
        x_sparse = jnp.take_along_axis(xpn, topk_idx[:, :, None], axis=1)
        E = x_sparse.shape[-1]
        lhs = jnp.transpose(x_sparse, (0, 2, 1))
        conv = jax.lax.conv_general_dilated(lhs, conv_w, window_strides=(1,), padding=[(DCONV - 1, DCONV - 1)], dimension_numbers=('NCH', 'OIH', 'NCH'), feature_group_count=E)
        conv = conv[:, :, :Lx]
        x_conv = jnp.transpose(conv, (0, 2, 1))[:, :k]
        sigB = jax.nn.sigmoid(Bp)[0, 0]
        sigC = jax.nn.sigmoid(Cp)

        def step(h, xt):
            h = jnp.einsum('ben,mn->bem', h, A) + sigB * xt[:, :, None]
            out = jnp.einsum('ben,en->be', h, sigC)
            return (h, out)
        h0 = jnp.zeros((B, E, NST), x.dtype)
        _, outs = jax.lax.scan(step, h0, jnp.transpose(x_conv, (1, 0, 2)))
        x_proc = jnp.transpose(outs, (1, 0, 2))
        x_proc = x_proc @ w_out.T + b_out
        out = jnp.zeros((B, Lx, Dx), x.dtype)
        out = out.at[jnp.arange(B)[:, None], topk_idx].set(x_proc)
        return out + residual

    def _L0_ffn_ref(x, sW1, sb1, sW2, sb2, sW3, sb3, eW1, eb1, eW2, eb2, eW3, eb3, gW, gb):
        import jax, jax.numpy as jnp
        import numpy as np
        B, A = (1024, 8)
        IN, OUT = (64, 64)
        SH1, SH2 = (64, 128)
        EH1, EH2 = (128, 64)
        E, TOPK = (4, 2)

        def _shared_mlp(x, W1, b1, W2, b2, W3, b3):
            h = jax.nn.relu(x @ W1 + b1)
            h = jax.nn.relu(h @ W2 + b2)
            return h @ W3 + b3

        def _experts_mlp(x, eW1, eb1, eW2, eb2, eW3, eb3):
            h = jax.nn.relu(jnp.einsum('baf,efh->ebah', x, eW1) + eb1[:, None, None, :])
            h = jax.nn.relu(jnp.einsum('ebah,ehg->ebag', h, eW2) + eb2[:, None, None, :])
            o = jnp.einsum('ebag,ego->ebao', h, eW3) + eb3[:, None, None, :]
            return jnp.moveaxis(o, 0, -1)
        all_out = _experts_mlp(x, eW1, eb1, eW2, eb2, eW3, eb3)
        shared = _shared_mlp(x, sW1, sb1, sW2, sb2, sW3, sb3)
        gates = jax.nn.softmax(x @ gW + gb, axis=-1)
        topv, topi = jax.lax.top_k(gates, TOPK)
        topw = jax.nn.softmax(topv, axis=-1)
        sel = jnp.take_along_axis(all_out, topi[:, :, None, :], axis=-1)
        gated = jnp.sum(sel * topw[:, :, None, :], axis=-1)
        return shared + gated

    def _L1_attn_ref(x, w_qkv, w_proj, b_proj, temperature):
        import jax, jax.numpy as jnp
        import numpy as np
        NUM_HEADS = 8
        DIM = 64
        B, N, C = x.shape
        H = NUM_HEADS
        d = C // H
        scale = C ** (-0.5)
        qkv = (x @ w_qkv.T).reshape(B, N, 3, H, d).transpose(2, 0, 3, 1, 4)
        q, k, v = (qkv[0], qkv[1], qkv[2])
        attn = jnp.einsum('bhnd,bhmd->bhnm', q, k) * scale
        diag_mask = jnp.eye(N, dtype=attn.dtype) * jnp.asarray(-1000000000.0, attn.dtype)
        attn = attn - diag_mask
        attn = jax.nn.softmax(attn / temperature[0], axis=-1)
        out = jnp.einsum('bhnm,bhmd->bhnd', attn, v)
        out = out.transpose(0, 2, 1, 3).reshape(B, N, C)
        return out @ w_proj.T + b_proj

    def _L1_ffn_ref(x, gamma, beta, Wr, br, W1, b1, W2, b2):
        import jax, jax.numpy as jnp
        import numpy as np
        E = 8
        K = 2
        D = 64
        H = 128
        DOUT = 64
        EPS = 1e-05
        mu = jnp.mean(x, axis=-1, keepdims=True)
        var = jnp.mean(jnp.square(x - mu), axis=-1, keepdims=True)
        xn = (x - mu) * jax.lax.rsqrt(var + EPS) * gamma + beta
        logits = jnp.einsum('bsd,de->bse', xn, Wr) + br
        top_vals, top_idx = jax.lax.top_k(logits, K)
        w = jax.nn.softmax(top_vals, axis=-1)
        w_full = jnp.einsum('bsk,bske->bse', w, jax.nn.one_hot(top_idx, E, dtype=w.dtype))
        y = jnp.zeros(x.shape[:-1] + (DOUT,), x.dtype)
        for e in range(E):
            h = jax.nn.gelu(jnp.einsum('bsd,dh->bsh', xn, W1[e]) + b1[e], approximate=False)
            y_e = jnp.einsum('bsh,hd->bsd', h, W2[e]) + b2[e]
            y = y + y_e * w_full[..., e, None]
        return y

    def _L2_attn_ref(x, Wq, Wk, Wv):
        import jax, jax.numpy as jnp
        import numpy as np
        import math
        DIM = 64
        Q = jnp.einsum('bnd,ed->bne', x, Wq)
        K = jnp.einsum('bnd,ed->bne', x, Wk)
        V = jnp.einsum('bnd,ed->bne', x, Wv)
        D = x.shape[-1]
        scores = jnp.einsum('bqd,bkd->bqk', Q, K) / jnp.sqrt(jnp.float32(D))
        attn = jax.nn.softmax(scores, axis=1)
        out = jnp.einsum('bqk,bkd->bqd', attn, V)
        return out

    def _L2_ffn_ref(x, ln1_w, ln2_w, wq, wk, wv, wo, router_w, w1, w2, w3):
        import jax, jax.numpy as jnp
        import numpy as np
        B, T, C = (64, 96, 64)
        NH, NKV = (4, 2)
        HD = C // NH
        NREP = NH // NKV
        NE, TOPK = (8, 2)
        HID = int(8 / 3 * C)
        EPS_RMS = 1e-06

        def _rope_tables(t_len):
            inv_freq = 1.0 / 10000.0 ** (np.arange(0, HD, 2, dtype=np.float32) / HD)
            t = np.arange(t_len, dtype=np.float32)
            freqs = np.outer(t, inv_freq)
            emb = np.concatenate([freqs, freqs], axis=-1)
            return (jnp.asarray(np.cos(emb)), jnp.asarray(np.sin(emb)))

        def _rotate_half(x):
            h = x.shape[-1] // 2
            return jnp.concatenate([-x[..., h:], x[..., :h]], axis=-1)

        def _rmsnorm(v, w):
            return v * jax.lax.rsqrt(jnp.mean(v * v, axis=-1, keepdims=True) + EPS_RMS) * w
        Bx, Tx, Cx = x.shape
        h = _rmsnorm(x, ln1_w)
        q = (h @ wq.T).reshape(Bx, Tx, NH, HD).transpose(0, 2, 1, 3)
        k = (h @ wk.T).reshape(Bx, Tx, NKV, HD).transpose(0, 2, 1, 3)
        v = (h @ wv.T).reshape(Bx, Tx, NKV, HD).transpose(0, 2, 1, 3)
        cos, sin = _rope_tables(Tx)
        cos, sin = (cos[None, None], sin[None, None])
        q = q * cos + _rotate_half(q) * sin
        k = k * cos + _rotate_half(k) * sin
        k = jnp.repeat(k, NREP, axis=1)
        v = jnp.repeat(v, NREP, axis=1)
        scores = jnp.einsum('bhtd,bhsd->bhts', q, k) / jnp.sqrt(jnp.float32(HD))
        causal = jnp.tril(jnp.ones((Tx, Tx), dtype=bool))
        scores = jnp.where(causal[None, None], scores, jnp.float32(-1e+30))
        att = jax.nn.softmax(scores, axis=-1)
        y = jnp.einsum('bhts,bhsd->bhtd', att, v).transpose(0, 2, 1, 3).reshape(Bx, Tx, Cx)
        x = x + y @ wo.T
        flat = _rmsnorm(x, ln2_w).reshape(-1, Cx)
        probs = jax.nn.softmax(flat @ router_w.T, axis=-1)
        tp, ti = jax.lax.top_k(probs, TOPK)
        tp = tp / (jnp.sum(tp, axis=-1, keepdims=True) + 1e-09)
        weights = jnp.sum(tp[..., None] * jax.nn.one_hot(ti, NE, dtype=flat.dtype), axis=1)
        out = jnp.zeros_like(flat)
        for e in range(NE):
            hh = jax.nn.silu(flat @ w1[e].T) * (flat @ w3[e].T)
            out = out + weights[:, e:e + 1] * (hh @ w2[e].T)
        return x + out.reshape(Bx, Tx, Cx)

    def _L3_attn_ref(x, Wq, bq, Wk, bk, Wv, bv, scale):
        import jax, jax.numpy as jnp
        import numpy as np
        B, N, D = (4, 1024, 64)
        q = jnp.einsum('bnd,ed->bne', x, Wq) + bq
        k = jnp.einsum('bnd,ed->bne', x, Wk) + bk
        v = jnp.einsum('bnd,ed->bne', x, Wv) + bv
        scores = jnp.einsum('bqd,bkd->bqk', q, k) / scale[0]
        attn = jax.nn.softmax(scores, axis=-1)
        out = jnp.einsum('bqk,bkd->bqd', attn, v)
        return out

    def _L3_ffn_ref(x, gate_w, gate_b, w1, b1, w2, b2, gamma, beta):
        import jax, jax.numpy as jnp
        import numpy as np
        B, S, H, F, E, K = (8, 1024, 64, 128, 16, 2)
        EPS = 1e-05
        gate_logits = x @ gate_w + gate_b
        topk_vals, topk_idx = jax.lax.top_k(gate_logits, K)
        topk_w = jax.nn.softmax(topk_vals, axis=-1)
        h = jax.nn.relu(jnp.einsum('bsh,ehf->bsef', x, w1) + b1)
        expert_out = jnp.einsum('bsef,efh->bseh', h, w2) + b2
        sel = jnp.take_along_axis(expert_out, topk_idx[:, :, :, None], axis=2)
        moe = jnp.sum(topk_w[..., None] * sel, axis=2)
        y = x + moe
        mu = jnp.mean(y, axis=-1, keepdims=True)
        var = jnp.var(y, axis=-1, keepdims=True)
        return (y - mu) / jnp.sqrt(var + EPS) * gamma + beta
    h = _L0_tok_ref(x, L0_tok_ln_g, L0_tok_ln_b, L0_tok_Wq, L0_tok_bq, L0_tok_Wk, L0_tok_bk, L0_tok_Wv, L0_tok_bv, L0_tok_Wo, L0_tok_bo, 8)
    h = h + _L0_attn_ref(_layernorm(h, axis=-1), L0_attn_alpha, L0_attn_dyt_w, L0_attn_dyt_b, L0_attn_w_in, L0_attn_b_in, L0_attn_w_q, L0_attn_b_q, L0_attn_w_k, L0_attn_b_k, L0_attn_A, L0_attn_Bp, L0_attn_Cp, L0_attn_conv_w, L0_attn_w_out, L0_attn_b_out)
    h = h + _L0_ffn_ref(_layernorm(h, axis=-1), L0_ffn_sW1, L0_ffn_sb1, L0_ffn_sW2, L0_ffn_sb2, L0_ffn_sW3, L0_ffn_sb3, L0_ffn_eW1, L0_ffn_eb1, L0_ffn_eW2, L0_ffn_eb2, L0_ffn_eW3, L0_ffn_eb3, L0_ffn_gW, L0_ffn_gb)
    h = h + _L1_attn_ref(_layernorm(h, axis=-1), L1_attn_w_qkv, L1_attn_w_proj, L1_attn_b_proj, L1_attn_temperature)
    h = h + _L1_ffn_ref(_layernorm(h, axis=-1), L1_ffn_gamma, L1_ffn_beta, L1_ffn_Wr, L1_ffn_br, L1_ffn_W1, L1_ffn_b1, L1_ffn_W2, L1_ffn_b2)
    h = h + _L2_attn_ref(_layernorm(h, axis=-1), L2_attn_Wq, L2_attn_Wk, L2_attn_Wv)
    h = h + _L2_ffn_ref(_layernorm(h, axis=-1), L2_ffn_ln1_w, L2_ffn_ln2_w, L2_ffn_wq, L2_ffn_wk, L2_ffn_wv, L2_ffn_wo, L2_ffn_router_w, L2_ffn_w1, L2_ffn_w2, L2_ffn_w3)
    h = h + _L3_attn_ref(_layernorm(h, axis=-1), L3_attn_Wq, L3_attn_bq, L3_attn_Wk, L3_attn_bk, L3_attn_Wv, L3_attn_bv, L3_attn_scale)
    h = h + _L3_ffn_ref(_layernorm(h, axis=-1), L3_ffn_gate_w, L3_ffn_gate_b, L3_ffn_w1, L3_ffn_b1, L3_ffn_w2, L3_ffn_b2, L3_ffn_gamma, L3_ffn_beta)
    return h

_drawn_inputs = setup_inputs


def setup_inputs(seed=0):
    import zlib

    import numpy as np

    out = dict(_drawn_inputs(seed))
    spreads = {'L0_tok_ln_g': (1.0, 0.6),
     'L0_tok_ln_b': (0.0, 0.534),
     'L0_tok_bo': (0.0, 0.1),
     'L0_attn_dyt_w': (1.0, 0.6),
     'L0_attn_dyt_b': (0.0, 0.8),
     'L0_ffn_sb1': (0.0, 0.8),
     'L0_ffn_sb2': (0.0, 0.1),
     'L0_ffn_sb3': (0.0, 0.1),
     'L0_ffn_eb1': (0.0, 0.8),
     'L0_ffn_eb2': (0.0, 0.567),
     'L0_ffn_eb3': (0.0, 0.1),
     'L0_ffn_gb': (0.0, 0.8),
     'L1_ffn_br': (0.0, 0.672),
     'L2_ffn_ln1_w': (1.0, 0.6),
     'L2_ffn_ln2_w': (1.0, 0.6),
     'L3_attn_bq': (0.0, 2.0),
     'L3_attn_bk': (0.0, 2.0),
     'L3_attn_bv': (0.0, 1.218),
     'L3_ffn_gate_b': (0.0, 0.8),
     'L3_ffn_b1': (0.0, 2.0),
     'L3_ffn_b2': (0.0, 2.0),
     'L3_ffn_gamma': (1.0, 0.6),
     'L3_ffn_beta': (0.0, 1.032)}
    factors = {'x': 8.0,
     'L0_tok_Wq': 8.0,
     'L0_tok_bq': 8.0,
     'L0_tok_Wk': 8.0,
     'L0_tok_bk': 64.0,
     'L0_tok_Wv': 3.774,
     'L0_attn_w_in': 8.0,
     'L0_attn_b_in': 8.0,
     'L0_attn_w_q': 57.781,
     'L0_attn_w_k': 8.0,
     'L0_attn_A': 8.0,
     'L0_attn_Bp': 53.853,
     'L0_attn_Cp': 28.482,
     'L0_attn_conv_w': 8.0,
     'L0_attn_w_out': 8.0,
     'L0_attn_b_out': 8.0,
     'L0_ffn_eW1': 3.655,
     'L0_ffn_eW2': 3.234,
     'L1_attn_b_proj': 8.0,
     'L1_ffn_gamma': 8.0,
     'L1_ffn_beta': 8.0,
     'L1_ffn_Wr': 6.609,
     'L1_ffn_W1': 8.0,
     'L1_ffn_b1': 8.0,
     'L1_ffn_W2': 6.984,
     'L1_ffn_b2': 8.0,
     'L2_attn_Wq': 8.0,
     'L2_attn_Wk': 8.0,
     'L2_ffn_wq': 8.0,
     'L2_ffn_wk': 8.0,
     'L2_ffn_wv': 7.092,
     'L2_ffn_wo': 7.297,
     'L2_ffn_router_w': 8.0,
     'L2_ffn_w1': 8.0,
     'L2_ffn_w2': 8.0,
     'L2_ffn_w3': 8.0,
     'L3_attn_Wq': 8.0,
     'L3_attn_Wk': 8.0,
     'L3_ffn_gate_w': 4.167,
     'L3_ffn_w1': 8.0,
     'L3_ffn_w2': 8.0}
    for name, (base, spread) in spreads.items():
        noise = np.random.default_rng([zlib.crc32(name.encode()), seed]).standard_normal(out[name].shape)
        drawn = base * np.exp(spread * noise) if base else spread * noise
        out[name] = jnp.asarray(drawn.astype(out[name].dtype))
    for name, factor in factors.items():
        out[name] = (out[name] * factor).astype(out[name].dtype)
    return out
```

```python
from contextlib import ExitStack

import concourse.bass as bass
from concourse import mybir

F32 = mybir.dt.float32
BF16 = mybir.dt.bfloat16
U32 = mybir.dt.uint32
ALU = mybir.AluOpType
ACT = mybir.ActivationFunctionType
AX = mybir.AxisListType

P = 128
CLIPS, ROWS, DIM = 16, 1536, 64
TOK = ROWS // 3
NT = TOK // P
LANES = 1
HEADS, HD = 8, 8
EPS = 1e-5
EPS_RMS = 1e-6
EXP, NST, DCONV = 128, 16, 4
TOPK = int(TOK * 0.3)
TAIL = TOPK - P
SKEW = P + TOPK + 2
HID = int(8 / 3 * DIM)
HALF = HID // 2
ROWS2 = 96
NEG = -3.0e38
CAUSAL = -1.0e30
DIAG = 1.0e9

Q_PART = (1, 1, 2, 2, 1, 3)
K_PART = (1, 2, 1, 2, 3, 1)

SPLIT = [
    ("t_q", 512), ("t_k", 512), ("t_v", 64), ("a_in", 128),
    ("f0_s1", 64), ("f0_e1", 512), ("f0_g", 4),
    ("l1_q", 512), ("l1_k", 512), ("l1_v", 64), ("f1_g", 8), ("f1_w1", 1024),
    ("l2_q", 64), ("l2_k", 64), ("l2_v", 64),
    ("c_q", 512), ("c_k", 512), ("c_qs", 512), ("c_ks", 512), ("c_v", 32),
    ("f2_g", 8), ("f2_w1", 16 * ROWS2), ("f2_w3", 16 * ROWS2),
    ("l3_q", 64), ("l3_k", 64), ("l3_v", 64), ("f3_g", 16), ("f3_w1", 2048),
]
WHOLE = [
    ("ident", 128), ("ones", 128), ("ltmask", 128), ("iota", 160), ("iotae", 16),
    ("negmask", 128), ("negmaskT", 128),
    ("cos", 512), ("sin", 512),
    ("mones8", 256),
    ("qa1", 1), ("qa2", 1), ("ka1", 1), ("ka2", 1), ("ca1", 1), ("ca2", 1), ("da1", 1), ("da2", 1),
    ("ra1", 1), ("ra2", 1),
    ("t_g", 64), ("t_b", 64), ("t_bq", 4), ("t_bk", 4), ("t_bv", 64), ("t_wo", 64), ("t_bo", 64),
    ("a_alpha", 1), ("a_w", 64), ("a_b", 64), ("a_bin", 128), ("a_wq", 128), ("a_wk", 128), ("a_bq", 1), ("a_bk", 1),
    ("a_A", 16), ("a_AT", 16), ("a_BpT", 1), ("a_Cp", 16), ("a_conv", 4), ("a_wout", 64), ("a_bout", 64),
    ("f0_bs1", 1), ("f0_s2", 128), ("f0_bs2", 1), ("f0_be1", 4), ("f0_e2", 256), ("f0_be2", 4), ("f0_gb", 4),
    ("f0_w3", 5 * 64),
    ("l1_bk", 4), ("l1_wo", 64), ("l1_bo", 64), ("l1_temp", 1),
    ("f1_gam", 64), ("f1_bet", 64), ("f1_gb", 8), ("f1_b1", 8), ("f1_w2", 512),
    ("c_ln1", 64), ("c_ln2", 64), ("c_bk", 1), ("c_wo", 64), ("f2_w2", 1024),
    ("l3_bq", 1), ("l3_bk", 1), ("l3_bv", 64), ("l3_scale", 1),
    ("f3_gb", 16), ("f3_b1", 16), ("f3_w2", 1024), ("f3_gam", 64), ("f3_bet", 64),
]
BIASROW = [("f0_b3", 320), ("f1_b2", 512), ("f3_b2", 1024)]


def offsets(listing):
    at, out = 0, {}
    for name, n in listing:
        out[name] = (at, n)
        at += n
    return out, at


SPLIT_AT, SPLIT_N = offsets(SPLIT)
WHOLE_AT, WHOLE_N = offsets(WHOLE)
BIAS_AT, BIAS_N = offsets(BIASROW)
STAGES = ["tok", "sparse", "ffn0", "l1", "ffn1", "l2", "causal", "ffn2", "l3", "ffn3"]
CHUNK = 1024


class Signal:

    def __init__(self, name, sem, known, noted):
        self.name, self.sem, self.known, self.noted, self.count = name, sem, known, noted, 0

    def inc(self, *event):
        self.count += 1
        self.noted[(self.name, event)] = self.count
        return self.sem, 1

    def at(self, *event):
        assert not self.known or (self.name, event) in self.known, (self.name, event)
        return self.sem, self.known.get((self.name, event), 1)


class Banks:

    def __init__(self, name, slots, filled, freed, known, noted):
        self.name, self.slots, self.filled_sems, self.freed_sems = name, slots, filled, freed
        self.known, self.noted = known, noted
        self.order = []
        self.place = {}
        sums = [0] * len(slots)
        for n, key in enumerate(known.get((name, "order"), ())):
            sums[n % len(slots)] += known.get((name, "readers", key), 0)
            self.place[key] = (n % len(slots), n // len(slots) + 1, sums[n % len(slots)])
        noted[(name, "order")] = self.order

    def take(self, pe, *key):
        n = len(self.order)
        if n >= len(self.slots):
            pe.wait_ge(*self.read(*self.order[n - len(self.slots)]))
        self.order.append(key)
        return self.slots[n % len(self.slots)]

    def where(self, key):
        assert not self.known or key in self.place, key
        return self.place.get(key, (0, 1, 1))

    def view(self, *key):
        return self.slots[self.where(key)[0]]

    def fill(self, *key):
        return self.filled_sems[self.where(key)[0]], 1

    def filled(self, *key):
        slot, uses, _ = self.where(key)
        return self.filled_sems[slot], uses

    def free(self, *key):
        self.noted[(self.name, "readers", key)] = self.noted.get((self.name, "readers", key), 0) + 1
        return self.freed_sems[self.where(key)[0]], 1

    def read(self, *key):
        slot, _, readers = self.where(key)
        return self.freed_sems[slot], max(readers, 1)


def finish(eng, instruction, sig, *event):
    if isinstance(sig, Banks):
        instruction.then_inc(*sig.free(*event))
        eng.wait_ge(*sig.read(*event))
    else:
        instruction.then_inc(*sig.inc(*event))
        eng.wait_ge(sig.sem, sig.count)


def audio_tower(nc, x, wsplit, wwhole, wbias, skew, out, known, noted):
    ctx = ExitStack()
    with ctx:
        def sb(name, shape, dt=F32):
            return ctx.enter_context(nc.sbuf_tensor(name, shape, dt))

        def semaphore(name):
            return ctx.enter_context(nc.semaphore(name))

        turn_sems = []

        def turn_semaphore(name):
            turn_sems.append(semaphore(name))
            return turn_sems[-1]

        def signal(name):
            return Signal(name, turn_semaphore(name), known, noted)

        pair_t = [ctx.enter_context(nc.psum_tensor(f"pair{i}", [P, 1024], F32)) for i in range(3)]
        heads_t = ctx.enter_context(nc.psum_tensor("heads_bank", [P, 512], F32))
        turned_t = ctx.enter_context(nc.psum_tensor("turned_bank", [P, 512], F32))
        pair = Banks("pair", pair_t, [turn_semaphore(f"pair{i}_filled") for i in range(3)],
                     [turn_semaphore(f"pair{i}_freed") for i in range(3)], known, noted)
        heads_bank = Banks("heads", [heads_t], [turn_semaphore("heads_filled")], [turn_semaphore("heads_freed")],
                           known, noted)
        turned_bank = Banks("turned", [turned_t], [turn_semaphore("turned_filled")], [turn_semaphore("turned_freed")],
                            known, noted)

        whole = sb("whole", [P, WHOLE_N])
        w_ab = sb("w_ab", [P, SPLIT_N], BF16)
        w_ca = sb("w_ca", [P, SPLIT_N], BF16)
        bias3 = sb("bias3", [3, BIAS_N], BF16)
        identb = sb("identb", [P, P], BF16)
        monesb = sb("monesb", [P, 256], BF16)
        onesb = sb("onesb", [3, P], BF16)
        minus_half = sb("minus_half", [P, 12])
        sig_b = sb("sig_b", [NST, 1])
        scan_t = sb("scan_t", [P, NST, TOPK])
        t_bqs = sb("t_bqs", [P, 4])
        t_bo2 = sb("t_bo2", [P, 64])
        l1_qscale = sb("l1_qscale", [P, 1])
        l3_qscale = sb("l3_qscale", [P, 1])
        l3_bqs = sb("l3_bqs", [P, 1])
        diag3 = sb("diag3", [P, 3, P], BF16)
        causal_b = sb("causal_b", [P, 2, P], BF16)

        def W(name, rows=P, a=0, b=None):
            at, n = WHOLE_AT[name]
            return whole[0:rows, at + a:at + (n if b is None else b)]

        sig_c = sb("sig_c", [EXP, NST])

        def SW(name, a=0, b=None):
            at, n = SPLIT_AT[name]
            b = n if b is None else b
            return w_ab[:, at + a:at + b], w_ca[:, at + a:at + b]

        class Lane:
            def __init__(self, n):
                self.n = n
                self.h = sb(f"h_{n}", [P, NT, 64])
                self.base = sb(f"base_{n}", [P, NT, 64])
                self.normed = sb(f"normed_{n}", [P, NT, 64])
                self.stat = sb(f"stat_{n}", [P, 4, 12])
                self.xt0 = sb(f"xt0_{n}", [P, 3, 512], BF16)
                self.qs = sb(f"qs_{n}", [P, 8, 512], BF16)
                self.ks = sb(f"ks_{n}", [P, 8, 512], BF16)
                self.v = sb(f"v_{n}", [P, 2, NT, 8, 32])
                self.v64 = sb(f"v64_{n}", [P, NT, 65])
                self.v16 = sb(f"v16_{n}", [P, NT, 4, 32])
                self.att = sb(f"att_{n}", [P, 4, 512])
                self.hid = sb(f"hid_{n}", [P, 8, 512])
                self.small = sb(f"small_{n}", [P, 12, 4, 16])
                self.heads_out = sb(f"heads_out_{n}", [P, NT, 64])
                self.m3 = sb(f"m3_{n}", [P, NT, 65])
                self.idx = sb(f"idx_{n}", [P, 4, 8], U32)
                hid = self.hid[:, :, :].rearrange("p a b -> p (a b)")
                self.parts = hid[:, 0:12 * 6 * 32].bitcast(BF16).rearrange("p (t a d) -> p t a d", t=12, a=6)
                self.x = self.ks[:, :, :].rearrange("p a b -> p (a b)")[:, 1536:3072].bitcast(F32)\
                    .rearrange("p (t d) -> p t d", t=12)
                self.normed12 = self.ks[:, :, :].rearrange("p a b -> p (a b)")[:, 0:1536].bitcast(F32)\
                    .rearrange("p (t d) -> p t d", t=12)
                att = self.att[:, :, :].rearrange("p a b -> p (a b)")
                self.xt = [self.xt0[:, :, :]] + [att[:, 768 * k:768 * k + 768].bitcast(BF16).rearrange("p (a c) -> p a c", a=3)
                                                 for k in range(2)]

        lanes = [Lane(n) for n in range(LANES)]
        kern = sb("kern", [NST, SKEW])
        power = sb("power", [NST, NST])
        power_t = sb("power_t", [NST, NST])
        cent = sb("cent", [P, 12, 64])
        perm = sb("perm", [P, NT, 160])
        f_t = sb("f_t", [P, 2, 1024])
        pm_t = sb("pm_t", [P, 2, 1024], BF16)
        hid0 = lanes[0].hid[:, :, :].rearrange("p (a b) c -> p a (b c)", b=2)
        y_t = hid0[:, 2:4, :]
        neg_t = sb("neg_t", [P, 2, 32])
        m_t = sb("m_t", [P, 2, 1, NT, P], BF16)
        mc_t = sb("mc_t", [P, 2, 2, NT, P], BF16)
        m_left = sb("m_left", [P, 2, 8])
        qm_t = sb("qm_t", [P, 2, 2, 512], BF16)
        qmc_t = sb("qmc_t", [P, 2, 2, 512], BF16)
        qm1_t = qmc_t[:, 0, :, :]
        prob2 = sb("prob2", [P, 1024])
        prob = [hid0[:, 0, :], hid0[:, 1, :], prob2[:, :]]
        o_t = sb("o_t", [P, 2, 512])
        recip16 = sb("recip16", [P, NT, 4])
        r_t = sb("r_t", [P, 512])
        prod = sb("prod", [P, 1024])
        red = sb("red", [P, 2, 64])
        sq = prod[:, 0:768].rearrange("p (t d) -> p t d", t=12)

        def start_signal(name):
            return Signal(name, semaphore(name), known, noted)

        loaded = semaphore("loaded")
        staged = [semaphore("staged0"), semaphore("staged1")]
        set_v = start_signal("set_v")
        set_a = start_signal("set_a")
        set_p = start_signal("set_p")
        set_t = start_signal("set_t")
        skew_done = semaphore("skew_done")
        scan_loaded = semaphore("scan_loaded")
        stored = semaphore("stored")
        turn_done = semaphore("turn_done")
        go = {e: semaphore(f"go_{e}") for e in ("pe", "act", "dve", "pool")}
        clip_loaded = [turn_semaphore(f"clip_loaded{n}") for n in range(LANES)]

        def next_turn(eng, name):
            eng.nop().then_inc(turn_done, 1)
            eng.wait_ge(go[name], 1)
            eng.sem_clear(go[name])

        v_step = signal("v_step")
        a_step = signal("a_step")
        p_step = signal("p_step")
        var_ready = signal("var_ready")
        rstd_ready = signal("rstd_ready")
        part1_ready = signal("part1_ready")
        part1_copied = signal("part1_copied")
        parts_ready = signal("parts_ready")
        f_ready = signal("f_ready")
        p1_ready = signal("p1_ready")
        y1_ready = signal("y1_ready")
        p2_ready = signal("p2_ready")
        heads_ready = signal("heads_ready")
        v_ready = signal("v_ready")
        maxima_ready = signal("maxima_ready")
        shift_ready = signal("shift_ready")
        prob_used = signal("prob_used")
        att_ready = signal("att_ready")
        act_req = signal("act_req")
        act_rsp = signal("act_rsp")
        pe_req = signal("pe_req")
        pool_rsp = signal("pool_rsp")
        hid_a = signal("hid_a")
        hid_v = signal("hid_v")
        out_ready = signal("out_ready")

        block = ctx.enter_context(nc.Block())

        def mm3(pe, o, w, xt, start=True, stop=True):
            ab, ca = w
            pe.matmul(o, ab, xt[:, 0, :], start=start, stop=False)
            pe.matmul(o, ab, xt[:, 1, :], start=False, stop=False)
            return pe.matmul(o, ca, xt[:, 2, :], start=False, stop=stop)

        def mm3t(pe, o, xt, t, w):
            ab, ca = w
            c = slice(t * P, (t + 1) * P)
            pe.matmul(o, xt[:, 0, c], ab, start=True, stop=False)
            pe.matmul(o, xt[:, 1, c], ab, start=False, stop=False)
            return pe.matmul(o, xt[:, 2, c], ca, start=False, stop=True)

        ATT = {
            "tok": dict(units=[(n, src, g) for n in range(LANES) for src in range(2) for g in range(4)],
                        qk=lambda L, src, g, j: (L.qs[:, 2 * g + j, :], L.ks[:, 4 * src + g, :]), mtiles=1, m=m_t,
                        needs=lambda src, g: [("q", 0, g // 2), ("k", src, g // 2)]),
            "l1": dict(units=[(n, 0, g) for n in range(LANES) for g in range(4)],
                       qk=lambda L, src, g, j: (L.qs[:, 2 * g + j, :], L.ks[:, g, :]), mtiles=1, m=m_t,
                       needs=lambda src, g: [("q", 0, g // 2), ("k", 0, g // 2)]),
            "causal": dict(units=[(n, 0, g) for n in range(LANES) for g in range(2)],
                           qk=lambda L, src, g, j: (L.ks[:, 4 + 2 * g + j, :], L.ks[:, 2 * g + j, :]), mtiles=2, m=mc_t,
                           needs=lambda src, g: [("q", g), ("k", g)]),
        }

        def run_schedule(groups, do):
            for step in range(4 * groups + 12):
                for what, late in (("e", 7), ("w", 9), ("m", 0)):
                    k = step - late
                    if what in do and 0 <= k < 4 * groups:
                        do[what](k // 4, k % 4)
                for what, late in (("t", 5), ("o", 12), ("s", 14)):
                    k = step - late
                    if what in do and k >= 0 and k % 4 == 0 and k // 4 < groups and (what == "t" or k // 4 % 2 == 1):
                        do[what](k // 4)

        @block.tensor
        def _(pe):
            for k in range(8):
                T = 1 << k
                n = min(T, TOPK - T)
                pe.wait_ge(*set_v.at("power", k))
                pe.matmul(pair_t[0][0:NST, 0:n], power_t[:, :], kern[:, 0:n], start=True, stop=True)
                pe.matmul(pair_t[1][0:NST, 0:NST], power_t[:, :], power[:, :], start=True, stop=True)
                pe.matmul(pair_t[2][0:NST, 0:NST], power[:, :], power_t[:, :], start=True, stop=True).then_inc(*set_t.inc("power", k))
            pe.wait_ge(*set_v.at("all"))
            pe.wait_ge(scan_loaded, 16)

            def turn_features(st, L, src):
                n = L.n
                pe.wait_ge(*part1_copied.at(st, n))
                pe.wait_ge(*parts_ready.at(st, n))
                ps = pair.take(pe, st, n, "turn", src)[:].bitcast(BF16)
                for s in range(3):
                    for t in range(NT):
                        mm = pe.transpose(ps[:, s * 512 + t * P:s * 512 + (t + 1) * P],
                                          L.parts[:, src * NT + t, 2 * s:2 * s + 2, :].rearrange("p a d -> p (a d)"),
                                          identb[:, :])
                mm.then_inc(*pair.fill(st, n, "turn", src))

            def wait_xt(st, n, src):
                pe.wait_ge(*pair.read(st, n, "turn", src))

            def project(st, L, what, src, w, tiles=2):
                ps = pair.take(pe, st, L.n, what)
                for j in range(tiles):
                    mm = mm3(pe, ps[:, j * 512:(j + 1) * 512], SW(*w[j]), L.xt[src])
                mm.then_inc(*pair.fill(st, L.n, what))

            def values(st, L, src, w, cols):
                ps = pair.take(pe, st, L.n, "v", src)
                for t in range(NT):
                    mm = mm3t(pe, ps[:, t * cols:(t + 1) * cols], L.xt[src], t, SW(w))
                mm.then_inc(*pair.fill(st, L.n, "v", src))

            def attention(st):
                cfg = ATT[st]
                units = cfg["units"]

                def scores(i, it):
                    n, src, g = units[i]
                    L = lanes[n]
                    if it == 0:
                        for what in cfg["needs"](src, g):
                            pe.wait_ge(*heads_ready.at(st, n, what))
                    cols = (it + 1) * P if st == "causal" else 512
                    ps = pair.take(pe, st, i, "m", it)
                    for j in range(2):
                        q, k = cfg["qk"](L, src, g, j)
                        mm = pe.matmul(ps[:, j * 512:j * 512 + cols], q[:, it * P:(it + 1) * P], k[:, 0:cols],
                                       start=True, stop=st == "tok")
                        d = ps[:, j * 512 + it * P:j * 512 + (it + 1) * P]
                        if st == "l1":
                            for a in range(3):
                                mm = pe.matmul(d, identb[:, :], diag3[:, a, :], start=False, stop=a == 2)
                        if st == "causal":
                            mm = pe.matmul(d, identb[:, :], causal_b[:, 0, :], start=False, stop=True)
                    mm.then_inc(*pair.fill(st, i, "m", it))

                def turn_maxima(i):
                    pe.wait_ge(*maxima_ready.at(st, i))
                    ps = turned_bank.take(pe, st, i, "t")[:].bitcast(BF16)
                    for j in range(cfg["mtiles"]):
                        for t in range(NT):
                            mm = pe.transpose(ps[:, j * 512 + t * P:j * 512 + (t + 1) * P], cfg["m"][:, i % 2, j, t, :],
                                              identb[:, :])
                    mm.then_inc(*turned_bank.fill(st, i, "t"))

                def shifted(i, jt):
                    n, src, g = units[i]
                    L = lanes[n]
                    if jt == 0:
                        pe.wait_ge(*shift_ready.at(st, i))
                    c0 = jt * P if st == "causal" else 0
                    ps = pair.take(pe, st, i, "e", jt)
                    for j in range(2):
                        q, k = cfg["qk"](L, src, g, j)
                        k = k[:, jt * P:(jt + 1) * P]
                        o = ps[:, j * 512 + c0:(j + 1) * 512]
                        d = ps[:, j * 512 + jt * P:j * 512 + (jt + 1) * P]
                        if st == "l1":
                            pe.matmul(o, k, q, start=True, stop=False)
                            for a in range(3):
                                pe.matmul(d, identb[:, :], diag3[:, a, :], start=False, stop=False)
                            mm = pe.matmul(o, monesb[:, j * P:(j + 1) * P], qm1_t[:, i % 2, :], start=False, stop=True)
                        else:
                            mm = pe.matmul(o, k, (qmc_t if st == "causal" else qm_t)[:, i % 2, j, c0:512], start=True, stop=st == "tok")
                        if st == "causal":
                            mm = pe.matmul(d, identb[:, :], causal_b[:, 1, :], start=False, stop=True)
                    mm.then_inc(*pair.fill(st, i, "e", jt))

                def weigh(i, jt):
                    n, src, g = units[i]
                    L = lanes[n]
                    pe.wait_ge(*pair.read(st, i, "e", jt))
                    if g % 2 == 0 and jt == 0:
                        pe.wait_ge(*v_ready.at(st, n, src))
                        heads_bank.take(pe, st, i + 1)
                    c0 = jt * P if st == "causal" else 0
                    for j in range(2):
                        h4 = (g % 2) * 2 + j
                        v = L.v16[:, jt, 2 * g + j, :] if st == "causal" else L.v[:, src, jt, 2 * g + j, :]
                        mm = pe.matmul(heads_t[32 * h4:32 * h4 + 32, c0:512], v,
                                       prob[(4 * i + jt) % 3][:, j * 512 + c0:(j + 1) * 512],
                                       start=jt == 0, stop=jt == NT - 1)
                    mm.then_inc(*prob_used.inc(st, i, jt))

                def turn_outputs(i):
                    pe.wait_ge(*heads_bank.read(st, i))
                    ps = turned_bank.take(pe, st, i, "s")
                    for t in range(NT):
                        mm = pe.transpose(ps[:, t * P:(t + 1) * P], o_t[:, (i // 2) % 2, t * P:(t + 1) * P], W("ident"))
                    mm.then_inc(*turned_bank.fill(st, i, "s"))

                run_schedule(len(units), dict(m=scores, t=turn_maxima, e=shifted, w=weigh, s=turn_outputs))

            def out_heads(st, L, w):
                n = L.n
                pe.wait_ge(*att_ready.at(st, n))
                ps = pair.take(pe, st, n, "at")
                for t in range(NT):
                    mm = pe.transpose(ps[0:64, t * P:(t + 1) * P], L.heads_out[:, t, :], W("ident"))
                mm.then_inc(*pair.fill(st, n, "at"))
                pe.wait_ge(*pair.read(st, n, "at"))
                ps = pair.take(pe, st, n, "wo")
                for t in range(NT):
                    mm = pe.matmul(ps[:, t * 64:(t + 1) * 64], L.att[0:64, 0, t * P:(t + 1) * P], W(w, 64), start=True, stop=True)
                mm.then_inc(*pair.fill(st, n, "wo"))

            def tok(L):
                for src in range(3):
                    turn_features("tok", L, src)
                for src in range(3):
                    wait_xt("tok", L.n, src)
                    if src == 0:
                        for a in range(2):
                            project("tok", L, ("q", 0, a), 0, [("t_q", 256 * a + 128 * j, 256 * a + 128 * j + 128) for j in range(2)])
                    else:
                        for a in range(2):
                            project("tok", L, ("k", src - 1, a), src,
                                    [("t_k", 256 * a + 128 * j, 256 * a + 128 * j + 128) for j in range(2)])
                        values("tok", L, src, "t_v", 64)

            def sparse(L):
                st, n = "sparse", L.n
                turn_features(st, L, 0)
                wait_xt(st, n, 0)
                ps = pair.take(pe, st, n, "xp")
                for t in range(NT):
                    mm = mm3t(pe, ps[:, t * P:(t + 1) * P], L.xt[0], t, SW("a_in"))
                mm.then_inc(*pair.fill(st, n, "xp"))
                pe.wait_ge(*pe_req.at(st, n, "kdiag"))
                ps = pair.take(pe, st, n, "kb")
                pe.matmul(ps[:, 0:512], W("ones"), L.att[:, 0, :], start=True, stop=True).then_inc(*pair.fill(st, n, "kb"))
                pe.wait_ge(*pe_req.at(st, n, "recip"))
                ps = pair.take(pe, st, n, "imp")
                for t in range(NT):
                    mm = pe.matmul(ps[:, 0:512], L.att[:, 1, t * P:(t + 1) * P], L.hid[:, t, :], start=t == 0, stop=t == NT - 1)
                mm.then_inc(*pair.fill(st, n, "imp"))
                pe.wait_ge(*pe_req.at(st, n, "perm"))
                ps = pair.take(pe, st, n, "xs")
                pv = perm
                for c, m in ((0, P), (1, TAIL)):
                    for t in range(NT):
                        mm = pe.matmul(ps[0:m, c * 512:c * 512 + EXP], pv[:, t, c * P:c * P + m], L.hid[:, 6, t * P:(t + 1) * P],
                                       start=t == 0, stop=t == NT - 1)
                mm.then_inc(*pair.fill(st, n, "xs"))
                ps = pair.take(pe, st, n, "pt")
                for c, m in ((0, P), (1, TAIL)):
                    for t in range(NT):
                        mm = pe.transpose(ps[0:m, c * 512 + t * P:c * 512 + (t + 1) * P], pv[:, t, c * P:c * P + m], W("ident"))
                mm.then_inc(*pair.fill(st, n, "pt"))
                pe.wait_ge(*pair.read(st, n, "xs"))
                for b in range(3):
                    ps = pair.take(pe, st, n, "scan", b)
                    for k in range(2):
                        s0, s1 = 6 * b + 3 * k, min(6 * b + 3 * k + 3, NST)
                        if s0 < s1:
                            o = ps[:, k * 512:k * 512 + (s1 - s0) * TOPK]
                            pe.matmul(o, L.hid[:, 7, 0:P], scan_t[:, s0:s1, :].rearrange("p n t -> p (n t)"), start=True, stop=False)
                            mm = pe.matmul(o.rearrange("p (n t) -> p n t", t=TOPK)[:, :, P:TOPK], L.hid[0:TAIL, 7, P:2 * P],
                                           scan_t[0:TAIL, s0:s1, 0:TAIL], start=False, stop=True)
                    mm.then_inc(*pair.fill(st, n, "scan", b))
                pe.wait_ge(*pe_req.at(st, n, "conv"))
                ps = pair.take(pe, st, n, "xo")
                y = L.att[:, 0, 160:160 + TOPK]
                pe.matmul(ps[:, 0:64], y[:, 0:P], W("a_wout"), start=True, stop=True)
                pe.matmul(ps[0:TAIL, 512:576], y[:, P:TOPK], W("a_wout"), start=True, stop=True).then_inc(*pair.fill(st, n, "xo"))
                pe.wait_ge(*pe_req.at(st, n, "xo"))
                pe.wait_ge(*pair.read(st, n, "pt"))
                ps = pair.take(pe, st, n, "back")
                for t in range(NT):
                    pe.matmul(ps[:, t * 64:(t + 1) * 64], L.hid[:, 4, t * P:(t + 1) * P], L.att[:, 1, 0:64], start=True, stop=False)
                    mm = pe.matmul(ps[:, t * 64:(t + 1) * 64], L.hid[0:TAIL, 5, t * P:(t + 1) * P], L.att[0:TAIL, 1, 64:128],
                                   start=False, stop=True)
                mm.then_inc(*pair.fill(st, n, "back"))

            def gates(st, L, w, E):
                ps = pair.take(pe, st, L.n, "gate")
                for t in range(NT):
                    mm = mm3t(pe, ps[:, t * E:(t + 1) * E], L.xt[0], t, SW(w))
                mm.then_inc(*pair.fill(st, L.n, "gate"))

            def experts_out(st, L, r, parts_of, E, bias=None):
                for tp in range(2):
                    ps = pair.take(pe, st, L.n, "out", r, tp)
                    for a in range(2):
                        t = 2 * tp + a
                        o = ps[:, a * 512:a * 512 + E * 64]
                        if bias is not None:
                            at, _ = BIAS_AT[bias]
                            pe.matmul(o, onesb[:, :], bias3[:, at + r * 512:at + r * 512 + E * 64], start=True, stop=False,
                                      skip_group_check=True)
                        for e in range(E):
                            ops = parts_of(e)
                            for k, (hid, w2, rows) in enumerate(ops):
                                mm = pe.matmul(o[:, e * 64:(e + 1) * 64], hid[0:rows, t * P:(t + 1) * P], w2,
                                               start=bias is None and e == 0 and k == 0, stop=True, skip_group_check=True)
                    mm.then_inc(*pair.fill(st, L.n, "out", r, tp))

            def ffn0(L):
                st, n = "ffn0", L.n
                turn_features(st, L, 0)
                wait_xt(st, n, 0)
                gates(st, L, "f0_g", 4)
                ps = pair.take(pe, st, n, "s1")
                mm3(pe, ps[0:64, 0:512], SW("f0_s1"), L.xt[0]).then_inc(*pair.fill(st, n, "s1"))
                for a in range(2):
                    project(st, L, ("e1", a), 0, [("f0_e1", 256 * a + 128 * j, 256 * a + 128 * j + 128) for j in range(2)])
                pe.wait_ge(*pair.read(st, n, "s1"))
                ps = pair.take(pe, st, n, "s2")
                pe.matmul(ps[:, 0:512], W("f0_s2", 64), L.hid[0:64, 5, :], start=True, stop=True).then_inc(*pair.fill(st, n, "s2"))
                for a in range(2):
                    pe.wait_ge(*pair.read(st, n, ("e1", a)))
                    ps = pair.take(pe, st, n, "e2", a)
                    for j in range(2):
                        e = 2 * a + j
                        mm = pe.matmul(ps[0:64, j * 512:(j + 1) * 512], W("f0_e2", P, e * 64, e * 64 + 64), L.hid[:, e, :],
                                       start=True, stop=True)
                    mm.then_inc(*pair.fill(st, n, "e2", a))
                pe.wait_ge(*pair.read(st, n, "s2"))
                pe.wait_ge(*pair.read(st, n, "e2", 0))
                pe.wait_ge(*pair.read(st, n, "e2", 1))

                def ops(e):
                    if e == 4:
                        return [(L.hid[:, 4, :], W("f0_w3", P, 256, 320), P)]
                    return [(L.att[:, e, :], W("f0_w3", 64, e * 64, e * 64 + 64), 64)]
                experts_out(st, L, 0, ops, 5, "f0_b3")

            def ffn_relu(st, L, g, E, w1, w2, bias, rounds):
                n = L.n
                turn_features(st, L, 0)
                wait_xt(st, n, 0)
                gates(st, L, g, E)
                for r in range(rounds):
                    for a in range(4):
                        e = 8 * r + 2 * a
                        project(st, L, ("h", r, a), 0, [(w1, (e + j) * 128, (e + j + 1) * 128) for j in range(2)])
                    for a in range(4):
                        pe.wait_ge(*pair.read(st, n, ("h", r, a)))
                    experts_out(st, L, r, lambda e: [(L.hid[:, e, :], W(w2, P, (8 * r + e) * 64, (8 * r + e) * 64 + 64), P)], 8, bias)

            def plain(st, L, w, k_rows):
                n = L.n
                turn_features(st, L, 0)
                wait_xt(st, n, 0)
                ps = pair.take(pe, st, n, "qk")
                mm3(pe, ps[0:64, 0:512], SW(w + "_q"), L.xt[0])
                mm3(pe, ps[0:64, 512:1024], SW(w + "_k"), L.xt[0]).then_inc(*pair.fill(st, n, "qk"))
                values(st, L, 0, w + "_v", 64)

            def l2_attn(L):
                st, n = "l2", L.n
                plain(st, L, "l2", 64)
                pe.wait_ge(*pair.read(st, n, "qk"))
                for a in range(2):
                    ps = pair.take(pe, st, n, "s", a)
                    for j in range(2):
                        jt = 2 * a + j
                        mm = pe.matmul(ps[:, j * 512:(j + 1) * 512], L.att[0:64, 1, jt * P:(jt + 1) * P], L.att[0:64, 0, :],
                                       start=True, stop=True)
                    mm.then_inc(*pair.fill(st, n, "s", a))
                pe.wait_ge(*v_ready.at(st, n, "scaled"))
                ps = pair.take(pe, st, n, "wo")
                for t in range(NT):
                    for jt in range(NT):
                        mm = pe.matmul(ps[:, t * 64:(t + 1) * 64], L.hid[:, jt, t * P:(t + 1) * P], L.v64[:, jt, 0:64],
                                       start=jt == 0, stop=jt == NT - 1)
                mm.then_inc(*pair.fill(st, n, "wo"))

            def l3_attn(L):
                st, n = "l3", L.n
                plain(st, L, "l3", 65)
                pe.wait_ge(*pair.read(st, n, "qk"))
                for a in range(2):
                    ps = pair.take(pe, st, n, "m", a)
                    for j in range(2):
                        it = 2 * a + j
                        mm = pe.matmul(ps[:, j * 512:(j + 1) * 512], L.att[0:64, 0, it * P:(it + 1) * P], L.att[0:64, 1, :],
                                       start=True, stop=True)
                    mm.then_inc(*pair.fill(st, n, "m", a))
                pe.wait_ge(*maxima_ready.at(st, n))
                ps = pair.take(pe, st, n, "turnm")
                for t in range(NT):
                    mm = pe.transpose(ps[0:65, t * P:(t + 1) * P], L.m3[:, t, 0:65],
                                      W("ident"))
                mm.then_inc(*pair.fill(st, n, "turnm"))
                pe.wait_ge(*pair.read(st, n, "turnm"))
                for a in range(2):
                    ps = pair.take(pe, st, n, "s", a)
                    for j in range(2):
                        jt = 2 * a + j
                        mm = pe.matmul(ps[:, j * 512:(j + 1) * 512], L.att[0:65, 1, jt * P:(jt + 1) * P], L.att[0:65, 0, :],
                                       start=True, stop=True)
                    mm.then_inc(*pair.fill(st, n, "s", a))
                pe.wait_ge(*pair.read(st, n, "s", 1))
                pe.wait_ge(*v_ready.at(st, n, 0))
                ps = pair.take(pe, st, n, "wo")
                for t in range(NT):
                    for jt in range(NT):
                        mm = pe.matmul(ps[:, t * 65:t * 65 + 65], L.hid[:, jt, t * P:(t + 1) * P], L.v64[:, jt, :],
                                       start=jt == 0, stop=jt == NT - 1)
                mm.then_inc(*pair.fill(st, n, "wo"))

            def causal(L):
                st = "causal"
                turn_features(st, L, 0)
                wait_xt(st, L.n, 0)
                for what in "qk":
                    for tile in range(4):
                        project(st, L, (what, tile), 0, [("c_" + what, 128 * tile, 128 * tile + 128),
                                                         ("c_" + what + "s", 128 * tile, 128 * tile + 128)])
                values(st, L, 0, "c_v", 32)

            def ffn2(L):
                st, n = "ffn2", L.n
                turn_features(st, L, 0)
                wait_xt(st, n, 0)
                gates(st, L, "f2_g", 8)
                for r in range(2):
                    for c in range(8):
                        a = (8 * r + c) * ROWS2
                        ps = pair.take(pe, st, n, "h", r, c)
                        mm3(pe, ps[0:ROWS2, 0:512], SW("f2_w1", a, a + ROWS2), L.xt[0])
                        mm3(pe, ps[0:ROWS2, 512:1024], SW("f2_w3", a, a + ROWS2), L.xt[0]).then_inc(*pair.fill(st, n, "h", r, c))
                    pe.wait_ge(*hid_v.at(st, n, r, 7))
                    experts_out(st, L, r, lambda e: [
                        (L.hid[:, 2 * e + c, :], W("f2_w2", ROWS2, (8 * r + 2 * e + c) * 64, (8 * r + 2 * e + c) * 64 + 64), ROWS2)
                        for c in range(2)], 4)

            def l1(L):
                turn_features("l1", L, 0)
                wait_xt("l1", L.n, 0)
                for what in "qk":
                    for a in range(2):
                        project("l1", L, (what, 0, a), 0, [("l1_" + what, 256 * a + 128 * j, 256 * a + 128 * j + 128) for j in range(2)])
                values("l1", L, 0, "l1_v", 64)

            with pe.Fori(0, CLIPS // LANES) as turn:
                for st in STAGES:
                    if st == "tok":
                        for L in lanes:
                            tok(L)
                        attention("tok")
                        for L in lanes:
                            out_heads("tok", L, "t_wo")
                    if st == "sparse":
                        for L in lanes:
                            sparse(L)
                    if st == "ffn0":
                        for L in lanes:
                            ffn0(L)
                    if st == "l1":
                        for L in lanes:
                            l1(L)
                        attention("l1")
                        for L in lanes:
                            out_heads("l1", L, "l1_wo")
                    if st == "ffn1":
                        for L in lanes:
                            ffn_relu("ffn1", L, "f1_g", 8, "f1_w1", "f1_w2", "f1_b2", 1)
                    if st == "l2":
                        for L in lanes:
                            l2_attn(L)
                    if st == "causal":
                        for L in lanes:
                            causal(L)
                        attention("causal")
                        for L in lanes:
                            out_heads("causal", L, "c_wo")
                    if st == "ffn2":
                        for L in lanes:
                            ffn2(L)
                    if st == "l3":
                        for L in lanes:
                            l3_attn(L)
                    if st == "ffn3":
                        for L in lanes:
                            ffn_relu("ffn3", L, "f3_g", 16, "f3_w1", "f3_w2", "f3_b2", 2)
                next_turn(pe, "pe")


        @block.scalar
        def _(act):
            def copy(o, i, scale=1.0):
                return act.activation(o, i, ACT.Copy, scale=scale)

            act.wait_ge(loaded, 48)
            act.activation(sig_c[:, :], W("a_Cp"), ACT.Sigmoid).then_inc(*set_a.inc("c"))
            act.activation(sig_b[:, :], W("a_BpT", NST), ACT.Sigmoid).then_inc(*set_a.inc("b"))
            act.wait_ge(*set_v.at("all"))
            units = [0]
            split_units = []

            def features(st, L, srcs=1):
                act.wait_ge(*part1_ready.at(st, L.n))
                T = srcs * NT
                act.activation(L.parts[:, 0:T, 1:5:3, :], L.parts[:, 0:T, 0:1, :].broadcast_to([P, T, 2, 64]), ACT.Copy)\
                    .then_inc(*part1_copied.inc(st, L.n))
                for src in range(srcs):
                    act.wait_ge(*pair.filled(st, L.n, "turn", src))
                    ps = pair.view(st, L.n, "turn", src)[:].bitcast(BF16)
                    copy(L.xt[src][:, 0:2, :].rearrange("p a b -> p (a b)"), ps[:, 0:1024]).then_inc(*pair.free(st, L.n, "turn", src))

            def heads_f(st, L, what, bias, scale):
                u = units[0]
                units[0] += 1
                act.wait_ge(*pair.filled(st, L.n, what))
                if u >= 2:
                    act.wait_ge(*heads_ready.at(*split_units[u - 2]))
                split_units.append((st, L.n, what))
                ps = pair.view(st, L.n, what)
                for j in range(2):
                    f = f_t[:, u % 2, j * 512:(j + 1) * 512]
                    if bias is None:
                        i = act.activation(f, ps[:, j * 512:(j + 1) * 512], ACT.Copy if isinstance(scale, float) else ACT.Identity, scale=scale)
                    else:
                        i = act.activation(f, ps[:, j * 512:(j + 1) * 512], ACT.Identity, bias=bias[j], scale=scale)
                finish(act, i, pair, st, L.n, what)
                first_parts(u, W(("q" if what[0] == "q" else "k") + "a1"))

            def first_parts(u, a1):
                act.activation(pm_t[:, u % 2, :], f_t[:, u % 2, :], ACT.Copy, scale=a1).then_inc(*p1_ready.inc(u))

            def attention(st):
                cfg = ATT[st]

                def exponentials(i, jt):
                    act.wait_ge(*pair.filled(st, i, "e", jt))
                    u = 4 * i + jt
                    if u >= 3:
                        act.wait_ge(*prob_used.at(st, (u - 3) // 4, (u - 3) % 4))
                    c0 = jt * P if st == "causal" else 0
                    ps = pair.view(st, i, "e", jt)[:].rearrange("p (j c) -> p j c", j=2)[:, :, c0:512]
                    pb = prob[u % 3].rearrange("p (j c) -> p j c", j=2)[:, :, c0:512]
                    act.activation(pb, ps, ACT.Exp, scale=0.25 if st == "causal" else 1.0).then_inc(*pair.free(st, i, "e", jt))

                def outputs(i):
                    act.wait_ge(*prob_used.at(st, i, 3))
                    if i >= 5:
                        act.wait_ge(*turned_bank.filled(st, i - 4, "s"))
                    copy(o_t[:, (i // 2) % 2, :], heads_t[:, :]).then_inc(*heads_bank.free(st, i))

                run_schedule(len(cfg["units"]), dict(e=exponentials, o=outputs))
                for L in lanes:
                    act.wait_ge(*pair.filled(st, L.n, "at"))
                    copy(L.att[0:64, 0, :], pair.view(st, L.n, "at")[0:64, 0:512]).then_inc(*pair.free(st, L.n, "at"))

            def tok(L):
                n = L.n
                features("tok", L, 3)
                for a in range(2):
                    heads_f("tok", L, ("q", 0, a), [t_bqs[:, 2 * a + j:2 * a + j + 1] for j in range(2)], 0.125)
                for src in range(2):
                    for a in range(2):
                        heads_f("tok", L, ("k", src, a), [W("t_bk", P, 2 * a + j, 2 * a + j + 1) for j in range(2)], 1.0)

            def l1(L):
                features("l1", L)
                for a in range(2):
                    heads_f("l1", L, ("q", 0, a), None, l1_qscale[:, 0:1])
                for a in range(2):
                    heads_f("l1", L, ("k", 0, a), [W("l1_bk", P, 2 * a + j, 2 * a + j + 1) for j in range(2)], 1.0)

            def sparse(L):
                st, n = "sparse", L.n
                act.wait_ge(*act_req.at(st, n, "tanh"))
                act.activation(L.normed[:, 0:NT, :], L.base[:, :, :], ACT.Tanh, scale=W("a_alpha")).then_inc(*act_rsp.inc(st, n, "tanh"))
                features(st, L)
                act.wait_ge(*act_req.at(st, n, "soft"))
                for t in range(NT):
                    i = act.activation(L.hid[:, t, :], L.att[:, 2, :], ACT.Exp, bias=L.small[:, 3, t, 0:1], scale=L.small[:, 0, t, 0:1],
                                       accum_out=L.small[:, 4, t, 0:1])
                i.then_inc(*act_rsp.inc(st, n, "soft"))
                act.wait_ge(*pair.filled(st, n, "pt"))
                ps = pair.view(st, n, "pt")
                copy(L.hid[:, 4, :], ps[:, 0:512])
                copy(L.hid[0:TAIL, 5, :], ps[0:TAIL, 512:1024]).then_inc(*pair.free(st, n, "pt"))

            def small_exp(st, L, tag, o, i):
                act.wait_ge(*act_req.at(st, L.n, tag))
                act.activation(o, i, ACT.Exp).then_inc(*act_rsp.inc(st, L.n, tag))

            def top2_exp(st, L):
                small_exp(st, L, "top", L.small[:, 6, :, 1:2], L.small[:, 6, :, 0:1])

            def ffn0(L):
                st, n = "ffn0", L.n
                features(st, L)
                small_exp(st, L, "probs", L.small[:, 3, :, 0:4], L.small[:, 2, :, 0:4])
                top2_exp(st, L)
                act.wait_ge(*pair.filled(st, n, "s1"))
                act.activation(L.hid[0:64, 5, :], pair.view(st, n, "s1")[0:64, 0:512], ACT.Relu, bias=W("f0_bs1", 64))\
                    .then_inc(*pair.free(st, n, "s1"))
                for a in range(2):
                    act.wait_ge(*pair.filled(st, n, ("e1", a)))
                    ps = pair.view(st, n, ("e1", a))
                    for j in range(2):
                        i = act.activation(L.hid[:, 2 * a + j, :], ps[:, j * 512:(j + 1) * 512], ACT.Relu,
                                           bias=W("f0_be1", P, 2 * a + j, 2 * a + j + 1))
                    i.then_inc(*pair.free(st, n, ("e1", a)))

            def ffn_h(st, L, rounds, b1, func):
                n = L.n
                features(st, L)
                top2_exp(st, L)
                for r in range(rounds):
                    if r:
                        act.wait_ge(*pair.filled(st, n, "out", r - 1, 1))
                    for a in range(4):
                        act.wait_ge(*pair.filled(st, n, ("h", r, a)))
                        ps = pair.view(st, n, ("h", r, a))
                        for j in range(2 if st == "ffn1" else 1):
                            e = 2 * a + j
                            last = j == 1 or st == "ffn3"
                            ins = act.activation(L.hid[:, e, :], ps[:, j * 512:(j + 1) * 512], func,
                                                 bias=W(b1, P, 8 * r + e, 8 * r + e + 1))
                            if last:
                                ins.then_inc(*pair.free(st, n, ("h", r, a)))

            def plain(st, L, bq, bk, qscale):
                n = L.n
                features(st, L)
                act.wait_ge(*pair.filled(st, n, "qk"))
                ps = pair.view(st, n, "qk")
                if bq is None:
                    copy(L.att[0:64, 0, :], ps[0:64, 0:512], scale=0.125)
                    copy(L.att[0:64, 1, :], ps[0:64, 512:1024]).then_inc(*pair.free(st, n, "qk"))
                else:
                    act.activation(L.att[0:64, 0, :], ps[0:64, 0:512], ACT.Identity, bias=bq, scale=qscale)
                    act.activation(L.att[0:64, 1, :], ps[0:64, 512:1024], ACT.Identity, bias=bk)\
                        .then_inc(*pair.free(st, n, "qk"))

            def l2(L):
                st, n = "l2", L.n
                plain(st, L, None, None, None)
                for a in range(2):
                    act.wait_ge(*maxima_ready.at(st, n, a))
                    ps = pair.view(st, n, "s", a)
                    for j in range(2):
                        jt = 2 * a + j
                        i = act.activation(L.hid[:, jt, :], ps[:, j * 512:(j + 1) * 512], ACT.Exp, bias=L.small[:, 10, jt, 0:1],
                                           accum_out=L.small[:, 11, jt, 0:1])
                    i.then_inc(*pair.free(st, n, "s", a))

            def l3(L):
                st, n = "l3", L.n
                plain(st, L, l3_bqs[0:64, 0:1], W("l3_bk", 64), l3_qscale[0:64, 0:1])
                act.wait_ge(*pair.filled(st, n, "turnm"))
                copy(L.att[64:65, 0, :], pair.view(st, n, "turnm")[64:65, 0:512]).then_inc(*pair.free(st, n, "turnm"))
                for a in range(2):
                    act.wait_ge(*pair.filled(st, n, "s", a))
                    ps = pair.view(st, n, "s", a)
                    act.activation(L.hid[:, 2 * a:2 * a + 2, :].rearrange("p a b -> p (a b)"), ps[:, :], ACT.Exp)\
                        .then_inc(*pair.free(st, n, "s", a))

            def ffn2(L):
                st, n = "ffn2", L.n
                features(st, L)
                small_exp(st, L, "probs", L.small[:, 3, :, 0:8], L.small[:, 2, :, 0:8])
                for r in range(2):
                    for c in range(8):
                        k = 8 * r + c
                        act.wait_ge(*pair.filled(st, n, "h", r, c))
                        if k >= 2:
                            act.wait_ge(*hid_v.at(st, n, (k - 2) // 8, (k - 2) % 8))
                        act.activation(L.att[0:ROWS2, k % 2, :], pair.view(st, n, "h", r, c)[0:ROWS2, 0:512], ACT.Silu)\
                            .then_inc(*hid_a.inc(st, n, r, c))

            with act.Fori(0, CLIPS // LANES) as turn:
                for st in STAGES:
                    for L in lanes:
                        if st == "tok":
                            tok(L)
                        elif st == "sparse":
                            sparse(L)
                        elif st == "ffn0":
                            ffn0(L)
                        elif st == "l1":
                            l1(L)
                        elif st == "ffn1":
                            ffn_h(st, L, 1, "f1_b1", ACT.Gelu)
                        elif st == "l2":
                            l2(L)
                        elif st == "causal":
                            features(st, L)
                            for what in [(w, g) for w in "qk" for g in range(2)]:
                                act.wait_ge(*f_ready.at(st, L.n, what))
                                first_parts(units[0], W({"q": "c", "k": "d"}[what[0]] + "a1"))
                                split_units.append((st, L.n, what))
                                units[0] += 1
                        elif st == "ffn2":
                            ffn2(L)
                        elif st == "l3":
                            l3(L)
                        elif st == "ffn3":
                            ffn_h(st, L, 2, "f3_b1", ACT.Relu)
                    if st in ATT:
                        attention(st)
                next_turn(act, "act")

        @block.gpsimd
        def _(pool):
            units = [0]

            def rstd(st, L, tag, T):
                pool.wait_ge(*var_ready.at(st, L.n, tag))
                pool.tensor_tensor(L.stat[:, 3, 0:T], L.stat[:, 2, 0:T], minus_half[:, 0:T], ALU.pow)\
                    .then_inc(*rstd_ready.inc(st, L.n, tag))

            def split_heads(st, L, what, dst):
                u = units[0]
                units[0] += 1
                b = u % 2
                pool.wait_ge(*p1_ready.at(u))
                pool.tensor_tensor(f_t[:, b, :], f_t[:, b, :], pm_t[:, b, :], ALU.subtract).then_inc(*y1_ready.inc(u))
                pool.wait_ge(*p2_ready.at(u))
                if isinstance(dst, int):
                    for j in range(2):
                        r = slice(64 * j, 64 * j + 64)
                        o = L.qs[r, 4 * dst + j:4 * dst + j + 3:2, :]
                        i, m = [t[r, b, :].rearrange("p (a c) -> p a c", a=2) for t in (f_t, pm_t)]
                        ins = pool.tensor_tensor(o, i, m, ALU.subtract)
                        if j == 0:
                            finish(pool, ins, p_step)
                        else:
                            finish(pool, ins, heads_ready, st, L.n, what)
                    return
                pool.tensor_tensor(dst, f_t[:, b, :], pm_t[:, b, :], ALU.subtract).then_inc(*heads_ready.inc(st, L.n, what))

            def two(t, a):
                return t[:, a:a + 2, :].rearrange("p a b -> p (a b)")

            with pool.Fori(0, CLIPS // LANES) as turn:
                for st in STAGES:
                    for L in lanes:
                        n = L.n
                        if st == "tok":
                            rstd(st, L, "ln", 12)
                            for a in range(2):
                                split_heads(st, L, ("q", 0, a), a)
                            for src in range(2):
                                for a in range(2):
                                    split_heads(st, L, ("k", src, a), two(L.ks, 4 * src + 2 * a))
                        elif st == "sparse":
                            rstd(st, L, "ln", NT)
                            rstd(st, L, "norm", NT)
                        elif st == "l1":
                            rstd(st, L, "ln", NT)
                            for a in range(2):
                                split_heads(st, L, ("q", 0, a), a)
                            for a in range(2):
                                split_heads(st, L, ("k", 0, a), two(L.ks, 2 * a))
                        elif st == "causal":
                            rstd(st, L, "ln", NT)
                            rstd(st, L, "rms", NT)
                            for g in range(2):
                                split_heads(st, L, ("q", g), two(L.ks, 4 + 2 * g))
                            for g in range(2):
                                split_heads(st, L, ("k", g), two(L.ks, 2 * g))
                        elif st == "ffn2":
                            rstd(st, L, "rms", NT)
                        else:
                            rstd(st, L, "ln", NT)
                            if st in ("ffn1", "ffn3"):
                                rstd(st, L, "ln2", NT)
                next_turn(pool, "pool")

        @block.sync
        def _(sp):
            sp.dma_start(whole[:, :], wwhole).then_inc(loaded, 16)
            sp.dma_start(f_t[0:3, 0, 0:1024], wbias[:, 0:1024]).then_inc(loaded, 16)
            sp.dma_start(f_t[0:3, 1, 0:BIAS_N - 1024], wbias[:, 1024:BIAS_N]).then_inc(loaded, 16)
            for c in range(-(-SPLIT_N // CHUNK)):
                a, b = c * CHUNK, min((c + 1) * CHUNK, SPLIT_N)
                sp.wait_ge(*set_v.at("free", c))
                sp.dma_start(f_t[:, c % 2, 0:b - a], wsplit[:, a:b]).then_inc(staged[c % 2], 16)
            sp.wait_ge(*set_v.at("kernels"))
            sp.dma_start(skew.rearrange("n (s t) -> n s t", t=SKEW), kern[:, :].unsqueeze(1).broadcast_to([NST, P, SKEW]))\
                .then_inc(skew_done, 16)
            sp.wait_ge(skew_done, 16)
            sp.dma_start(scan_t[:, :, :], skew[:, 0:P * (SKEW - 1)].rearrange("n (s t) -> s n t", t=SKEW - 1)[:, :, 0:TOPK])\
                .then_inc(scan_loaded, 16)
            clip_in = x.rearrange("b (t p) d -> b p t d", p=P)
            clip_out = out.rearrange("b (t p) d -> b p t d", p=P)
            with sp.Fori(0, CLIPS // LANES) as turn:
                for L in lanes:
                    sp.dma_start(L.x, clip_in[turn * LANES + L.n]).then_inc(clip_loaded[L.n], 16)
                for L in lanes:
                    sp.wait_ge(*out_ready.at(L.n))
                    sp.dma_start(clip_out[turn * LANES + L.n], L.h[:, :, :]).then_inc(stored, 16)
                sp.wait_ge(stored, 16 * LANES)
                sp.wait_ge(turn_done, 4)
                for s in turn_sems + [stored, turn_done]:
                    sp.sem_clear(s)
                for e in go.values():
                    sp.sem_inc(e, 1)

        @block.vector
        def _(dve):
            def step(i):
                finish(dve, i, v_step)

            def bcast(a, shape, axis=2):
                return a.unsqueeze(axis).broadcast_to(shape)

            def start(i, *event):
                finish(dve, i, set_v, *(event or ("step", set_v.count)))

            dve.wait_ge(loaded, 48)
            start(dve.memset(kern[:, :], 0.0))
            start(dve.tensor_copy(power[:, :], W("a_A", NST)))
            start(dve.tensor_copy(power_t[:, :], W("a_AT", NST)))
            dve.wait_ge(*set_a.at("b"))
            start(dve.tensor_copy(kern[:, 0:1], sig_b[:, :]), "power", 0)
            for k in range(8):
                T = 1 << k
                n = min(T, TOPK - T)
                dve.wait_ge(*set_t.at("power", k))
                start(dve.tensor_copy(kern[:, T:T + n], pair_t[0][0:NST, 0:n]))
                start(dve.tensor_copy(power[:, :], pair_t[1][0:NST, 0:NST]))
                start(dve.tensor_copy(power_t[:, :], pair_t[2][0:NST, 0:NST]), *(("power", k + 1) if k < 7 else ("kernels",)))
            for a, b, s in ((0, 1024, 0), (1024, BIAS_N, 1)):
                f, pm, y = f_t[0:3, s, 0:b - a], pm_t[0:3, s, 0:b - a], y_t[0:3, s, 0:b - a]
                start(dve.tensor_scalar(pm, f, W("ra1", 3), None, ALU.mult))
                start(dve.tensor_tensor(y, f, pm, ALU.subtract))
                start(dve.tensor_scalar(pm, y, W("ra2", 3), None, ALU.mult))
                start(dve.tensor_tensor(bias3[:, a:b], y, pm, ALU.subtract), "free", s)
            for c in range(-(-SPLIT_N // CHUNK)):
                a, b = c * CHUNK, min((c + 1) * CHUNK, SPLIT_N)
                s, n = c % 2, b - a
                dve.wait_ge(staged[s], 16 * (c // 2 + 1))
                f, p1, p2, y = f_t[:, s, 0:n], pm_t[:, 0, 0:n], pm_t[:, 1, 0:n], y_t[:, 0, 0:n]
                start(dve.tensor_copy(p1, f))
                start(dve.tensor_tensor(y, f, p1, ALU.subtract), *(("free", c + 2) if c + 2 < -(-SPLIT_N // CHUNK) else ()))
                start(dve.tensor_copy(p2, y))
                start(dve.tensor_tensor(w_ca[0:64, a:b], y[0:64], p2[0:64], ALU.subtract))
                start(dve.tensor_copy(w_ca[64:P, a:b], p1[64:P]))
                start(dve.tensor_copy(w_ab[0:64, a:b], p1[0:64]))
                start(dve.tensor_copy(w_ab[64:P, a:b], p2[64:P]))
            for i in (
                dve.tensor_copy(identb[:, :], W("ident")),
                dve.tensor_copy(monesb[:, :], W("mones8")),
                dve.memset(onesb[:, :], 1.0),
                dve.memset(m_t[:, :, :, :, :], 0.0),
                dve.memset(mc_t[:, :, :, :, :], 0.0),
                dve.memset(qm_t[:, :, :, :], 0.0),
                dve.tensor_copy(causal_b[:, 0, :], W("negmask")),
                dve.tensor_copy(causal_b[:, 1, :], W("negmaskT")),
                dve.tensor_scalar(t_bqs[:, :], W("t_bq"), 0.125, None, ALU.mult),
                dve.tensor_scalar(t_bo2[:, :], W("t_bo"), 2.0, None, ALU.mult),
                dve.reciprocal(l3_qscale[:, :], W("l3_scale")),
                dve.reciprocal(l1_qscale[:, :], W("l1_temp")),
            ):
                i.then_inc(*set_v.inc("const", set_v.count))
            for L in lanes:
                for i in (dve.memset(L.v[:, :, :, :, :], 0.0), dve.memset(L.v16[:, :, :, :], 0.0), dve.memset(L.v64[:, :, 64:65], 1.0),
                          dve.memset(L.m3[:, :, :], 0.0), dve.memset(L.qs[:, :, :], 0.0)):
                    i.then_inc(*set_v.inc("const", set_v.count))
            dve.wait_ge(set_v.sem, set_v.count)
            start(dve.tensor_scalar(y_t[:, 0, 0:P], W("ident"), l1_qscale[:, 0:1], DIAG, ALU.mult, ALU.mult))
            start(dve.tensor_copy(diag3[:, 0, :], y_t[:, 0, 0:P]))
            start(dve.tensor_tensor(y_t[:, 1, 0:P], y_t[:, 0, 0:P], diag3[:, 0, :], ALU.subtract))
            start(dve.tensor_copy(diag3[:, 1, :], y_t[:, 1, 0:P]))
            start(dve.tensor_tensor(diag3[:, 2, :], y_t[:, 1, 0:P], diag3[:, 1, :], ALU.subtract))
            start(dve.tensor_scalar(l1_qscale[:, :], l1_qscale[:, :], 0.125, None, ALU.mult))
            start(dve.tensor_tensor(l3_bqs[:, :], W("l3_bq"), l3_qscale[:, :], ALU.mult))
            for L in lanes:
                for i in (dve.memset(L.v[:, :, :, :, 8:9], 1.0), dve.memset(L.v16[:, :, :, 16:17], 1.0)):
                    i.then_inc(*set_v.inc("const", set_v.count))
            dve.wait_ge(set_v.sem, set_v.count)
            start(dve.memset(minus_half[:, :], -0.5), "all")

            def layernorm(st, L, tag, src, T, dst, gamma=None, beta=None, eps=EPS, centre=True):
                if centre:
                    step(dve.tensor_reduce(L.stat[:, 0, 0:T], src, AX.X, ALU.add))
                    step(dve.tensor_scalar(L.stat[:, 1, 0:T], L.stat[:, 0, 0:T], 1.0 / DIM, None, ALU.mult))
                    step(dve.tensor_tensor(cent[:, 0:T, :], src, bcast(L.stat[:, 1, 0:T], [P, T, 64]), ALU.subtract))
                    src = cent[:, 0:T, :]
                step(dve.tensor_tensor(sq[:, 0:T, :], src, src, ALU.mult))
                step(dve.tensor_reduce(L.stat[:, 0, 0:T], sq[:, 0:T, :], AX.X, ALU.add))
                dve.tensor_scalar(L.stat[:, 2, 0:T], L.stat[:, 0, 0:T], 1.0 / DIM, eps, ALU.mult, ALU.add)\
                    .then_inc(*var_ready.inc(st, L.n, tag))
                dve.wait_ge(*rstd_ready.at(st, L.n, tag))
                step(dve.tensor_tensor(dst, src, bcast(L.stat[:, 3, 0:T], [P, T, 64]), ALU.mult))
                if gamma is not None:
                    step(dve.tensor_tensor(dst, dst, bcast(gamma, [P, T, 64], 1), ALU.mult))
                if beta is not None:
                    step(dve.tensor_tensor(dst, dst, bcast(beta, [P, T, 64], 1), ALU.add))

            def split_tokens(st, L, T=NT):
                x32 = L.normed12 if T == 12 else L.normed[:, :, :]
                finish(dve, dve.tensor_copy(L.parts[:, 0:T, 0, :], x32), part1_ready, st, L.n)
                step(dve.tensor_tensor(cent[:, 0:T, :], x32, L.parts[:, 0:T, 0, :], ALU.subtract))
                step(dve.tensor_copy(L.parts[:, 0:T, 2:4, :], bcast(cent[:, 0:T, :], [P, T, 2, 64])))
                dve.tensor_tensor(L.parts[:, 0:T, 5, :], cent[:, 0:T, :], L.parts[:, 0:T, 2, :], ALU.subtract)\
                    .then_inc(*parts_ready.inc(st, L.n))

            def turned(st, L, src=0):
                dve.wait_ge(*pair.filled(st, L.n, "turn", src))
                ps = pair.view(st, L.n, "turn", src)[:].bitcast(BF16)
                dve.tensor_copy(L.xt[src][:, 2, :], ps[:, 1024:1536]).then_inc(*pair.free(st, L.n, "turn", src))

            units = [0]

            def split2(a2):
                u = units[0]
                units[0] += 1
                dve.wait_ge(*y1_ready.at(u))
                dve.tensor_scalar(pm_t[:, u % 2, :], f_t[:, u % 2, :], a2, None, ALU.mult).then_inc(*p2_ready.inc(u))

            def values8(st, L, src, s, bias):
                dve.wait_ge(*pair.filled(st, L.n, "v", s))
                ps = pair.view(st, L.n, "v", s)
                for t in range(NT):
                    o, i = L.v[:, src, t, :, 0:8], ps[:, t * 64:(t + 1) * 64].rearrange("p (h d) -> p h d", h=8)
                    ins = dve.tensor_tensor(o, i, W(bias).rearrange("p (h d) -> p h d", h=8), ALU.add) if bias else dve.tensor_copy(o, i)
                finish(dve, ins, pair, st, L.n, "v", s)
                dve.nop().then_inc(*v_ready.inc(st, L.n, src))

            def attention(st):
                cfg = ATT[st]

                def maxima(i, it):
                    dve.wait_ge(*pair.filled(st, i, "m", it))
                    cols = (it + 1) * P if st == "causal" else 512
                    ps = pair.view(st, i, "m", it)[:].rearrange("p (j c) -> p j c", j=2)[:, :, 0:cols]
                    b = i % 2
                    finish(dve, dve.tensor_reduce(neg_t[:, b, 2 * it:2 * it + 2], ps, AX.X, ALU.max, negate=True), pair, st, i, "m", it)
                    if it < NT - 1:
                        return
                    neg = neg_t[:, b, 0:8].rearrange("p (t j) -> p t j", j=2)
                    left = m_left[:, b, :].rearrange("p (t j) -> p t j", j=2)
                    if st == "causal":
                        rows = [mc_t[:, b, :, :, 96 + k].rearrange("p j t -> p t j") for k in range(3)]
                    else:
                        rows = [m_t[:, b, 0, :, :].rearrange("p t (j c) -> p t j c", j=2)[:, :, :, 48 + k] for k in range(3)]
                    step(dve.tensor_copy(rows[0], neg))
                    step(dve.tensor_tensor(left, neg, rows[0], ALU.subtract))
                    step(dve.tensor_copy(rows[1], left))
                    dve.tensor_tensor(rows[2], left, rows[1], ALU.subtract).then_inc(*maxima_ready.inc(st, i))

                def shift(i):
                    n, src, g = cfg["units"][i]
                    L = lanes[n]
                    dve.wait_ge(*turned_bank.filled(st, i, "t"))
                    if i >= 2:
                        dve.wait_ge(*pair.filled(st, i - 2, "e", 3))
                    ps = turned_t[:].bitcast(BF16)
                    if st == "tok":
                        for j in range(2):
                            r = slice(64 * j, 64 * j + 64)
                            ins = dve.tensor_tensor(qm_t[r, i % 2, j, :], L.qs[r, 2 * g + j, :], ps[r, 0:512], ALU.add)
                            if j == 0:
                                step(ins)
                    elif st == "l1":
                        ins = dve.tensor_copy(qm1_t[:, i % 2, :], ps[:, 0:512])
                    else:
                        ins = dve.tensor_tensor(qmc_t[:, i % 2, :, :], L.ks[:, 4 + 2 * g:6 + 2 * g, :],
                                                ps[:, 0:1024].rearrange("p (j c) -> p j c", j=2), ALU.add)
                    finish(dve, ins, turned_bank, st, i, "t")
                    dve.nop().then_inc(*shift_ready.inc(st, i))

                def normalise(i):
                    n, src, g = cfg["units"][i]
                    L = lanes[n]
                    d = 16 if st == "causal" else 8
                    dve.wait_ge(*turned_bank.filled(st, i, "s"))
                    ps = turned_t[:].rearrange("p (t h c) -> p t h c", t=NT, h=4)
                    r = recip16[:, :, :].unsqueeze(3)
                    step(dve.reciprocal(r, ps[:, :, :, d:d + 1]))
                    og = g // 2
                    o = L.heads_out[:, :, 4 * d * og:4 * d * og + 4 * d].rearrange("p t (h c) -> p t h c", h=4)
                    if src == 0:
                        finish(dve, dve.tensor_tensor(o, ps[:, :, :, 0:d], r.broadcast_to([P, NT, 4, d]), ALU.mult), turned_bank, st, i, "s")
                    else:
                        x8 = red[:, :, :].rearrange("p a (t h c) -> p (a t) h c", h=4, t=2)
                        finish(dve, dve.tensor_tensor(x8, ps[:, :, :, 0:d], r.broadcast_to([P, NT, 4, d]), ALU.mult), turned_bank, st, i, "s")
                        step(dve.tensor_tensor(o, o, x8, ALU.add))
                    if i + 1 == len(cfg["units"]) or cfg["units"][i + 1][0] != n:
                        dve.nop().then_inc(*att_ready.inc(st, n))

                run_schedule(len(cfg["units"]), dict(m=maxima, t=shift, s=normalise))

            def rows_add(st, L, first, bias=None):
                dve.wait_ge(*pair.filled(st, L.n, "wo"))
                ps = pair.view(st, L.n, "wo")[:, 0:NT * 64].rearrange("p (t d) -> p t d", t=NT)
                if bias is not None:
                    if not first:
                        step(dve.tensor_tensor(L.h[:, :, :], L.h[:, :, :], bcast(bias, [P, NT, 64], 1), ALU.add))
                        bias = None
                o = L.h[:, :, :]
                finish(dve, dve.tensor_tensor(o, ps, o if bias is None else bcast(bias, [P, NT, 64], 1), ALU.add), pair, st, L.n, "wo")

            def gating(st, L, E, bias=None, soft=False, renorm=False):
                n, S = L.n, L.small
                Ep = max(E, 8)
                dve.wait_ge(*pair.filled(st, n, "gate"))
                ps = pair.view(st, n, "gate")[:, 0:NT * E].rearrange("p (t e) -> p t e", t=NT)
                if E < 8:
                    step(dve.memset(S[:, 0, :, E:8], NEG))
                if bias is not None:
                    ins = dve.tensor_tensor(S[:, 0, :, 0:E], ps, bcast(bias, [P, NT, E], 1), ALU.add)
                else:
                    ins = dve.tensor_copy(S[:, 0, :, 0:E], ps)
                finish(dve, ins, pair, st, n, "gate")
                if soft:
                    step(dve.tensor_reduce(S[:, 1, :, 0:1], S[:, 0, :, 0:E], AX.X, ALU.max))
                    finish(dve, dve.tensor_tensor(S[:, 2, :, 0:E], S[:, 0, :, 0:E], S[:, 1, :, 0:1].broadcast_to([P, NT, E]), ALU.subtract),
                           act_req, st, n, "probs")
                    dve.wait_ge(*act_rsp.at(st, n, "probs"))
                    step(dve.tensor_reduce(S[:, 1, :, 1:2], S[:, 3, :, 0:E], AX.X, ALU.add))
                    step(dve.reciprocal(S[:, 1, :, 2:3], S[:, 1, :, 1:2]))
                    step(dve.tensor_tensor(S[:, 0, :, 0:E], S[:, 3, :, 0:E], S[:, 1, :, 2:3].broadcast_to([P, NT, E]), ALU.mult))
                for t in range(NT):
                    step(dve.max(out=S[:, 4, t, 0:8], in_=S[:, 0, t, 0:Ep]))
                for t in range(NT):
                    step(dve.max_index(out=L.idx[:, t, :], in_max=S[:, 4, t, 0:8], in_values=S[:, 0, t, 0:Ep]))
                step(dve.tensor_copy(S[:, 5, :, 0:8], L.idx[:, :, :]))
                if renorm:
                    step(dve.tensor_tensor(S[:, 6, :, 0:1], S[:, 4, :, 0:1], S[:, 4, :, 1:2], ALU.add))
                    step(dve.tensor_scalar(S[:, 6, :, 0:1], S[:, 6, :, 0:1], 1e-9, None, ALU.add))
                    step(dve.reciprocal(S[:, 6, :, 1:2], S[:, 6, :, 0:1]))
                    step(dve.tensor_tensor(S[:, 7, :, 0:2], S[:, 4, :, 0:2], S[:, 6, :, 1:2].broadcast_to([P, NT, 2]), ALU.mult))
                else:
                    finish(dve, dve.tensor_tensor(S[:, 6, :, 0:1], S[:, 4, :, 1:2], S[:, 4, :, 0:1], ALU.subtract), act_req, st, n, "top")
                    dve.wait_ge(*act_rsp.at(st, n, "top"))
                    step(dve.tensor_scalar(S[:, 6, :, 2:3], S[:, 6, :, 1:2], 1.0, None, ALU.add))
                    step(dve.reciprocal(S[:, 7, :, 0:1], S[:, 6, :, 2:3]))
                    step(dve.tensor_tensor(S[:, 7, :, 1:2], S[:, 7, :, 0:1], S[:, 6, :, 1:2], ALU.mult))
                number = bcast(W("iotae", P, 0, E), [P, NT, E], 1)
                for k in range(2):
                    step(dve.tensor_tensor(S[:, 8 + k, :, 0:E], number, S[:, 5, :, k:k + 1].broadcast_to([P, NT, E]), ALU.is_equal))
                    step(dve.tensor_tensor(S[:, 8 + k, :, 0:E], S[:, 8 + k, :, 0:E], S[:, 7, :, k:k + 1].broadcast_to([P, NT, E]), ALU.mult))
                step(dve.tensor_tensor(S[:, 8, :, 0:E], S[:, 8, :, 0:E], S[:, 9, :, 0:E], ALU.add))
                if st == "ffn0":
                    step(dve.memset(S[:, 8, :, 4:5], 1.0))

            def combine(st, L, r, E, acc):
                for tp in range(2):
                    dve.wait_ge(*pair.filled(st, L.n, "out", r, tp))
                    ps = pair.view(st, L.n, "out", r, tp)[:].rearrange("p (t c) -> p t c", t=2)[:, :, 0:E * 64]\
                        .rearrange("p t (e d) -> p t e d", e=E)
                    w = bcast(L.small[:, 8, 2 * tp:2 * tp + 2, r * E:(r + 1) * E], [P, 2, E, 64], 3)
                    o = prod[:, 0:2 * E * 64].rearrange("p (t e d) -> p t e d", t=2, e=E)
                    finish(dve, dve.tensor_tensor(o, ps, w, ALU.mult), pair, st, L.n, "out", r, tp)
                    step(dve.tensor_reduce(red[:, :, :], o.rearrange("p t e d -> p t d e"), AX.X, ALU.add))
                    step(dve.tensor_tensor(acc[:, 2 * tp:2 * tp + 2, :], acc[:, 2 * tp:2 * tp + 2, :], red[:, :, :], ALU.add))

            def tok(L):
                n = L.n
                dve.wait_ge(clip_loaded[n], 16)
                layernorm("tok", L, "ln", L.x, 12, L.normed12, W("t_g"), W("t_b"))
                split_tokens("tok", L, 12)
                for src in range(3):
                    turned("tok", L, src)

            def tok_heads(L):
                for w in "qqkkkk":
                    split2(W(w + "a2"))
                for src in range(2):
                    values8("tok", L, src, src + 1, "t_bv")

            def sparse(L):
                st, n, S = "sparse", L.n, L.small
                layernorm(st, L, "ln", L.h[:, :, :], NT, L.base[:, :, :])
                finish(dve, dve.tensor_tensor(L.h[:, :, :], L.h[:, :, :], L.base[:, :, :], ALU.add), act_req, st, n, "tanh")
                dve.wait_ge(*act_rsp.at(st, n, "tanh"))
                xn = L.normed[:, 0:NT, :]
                step(dve.tensor_tensor(xn, xn, bcast(W("a_w"), [P, NT, 64], 1), ALU.mult))
                step(dve.tensor_tensor(xn, xn, bcast(W("a_b"), [P, NT, 64], 1), ALU.add))
                split_tokens(st, L)
                turned(st, L)
                dve.wait_ge(*pair.filled(st, n, "xp"))
                xp = L.hid[:, 6, :].rearrange("p (t e) -> p t e", t=NT)
                xq = L.hid[:, 7, :].rearrange("p (t e) -> p t e", t=NT)
                ps = pair.view(st, n, "xp")[:, 0:512].rearrange("p (t e) -> p t e", t=NT)
                finish(dve, dve.tensor_tensor(xp, ps, bcast(W("a_bin"), [P, NT, EXP], 1), ALU.add), pair, st, n, "xp")
                step(dve.tensor_tensor(xq, xp, xp, ALU.mult))
                step(dve.tensor_reduce(L.stat[:, 0, 0:NT], xq, AX.X, ALU.add))
                dve.tensor_scalar(L.stat[:, 2, 0:NT], L.stat[:, 0, 0:NT], 1e-24, None, ALU.max).then_inc(*var_ready.inc(st, n, "norm"))
                dve.wait_ge(*rstd_ready.at(st, n, "norm"))
                step(dve.tensor_tensor(xp, xp, bcast(L.stat[:, 3, 0:NT], [P, NT, EXP]), ALU.mult))
                for k, w in ((0, "a_wq"), (1, "a_wk")):
                    step(dve.tensor_tensor(xq, xp, bcast(W(w), [P, NT, EXP], 1), ALU.mult))
                    step(dve.tensor_reduce(S[:, k, :, 0:1], xq, AX.X, ALU.add))
                    step(dve.tensor_scalar(S[:, k, :, 0:1], S[:, k, :, 0:1], W("a_bq" if k == 0 else "a_bk"), None, ALU.add))
                diag = L.att[:, 0, :].rearrange("p (t e) -> p t e", t=NT)
                ident = bcast(W("ident"), [P, NT, P], 1)
                finish(dve, dve.tensor_tensor(diag, ident, S[:, 1, :, 0:1].broadcast_to([P, NT, P]), ALU.mult), pe_req, st, n, "kdiag")
                dve.wait_ge(*pair.filled(st, n, "kb"))
                finish(dve, dve.tensor_copy(L.att[:, 2, :], pair.view(st, n, "kb")[:, 0:512]), pair, st, n, "kb")
                step(dve.tensor_reduce(S[:, 2, 0, 0:1], L.att[:, 2, :], AX.X, ALU.max))
                step(dve.tensor_reduce(S[:, 2, 0, 1:2], L.att[:, 2, :], AX.X, ALU.min))
                step(dve.tensor_scalar(S[:, 3, :, 0:1], S[:, 0, :, 0:1], S[:, 2, 0, 0:1], None, ALU.mult))
                step(dve.tensor_scalar(S[:, 3, :, 1:2], S[:, 0, :, 0:1], S[:, 2, 0, 1:2], None, ALU.mult))
                step(dve.tensor_tensor(S[:, 3, :, 0:1], S[:, 3, :, 0:1], S[:, 3, :, 1:2], ALU.max))
                finish(dve, dve.tensor_scalar(S[:, 3, :, 0:1], S[:, 3, :, 0:1], -1.0, None, ALU.mult), act_req, st, n, "soft")
                dve.wait_ge(*act_rsp.at(st, n, "soft"))
                step(dve.reciprocal(S[:, 4, :, 1:2], S[:, 4, :, 0:1]))
                recip = L.att[:, 1, :].rearrange("p (t e) -> p t e", t=NT)
                finish(dve, dve.tensor_copy(recip, S[:, 4, :, 1:2].broadcast_to([P, NT, P])), pe_req, st, n, "recip")
                dve.wait_ge(*pair.filled(st, n, "imp"))
                imp = L.att[:, 3, :]
                finish(dve, dve.tensor_scalar(imp, pair.view(st, n, "imp")[:, 0:512], 1.0 / TOK, None, ALU.mult), pair, st, n, "imp")
                step(dve.tensor_tensor(diag, imp.rearrange("p (t e) -> p t e", t=NT), ident, ALU.mult))
                step(dve.tensor_reduce(S[:, 5, :, 0:1], diag, AX.X, ALU.add))
                for t in range(NT):
                    step(dve.tensor_scalar(r_t[:, :], imp, S[:, 5, t, 0:1], 0.0, ALU.is_gt, ALU.add, accum_out=S[:, 6, t, 0:1]))
                    c = (t + 1) * P
                    if t:
                        step(dve.tensor_scalar(r_t[:, 0:t * P], imp[:, 0:t * P], S[:, 5, t, 0:1], 0.0, ALU.is_equal, ALU.add,
                                               accum_out=S[:, 6, t, 1:2]))
                    else:
                        step(dve.memset(S[:, 6, 0, 1:2], 0.0))
                    step(dve.scalar_tensor_tensor(out=r_t[:, 0:P], in0=imp[:, t * P:c], scalar=S[:, 5, t, 0:1], in1=W("ltmask", P, 0, P),
                                                  op0=ALU.is_equal, op1=ALU.mult, accum_out=S[:, 6, t, 2:3]))
                step(dve.tensor_reduce(S[:, 7, :, 0:1], S[:, 6, :, 0:3], AX.X, ALU.add))
                finish(dve, dve.tensor_tensor(perm[:, :, :], bcast(W("iota"), [P, NT, 160], 1), S[:, 7, :, 0:1].broadcast_to([P, NT, 160]),
                                              ALU.is_equal), pe_req, st, n, "perm")
                dve.wait_ge(*pair.filled(st, n, "xs"))
                ps = pair.view(st, n, "xs")
                step(dve.tensor_copy(L.hid[0:TAIL, 7, P:2 * P], ps[0:TAIL, 512:512 + P]))
                finish(dve, dve.tensor_copy(L.hid[:, 7, 0:P], ps[:, 0:P]), pair, st, n, "xs")
                step(dve.memset(L.att[:, 0, 0:DCONV - 1], 0.0))
                acc = L.att[:, 0, DCONV - 1:DCONV - 1 + TOPK]
                for k in range(NST):
                    b, c = k // 6, 512 * (k % 6 // 3) + TOPK * (k % 3)
                    if k % 6 == 0:
                        dve.wait_ge(*pair.filled(st, n, "scan", b))
                    ps = pair.view(st, n, "scan", b)[:, c:c + TOPK]
                    if k == 0:
                        i = dve.tensor_scalar(acc, ps, sig_c[:, 0:1], None, ALU.mult)
                    else:
                        i = dve.scalar_tensor_tensor(out=acc, in0=ps, scalar=sig_c[:, k:k + 1], in1=acc, op0=ALU.mult, op1=ALU.add)
                    if k % 6 == 5 or k == NST - 1:
                        finish(dve, i, pair, st, n, "scan", b)
                    else:
                        step(i)
                y = L.att[:, 0, 160:160 + TOPK]
                step(dve.tensor_scalar(y, L.att[:, 0, 0:TOPK], W("a_conv", P, 0, 1), None, ALU.mult))
                for j in range(1, DCONV):
                    i = dve.scalar_tensor_tensor(out=y, in0=L.att[:, 0, j:j + TOPK], scalar=W("a_conv", P, j, j + 1), in1=y,
                                                 op0=ALU.mult, op1=ALU.add)
                    finish(dve, i, pe_req, st, n, "conv" if j == DCONV - 1 else ("conv", j))
                dve.wait_ge(*pair.filled(st, n, "xo"))
                ps = pair.view(st, n, "xo")
                step(dve.tensor_tensor(L.att[:, 1, 0:64], ps[:, 0:64], W("a_bout"), ALU.add))
                finish(dve, dve.tensor_tensor(L.att[0:TAIL, 1, 64:128], ps[0:TAIL, 512:576], W("a_bout", TAIL), ALU.add), pair, st, n, "xo")
                dve.nop().then_inc(*pe_req.inc(st, n, "xo"))
                dve.wait_ge(*pair.filled(st, n, "back"))
                ps = pair.view(st, n, "back")[:, 0:NT * 64].rearrange("p (t d) -> p t d", t=NT)
                finish(dve, dve.tensor_tensor(L.h[:, :, :], ps, L.h[:, :, :], ALU.add), pair, st, n, "back")

            def ffn0(L):
                st, n = "ffn0", L.n
                layernorm(st, L, "ln", L.h[:, :, :], NT, L.normed[:, 0:NT, :])
                split_tokens(st, L)
                turned(st, L)
                gating(st, L, 4, W("f0_gb"), soft=True)
                dve.wait_ge(*pair.filled(st, n, "s2"))
                dve.tensor_scalar(L.hid[:, 4, :], pair.view(st, n, "s2")[:, 0:512], W("f0_bs2"), 0.0, ALU.add, ALU.max)\
                    .then_inc(*pair.free(st, n, "s2"))
                for a in range(2):
                    dve.wait_ge(*pair.filled(st, n, "e2", a))
                    ps = pair.view(st, n, "e2", a)
                    for j in range(2):
                        e = 2 * a + j
                        i = dve.tensor_scalar(L.att[0:64, e, :], ps[0:64, j * 512:(j + 1) * 512], W("f0_be2", 64, e, e + 1), 0.0, ALU.add, ALU.max)
                    i.then_inc(*pair.free(st, n, "e2", a))
                combine(st, L, 0, 5, L.h)

            def l1(L):
                layernorm("l1", L, "ln", L.h[:, :, :], NT, L.normed[:, 0:NT, :])
                split_tokens("l1", L)
                turned("l1", L)

            def l1_heads(L):
                for w in "qqkk":
                    split2(W(w + "a2"))
                values8("l1", L, 0, 0, None)

            def ffn1(L):
                st = "ffn1"
                layernorm(st, L, "ln", L.h[:, :, :], NT, L.base[:, :, :])
                layernorm(st, L, "ln2", L.base[:, :, :], NT, L.normed[:, 0:NT, :], W("f1_gam"), W("f1_bet"))
                split_tokens(st, L)
                turned(st, L)
                gating(st, L, 8, W("f1_gb"))
                combine(st, L, 0, 8, L.h)

            def values64(st, L, bias=None):
                dve.wait_ge(*pair.filled(st, L.n, "v", 0))
                ps = pair.view(st, L.n, "v", 0)[:, 0:NT * 64].rearrange("p (t d) -> p t d", t=NT)
                v = L.v64[:, :, 0:64]
                ins = dve.tensor_copy(v, ps) if bias is None else dve.tensor_tensor(v, ps, bcast(bias, [P, NT, 64], 1), ALU.add)
                finish(dve, ins, pair, st, L.n, "v", 0)

            def l2(L):
                st, n, S = "l2", L.n, L.small
                layernorm(st, L, "ln", L.h[:, :, :], NT, L.normed[:, 0:NT, :])
                split_tokens(st, L)
                turned(st, L)
                values64(st, L)
                for a in range(2):
                    dve.wait_ge(*pair.filled(st, n, "s", a))
                    ps = pair.view(st, n, "s", a)[:].rearrange("p (j c) -> p j c", j=2)
                    dve.tensor_reduce(S[:, 10, 2 * a:2 * a + 2, 0:1], ps, AX.X, ALU.max, negate=True).then_inc(*maxima_ready.inc(st, n, a))
                for a in range(2):
                    dve.wait_ge(*pair.read(st, n, "s", a))
                step(dve.reciprocal(S[:, 11, :, 1:2], S[:, 11, :, 0:1]))
                finish(dve, dve.tensor_tensor(L.v64[:, :, 0:64], L.v64[:, :, 0:64], S[:, 11, :, 1:2].broadcast_to([P, NT, 64]), ALU.mult),
                       v_ready, st, n, "scaled")
                rows_add(st, L, False)

            def causal(L):
                st, n = "causal", L.n
                layernorm(st, L, "ln", L.h[:, :, :], NT, L.base[:, :, :])
                layernorm(st, L, "rms", L.base[:, :, :], NT, L.normed[:, 0:NT, :], W("c_ln1"), eps=EPS_RMS, centre=False)
                split_tokens(st, L)
                turned(st, L)

            def causal_heads(L):
                st, n = "causal", L.n
                whats = [(w, g) for w in "qk" for g in range(2)]
                masks = {"q": "c", "k": "d"}
                for k, (w, g) in enumerate(whats):
                    u = units[0] + (k > 0)
                    dve.wait_ge(*(heads_ready.at(st, n, whats[k - 2]) if k >= 2 else heads_ready.at("l1", n, ("k", 0, k))))
                    for j in range(2):
                        key = (st, n, (w, 2 * g + j))
                        f = f_t[:, u % 2, j * 512:(j + 1) * 512]
                        dve.wait_ge(*pair.filled(*key))
                        ps = pair.view(*key)
                        step(dve.tensor_tensor(prod[:, 0:512], ps[:, 0:512], W("cos"), ALU.mult))
                        finish(dve, dve.tensor_tensor(prod[:, 512:1024], ps[:, 512:1024], W("sin"), ALU.mult), pair, *key)
                        if w == "q":
                            step(dve.tensor_tensor(f, prod[:, 0:512], prod[:, 512:1024], ALU.add))
                        else:
                            step(dve.scalar_tensor_tensor(out=f, in0=prod[:, 0:512], scalar=W("c_bk"), in1=prod[:, 512:1024],
                                                          op0=ALU.add, op1=ALU.add))
                    dve.nop().then_inc(*f_ready.inc(st, n, (w, g)))
                    if k:
                        split2(W(masks[whats[k - 1][0]] + "a2"))
                split2(W(masks["k"] + "a2"))
                dve.wait_ge(*pair.filled(st, n, "v", 0))
                ps = pair.view(st, n, "v", 0)[:, 0:NT * 32].rearrange("p (t h d) -> p t h d", t=NT, h=2)
                step(dve.tensor_copy(L.v16[:, :, 0:4:2, 0:16], ps))
                finish(dve, dve.tensor_copy(L.v16[:, :, 1:4:2, 0:16], ps), pair, st, n, "v", 0)
                dve.nop().then_inc(*v_ready.inc(st, n, 0))

            def causal_out(L):
                st, n = "causal", L.n
                dve.wait_ge(*pair.filled(st, n, "wo"))
                ps = pair.view(st, n, "wo")[:, 0:NT * 64].rearrange("p (t d) -> p t d", t=NT)
                finish(dve, dve.tensor_tensor(L.base[:, :, :], ps, L.base[:, :, :], ALU.add), pair, st, n, "wo")
                step(dve.tensor_tensor(L.h[:, :, :], L.h[:, :, :], L.base[:, :, :], ALU.add))

            def ffn2(L):
                st, n = "ffn2", L.n
                layernorm(st, L, "rms", L.base[:, :, :], NT, L.normed[:, 0:NT, :], W("c_ln2"), eps=EPS_RMS, centre=False)
                split_tokens(st, L)
                turned(st, L)
                gating(st, L, 8, soft=True, renorm=True)
                for r in range(2):
                    if r:
                        combine(st, L, 0, 4, L.h)
                    for c in range(8):
                        dve.wait_ge(*hid_a.at(st, n, r, c))
                        k = 8 * r + c
                        ps = pair.view(st, n, "h", r, c)
                        finish(dve, dve.tensor_tensor(L.hid[0:ROWS2, c, :], ps[0:ROWS2, 512:1024], L.att[0:ROWS2, k % 2, :], ALU.mult),
                               pair, st, n, "h", r, c)
                        dve.nop().then_inc(*hid_v.inc(st, n, r, c))
                combine(st, L, 1, 4, L.h)

            def l3(L):
                st, n, S = "l3", L.n, L.small
                layernorm(st, L, "ln", L.h[:, :, :], NT, L.normed[:, 0:NT, :])
                split_tokens(st, L)
                turned(st, L)
                values64(st, L, W("l3_bv"))
                step(dve.memset(L.att[64:65, 1, :], 1.0))
                dve.nop().then_inc(*v_ready.inc(st, n, 0))
                for a in range(2):
                    dve.wait_ge(*pair.filled(st, n, "m", a))
                    ps = pair.view(st, n, "m", a)[:].rearrange("p (j c) -> p j c", j=2)
                    i = dve.tensor_reduce(L.m3[:, 2 * a:2 * a + 2, 64:65], ps, AX.X, ALU.max, negate=True)
                    finish(dve, i, pair, st, n, "m", a)
                dve.nop().then_inc(*maxima_ready.inc(st, n))
                dve.wait_ge(*pair.filled(st, n, "wo"))
                ps = pair.view(st, n, "wo")[:, 0:NT * 65].rearrange("p (t d) -> p t d", t=NT)
                step(dve.reciprocal(S[:, 11, :, 1:2], ps[:, :, 64:65]))
                finish(dve, dve.tensor_tensor(cent[:, 0:NT, :], ps[:, :, 0:64], S[:, 11, :, 1:2].broadcast_to([P, NT, 64]), ALU.mult),
                       pair, st, n, "wo")
                step(dve.tensor_tensor(L.h[:, :, :], L.h[:, :, :], cent[:, 0:NT, :], ALU.add))

            def ffn3(L):
                st, n = "ffn3", L.n
                layernorm(st, L, "ln", L.h[:, :, :], NT, L.normed[:, 0:NT, :])
                step(dve.tensor_copy(L.base[:, :, :], L.normed[:, 0:NT, :]))
                split_tokens(st, L)
                turned(st, L)
                gating(st, L, 16, W("f3_gb"))
                for r in range(2):
                    for a in range(4):
                        e = 2 * a + 1
                        dve.wait_ge(*pair.filled(st, n, ("h", r, a)))
                        if r and a == 0:
                            dve.wait_ge(*pair.filled(st, n, "out", 0, 1))
                        ps = pair.view(st, n, ("h", r, a))
                        dve.tensor_scalar(L.hid[:, e, :], ps[:, 512:1024], W("f3_b1", P, 8 * r + e, 8 * r + e + 1), 0.0, ALU.add, ALU.max)\
                            .then_inc(*pair.free(st, n, ("h", r, a)))
                    combine(st, L, r, 8, L.base)
                layernorm(st, L, "ln2", L.base[:, :, :], NT, L.normed[:, 0:NT, :], W("f3_gam"), W("f3_bet"))
                finish(dve, dve.tensor_tensor(L.h[:, :, :], L.h[:, :, :], L.normed[:, 0:NT, :], ALU.add), out_ready, n)

            each = dict(tok=tok, sparse=sparse, ffn0=ffn0, l1=l1, ffn1=ffn1, l2=l2, causal=causal, ffn2=ffn2, l3=l3, ffn3=ffn3)
            heads = dict(tok=tok_heads, l1=l1_heads, causal=causal_heads)
            with dve.Fori(0, CLIPS // LANES) as turn:
                for st in STAGES:
                    for L in lanes:
                        each[st](L)
                        if st in ATT:
                            heads[st](L)
                    if st in ATT:
                        attention(st)
                        for L in lanes:
                            if st == "tok":
                                rows_add(st, L, True, t_bo2[:, :])
                            elif st == "l1":
                                rows_add(st, L, False, W("l1_bo"))
                            else:
                                causal_out(L)
                next_turn(dve, "dve")


def whole_array(w):
    import numpy as np
    a = np.zeros((P, WHOLE_N), np.float32)

    def put(name, v, rows=None):
        at, n = WHOLE_AT[name]
        v = np.asarray(v)
        a[0:v.shape[0], at:at + v.shape[1]] = v

    def rows(name, v):
        at, n = WHOLE_AT[name]
        a[:, at:at + n] = np.asarray(v).reshape(1, -1)

    p, c = np.arange(P)[:, None], np.arange(P)[None, :]
    put("ident", (p == c).astype(np.float32))
    rows("ones", np.ones(P, np.float32))
    put("ltmask", (c < p).astype(np.float32))
    rows("iota", np.arange(160, dtype=np.float32))
    rows("iotae", np.arange(16, dtype=np.float32))
    put("negmask", np.where(c > p, np.float32(CAUSAL), np.float32(0)))
    put("negmaskT", np.where(p > c, np.float32(CAUSAL), np.float32(0)))
    inv_freq = 1.0 / 10000.0 ** (np.arange(0, 16, 2, dtype=np.float32) / 16)
    freqs = np.outer(np.arange(TOK, dtype=np.float32), inv_freq)
    emb = np.concatenate([freqs, freqs], axis=-1)
    cos, sin = np.cos(emb).T, np.sin(emb).T
    sin = np.concatenate([-sin[0:8], sin[8:16]])
    for k in range(6):
        for name, t in (("cos", cos), ("sin", sin)):
            at, _ = WHOLE_AT[name]
            a[16 * k:16 * k + 16, at:at + TOK] = t
        for j in range(2):
            r = slice(64 * j + 8 * k, 64 * j + 8 * k + 8)
            a[r, WHOLE_AT["qa1"][0]] = Q_PART[k] >= 2
            a[r, WHOLE_AT["qa2"][0]] = Q_PART[k] == 3
            a[r, WHOLE_AT["ka1"][0]] = K_PART[k] >= 2
            a[r, WHOLE_AT["ka2"][0]] = K_PART[k] == 3
            for g in range(4):
                head = slice((2 * g + j) * 8, (2 * g + j) * 8 + 8)
                a[r, WHOLE_AT["t_bq"][0] + g] = w["L0_tok_bq"][head]
                a[r, WHOLE_AT["t_bk"][0] + g] = w["L0_tok_bk"][head]
        r = slice(16 * k, 16 * k + 16)
        a[r, WHOLE_AT["ca1"][0]] = Q_PART[k] >= 2
        a[r, WHOLE_AT["ca2"][0]] = Q_PART[k] == 3
        a[r, WHOLE_AT["da1"][0]] = K_PART[k] >= 2
        a[r, WHOLE_AT["da2"][0]] = K_PART[k] == 3
    a[1:3, WHOLE_AT["ra1"][0]] = 1
    a[2:3, WHOLE_AT["ra2"][0]] = 1
    for j in range(2):
        r = slice(64 * j + 48, 64 * j + 51)
        a[r, WHOLE_AT["mones8"][0] + j * P:WHOLE_AT["mones8"][0] + (j + 1) * P] = 1
        a[r, WHOLE_AT["t_bk"][0]:WHOLE_AT["t_bk"][0] + 4] = 1
        a[r, WHOLE_AT["l1_bk"][0]:WHOLE_AT["l1_bk"][0] + 4] = 1
    a[96:99, WHOLE_AT["c_bk"][0]] = 1
    for name, v in (("t_g", "L0_tok_ln_g"), ("t_b", "L0_tok_ln_b"), ("t_bv", "L0_tok_bv"), ("t_bo", "L0_tok_bo"),
                    ("a_alpha", "L0_attn_alpha"), ("a_w", "L0_attn_dyt_w"), ("a_b", "L0_attn_dyt_b"), ("a_bin", "L0_attn_b_in"),
                    ("a_wq", "L0_attn_w_q"), ("a_wk", "L0_attn_w_k"), ("a_bq", "L0_attn_b_q"), ("a_bk", "L0_attn_b_k"),
                    ("a_bout", "L0_attn_b_out"), ("f0_gb", "L0_ffn_gb"), ("l1_bo", "L1_attn_b_proj"), ("l1_temp", "L1_attn_temperature"),
                    ("f1_gam", "L1_ffn_gamma"), ("f1_bet", "L1_ffn_beta"), ("f1_gb", "L1_ffn_br"), ("c_ln1", "L2_ffn_ln1_w"),
                    ("c_ln2", "L2_ffn_ln2_w"), ("l3_bv", "L3_attn_bv"), ("l3_scale", "L3_attn_scale"), ("f3_gb", "L3_ffn_gate_b"),
                    ("f3_gam", "L3_ffn_gamma"), ("f3_bet", "L3_ffn_beta")):
        rows(name, w[v])
    put("a_Cp", w["L0_attn_Cp"])
    put("a_A", w["L0_attn_A"])
    put("a_AT", w["L0_attn_A"].T)
    put("a_BpT", w["L0_attn_Bp"].reshape(NST, 1))
    put("a_conv", w["L0_attn_conv_w"][:, 0, :])
    put("a_wout", w["L0_attn_w_out"].T)
    put("f0_bs1", w["L0_ffn_sb1"][:, None])
    put("f0_s2", w["L0_ffn_sW2"])
    put("f0_bs2", w["L0_ffn_sb2"][:, None])
    put("f0_be1", w["L0_ffn_eb1"].T)
    put("f0_e2", w["L0_ffn_eW2"].transpose(1, 0, 2).reshape(P, 256))
    put("f0_be2", w["L0_ffn_eb2"].T)
    put("f0_w3", w["L0_ffn_eW3"].transpose(1, 0, 2).reshape(64, 256))
    a[:, WHOLE_AT["f0_w3"][0] + 256:WHOLE_AT["f0_w3"][0] + 320] = w["L0_ffn_sW3"]
    put("f1_b1", w["L1_ffn_b1"].T)
    put("f1_w2", w["L1_ffn_W2"].transpose(1, 0, 2).reshape(P, 512))
    put("f2_w2", w["L2_ffn_w2"].reshape(8, 64, 2, HALF).transpose(3, 0, 2, 1).reshape(HALF, 1024))
    put("t_wo", w["L0_tok_Wo"].T)
    put("l1_wo", w["L1_attn_w_proj"].T)
    put("c_wo", w["L2_ffn_wo"].T)
    put("l3_bq", w["L3_attn_bq"][:, None])
    put("l3_bk", w["L3_attn_bk"][:, None])
    put("f3_b1", w["L3_ffn_b1"].T)
    put("f3_w2", w["L3_ffn_w2"].transpose(1, 0, 2).reshape(P, 1024))
    return a


def split_array(w):
    import numpy as np
    a = np.zeros((P, SPLIT_N), np.float32)

    def put(name, v):
        at, n = SPLIT_AT[name]
        a[0:64, at:at + n] = v
        a[64:P, at:at + n] = v

    def heads8(name, v):
        t = np.zeros((64, 4, 2, 64), np.float32)
        for k in range(6):
            t[:, :, :, 8 * k:8 * k + 8] = v.T.reshape(64, 4, 2, 8)
        put(name, t.reshape(64, 512))

    def heads16(name, v, repeat, swap):
        t = np.zeros((64, 4, P), np.float32)
        u = v.T.reshape(64, 4 // repeat, 16)
        if swap:
            u = np.concatenate([u[:, :, 8:16], u[:, :, 0:8]], axis=2)
        for k in range(6):
            t[:, :, 16 * k:16 * k + 16] = np.repeat(u, repeat, axis=1)
        put(name, t.reshape(64, 512))

    def experts(name, v):
        put(name, v.transpose(1, 0, 2).reshape(64, -1))

    heads8("t_q", w["L0_tok_Wq"])
    heads8("t_k", w["L0_tok_Wk"])
    put("t_v", w["L0_tok_Wv"].T)
    put("a_in", w["L0_attn_w_in"].T)
    put("f0_s1", w["L0_ffn_sW1"])
    experts("f0_e1", w["L0_ffn_eW1"])
    put("f0_g", w["L0_ffn_gW"])
    heads8("l1_q", w["L1_attn_w_qkv"][0:64])
    heads8("l1_k", w["L1_attn_w_qkv"][64:128])
    put("l1_v", w["L1_attn_w_qkv"][128:192].T)
    put("f1_g", w["L1_ffn_Wr"])
    experts("f1_w1", w["L1_ffn_W1"])
    for k, name in (("q", "Wq"), ("k", "Wk"), ("v", "Wv")):
        put("l2_" + k, w["L2_attn_" + name].T)
        put("l3_" + k, w["L3_attn_" + name].T)
    heads16("c_q", w["L2_ffn_wq"], 1, False)
    heads16("c_qs", w["L2_ffn_wq"], 1, True)
    heads16("c_k", w["L2_ffn_wk"], 2, False)
    heads16("c_ks", w["L2_ffn_wk"], 2, True)
    put("c_v", w["L2_ffn_wv"].T)
    put("f2_g", w["L2_ffn_router_w"].T)
    for name, v in (("f2_w1", w["L2_ffn_w1"]), ("f2_w3", w["L2_ffn_w3"])):
        t = np.zeros((64, 16, ROWS2), np.float32)
        t[:, :, 0:HALF] = v.reshape(16, HALF, 64).transpose(2, 0, 1)
        put(name, t.reshape(64, -1))
    put("f3_g", w["L3_ffn_gate_w"])
    experts("f3_w1", w["L3_ffn_w1"])
    return a


def bias_array(w):
    import numpy as np
    a = np.zeros((3, BIAS_N), np.float32)
    at = BIAS_AT["f0_b3"][0]
    a[:, at:at + 256] = w["L0_ffn_eb3"].reshape(1, 256)
    a[:, at + 256:at + 320] = w["L0_ffn_sb3"].reshape(1, 64)
    for name, v in (("f1_b2", w["L1_ffn_b2"]), ("f3_b2", w["L3_ffn_b2"])):
        at, n = BIAS_AT[name]
        a[:, at:at + n] = v.reshape(1, n)
    return a


def kernel(**inputs):
    import numpy as np
    import concourse.bacc as bacc
    from concourse.bass_utils import run_bass_kernel_spmd as run

    w = {k: np.asarray(v) for k, v in inputs.items()}
    arrays = {"in_x": np.ascontiguousarray(w["x"]), "in_split": split_array(w), "in_whole": whole_array(w), "in_bias": bias_array(w)}
    known = {}
    for _ in range(2):
        nc = bacc.Bacc("TRN2", target_bir_lowering=False, num_devices=1)
        noted = {}
        args = [nc.dram_tensor(n, a.shape, F32, kind="ExternalInput").ap() for n, a in arrays.items()]
        skew = nc.dram_tensor("skew", (NST, P * SKEW), F32, kind="Internal").ap()
        out = nc.dram_tensor("out", (CLIPS, TOK, DIM), F32, kind="ExternalOutput").ap()
        audio_tower(nc, args[0], args[1], args[2], args[3], skew, out, known, noted)
        known = noted
    r = run(nc, [arrays], core_ids=[0])
    return r.results[0]["out"]
```

```python
from contextlib import ExitStack

import concourse.bass as bass
from concourse import mybir

F32 = mybir.dt.float32
BF16 = mybir.dt.bfloat16
U32 = mybir.dt.uint32
ALU = mybir.AluOpType
ACT = mybir.ActivationFunctionType
AX = mybir.AxisListType

P = 128
CLIPS, ROWS, DIM = 16, 1536, 64
TOK = ROWS // 3
NT = TOK // P
LANES = 2
HEADS, HD = 8, 8
EPS = 1e-5
EPS_RMS = 1e-6
EXP, NST, DCONV = 128, 16, 4
TOPK = int(TOK * 0.3)
TAIL = TOPK - P
SKEW = P + TOPK + 2
HID = int(8 / 3 * DIM)
HALF = HID // 2
ROWS2 = 96
NEG = -3.0e38
CAUSAL = -1.0e30
DIAG = 1.0e9

Q_PART = (1, 1, 2, 2, 1, 3)
K_PART = (1, 2, 1, 2, 3, 1)

SPLIT = [
    ("t_q", 512), ("t_k", 512), ("t_v", 64), ("a_in", 128),
    ("f0_s1", 64), ("f0_e1", 512), ("f0_g", 4),
    ("l1_q", 512), ("l1_k", 512), ("l1_v", 64), ("f1_g", 8), ("f1_w1", 1024),
    ("l2_q", 64), ("l2_k", 64), ("l2_v", 64),
    ("c_q", 512), ("c_k", 512), ("c_qs", 512), ("c_ks", 512), ("c_v", 32),
    ("f2_g", 8), ("f2_w1", 16 * ROWS2), ("f2_w3", 16 * ROWS2),
    ("l3_q", 64), ("l3_k", 64), ("l3_v", 64), ("f3_g", 16), ("f3_w1", 2048),
]
WHOLE = [
    ("ident", 128), ("ones", 128), ("ltmask", 128), ("iota", 160), ("iotae", 16),
    ("cos", 512), ("sin", 512),
    ("qa1", 1), ("qa2", 1), ("ka1", 1), ("ka2", 1), ("ca1", 1), ("ca2", 1), ("da1", 1), ("da2", 1),
    ("ra1", 1), ("ra2", 1),
    ("t_g", 64), ("t_b", 64), ("t_bq", 4), ("t_bk", 4), ("t_bv", 64), ("t_wo", 64), ("t_bo", 64),
    ("a_alpha", 1), ("a_w", 64), ("a_b", 64), ("a_bin", 128), ("a_wq", 128), ("a_wk", 128), ("a_bq", 1), ("a_bk", 1),
    ("a_A", 16), ("a_AT", 16), ("a_BpT", 1), ("a_Cp", 16), ("a_conv", 4), ("a_wout", 64), ("a_bout", 64),
    ("f0_bs1", 1), ("f0_s2", 128), ("f0_bs2", 1), ("f0_be1", 4), ("f0_e2", 256), ("f0_be2", 4), ("f0_gb", 4),
    ("f0_w3", 5 * 64),
    ("l1_bk", 4), ("l1_wo", 64), ("l1_bo", 64), ("l1_temp", 1),
    ("f1_gam", 64), ("f1_bet", 64), ("f1_gb", 8), ("f1_b1", 8), ("f1_w2", 512),
    ("c_ln1", 64), ("c_ln2", 64), ("c_bk", 1), ("c_wo", 64), ("f2_w2", 1024),
    ("l3_bq", 1), ("l3_bk", 1), ("l3_bv", 64), ("l3_scale", 1),
    ("f3_gb", 16), ("f3_b1", 16), ("f3_w2", 1024), ("f3_gam", 64), ("f3_bet", 64),
    ("negmask", 128), ("negmaskT", 128), ("mones8", 256),
]
BIASROW = [("f0_b3", 320), ("f1_b2", 512), ("f3_b2", 1024)]


def offsets(listing):
    at, out = 0, {}
    for name, n in listing:
        out[name] = (at, n)
        at += n
    return out, at


SPLIT_AT, SPLIT_N = offsets(SPLIT)
WHOLE_AT, WHOLE_N = offsets(WHOLE)
BIAS_AT, BIAS_N = offsets(BIASROW)
KEPT = WHOLE_AT["negmask"][0]
STAGES = ["tok", "sparse", "ffn0", "l1", "ffn1", "l2", "causal", "ffn2", "l3", "ffn3"]
CHUNK = 1024


class Signal:

    def __init__(self, name, sem, known, noted):
        self.name, self.sem, self.known, self.noted, self.count = name, sem, known, noted, 0

    def inc(self, *event):
        self.count += 1
        self.noted[(self.name, event)] = self.count
        return self.sem, 1

    def at(self, *event):
        assert not self.known or (self.name, event) in self.known, (self.name, event)
        return self.sem, self.known.get((self.name, event), 1)


class Banks:

    def __init__(self, name, slots, filled, freed, known, noted):
        self.name, self.slots, self.filled_sems, self.freed_sems = name, slots, filled, freed
        self.known, self.noted = known, noted
        self.order = []
        self.place = {}
        sums = [0] * len(slots)
        for n, key in enumerate(known.get((name, "order"), ())):
            sums[n % len(slots)] += known.get((name, "readers", key), 0)
            self.place[key] = (n % len(slots), n // len(slots) + 1, sums[n % len(slots)])
        noted[(name, "order")] = self.order

    def take(self, pe, *key):
        n = len(self.order)
        if n >= len(self.slots):
            pe.wait_ge(*self.read(*self.order[n - len(self.slots)]))
        self.order.append(key)
        return self.slots[n % len(self.slots)]

    def where(self, key):
        assert not self.known or key in self.place, key
        return self.place.get(key, (0, 1, 1))

    def view(self, *key):
        return self.slots[self.where(key)[0]]

    def fill(self, *key):
        return self.filled_sems[self.where(key)[0]], 1

    def filled(self, *key):
        slot, uses, _ = self.where(key)
        return self.filled_sems[slot], uses

    def free(self, *key):
        self.noted[(self.name, "readers", key)] = self.noted.get((self.name, "readers", key), 0) + 1
        return self.freed_sems[self.where(key)[0]], 1

    def read(self, *key):
        slot, _, readers = self.where(key)
        return self.freed_sems[slot], max(readers, 1)


def in_turn(lanes_steps):
    live = list(lanes_steps)
    while live:
        live = [steps for steps in live if next(steps, "end") != "end"]


def finish(eng, instruction, sig, *event):
    if isinstance(sig, Banks):
        instruction.then_inc(*sig.free(*event))
        eng.wait_ge(*sig.read(*event))
    else:
        instruction.then_inc(*sig.inc(*event))
        eng.wait_ge(sig.sem, sig.count)


def audio_tower(nc, x, wsplit, wwhole, wbias, skew, out, known, noted):
    ctx = ExitStack()
    with ctx:
        def sb(name, shape, dt=F32):
            return ctx.enter_context(nc.sbuf_tensor(name, shape, dt))

        def semaphore(name):
            return ctx.enter_context(nc.semaphore(name))

        turn_sems = []

        def turn_semaphore(name):
            turn_sems.append(semaphore(name))
            return turn_sems[-1]

        def signal(name):
            return Signal(name, turn_semaphore(name), known, noted)

        pair_t = [ctx.enter_context(nc.psum_tensor(f"pair{i}", [P, 1024], F32)) for i in range(3)]
        heads_t = ctx.enter_context(nc.psum_tensor("heads_bank", [P, 512], F32))
        turned_t = ctx.enter_context(nc.psum_tensor("turned_bank", [P, 512], F32))
        pair = Banks("pair", pair_t, [turn_semaphore(f"pair{i}_filled") for i in range(3)],
                     [turn_semaphore(f"pair{i}_freed") for i in range(3)], known, noted)
        heads_bank = Banks("heads", [heads_t], [turn_semaphore("heads_filled")], [turn_semaphore("heads_freed")],
                           known, noted)
        turned_bank = Banks("turned", [turned_t], [turn_semaphore("turned_filled")], [turn_semaphore("turned_freed")],
                            known, noted)

        whole = sb("whole", [P, KEPT])
        w_ab = sb("w_ab", [P, SPLIT_N], BF16)
        w_ca = sb("w_ca", [P, SPLIT_N], BF16)
        bias3 = sb("bias3", [3, BIAS_N], BF16)
        identb = sb("identb", [P, P], BF16)
        monesb = sb("monesb", [P, 256], BF16)
        onesb = sb("onesb", [3, P], BF16)
        minus_half = sb("minus_half", [P, 12])
        sig_b = sb("sig_b", [NST, 1])
        scan_t = sb("scan_t", [P, NST, TOPK])
        t_bqs = sb("t_bqs", [P, 4])
        t_bo2 = sb("t_bo2", [P, 64])
        l1_qscale = sb("l1_qscale", [P, 1])
        l3_qscale = sb("l3_qscale", [P, 1])
        l3_bqs = sb("l3_bqs", [P, 1])
        diag3 = sb("diag3", [P, 3, P], BF16)
        causal_b = sb("causal_b", [P, 2, P], BF16)

        def W(name, rows=P, a=0, b=None):
            at, n = WHOLE_AT[name]
            if at >= KEPT:
                return lanes[0].arena[0:rows, at - KEPT:at - KEPT + n]
            return whole[0:rows, at + a:at + (n if b is None else b)]

        sig_c = sb("sig_c", [EXP, NST])

        def SW(name, a=0, b=None):
            at, n = SPLIT_AT[name]
            b = n if b is None else b
            return w_ab[:, at + a:at + b], w_ca[:, at + a:at + b]

        class Lane:
            def __init__(self, n):
                self.n = n
                rows = sb(f"rows_{n}", [P, 1536])
                self.h, self.base, self.normed = [rows[:, 256 * k:256 * k + 256].rearrange("p (t d) -> p t d", t=NT)
                                                  for k in range(3)]
                self.small = rows[:, 768:1536].rearrange("p (a t e) -> p a t e", a=12, t=NT)
                self.stat = sb(f"stat_{n}", [P, 4, 12])
                self.xt0 = sb(f"xt0_{n}", [P, 3, 512], BF16)
                self.v64 = sb(f"v64_{n}", [P, NT, 65])
                self.heads_out = sb(f"heads_out_{n}", [P, NT, 64])
                self.idx = sb(f"idx_{n}", [P, 4, 8], U32)
                self.arena = sb(f"arena_{n}", [P, 6144])

                def part(a, n, dt=F32):
                    return self.arena[:, a:a + n] if dt == F32 else self.arena[:, a:a + n].bitcast(dt)
                self.qs = part(0, 2048, BF16).rearrange("p (a c) -> p a c", a=8)
                self.ks = part(2048, 2048, BF16).rearrange("p (a c) -> p a c", a=8)
                self.v = part(4096, 2048).rearrange("p (s t h d) -> p s t h d", s=2, t=NT, h=8)
                self.hid = part(0, 4096).rearrange("p (a c) -> p a c", a=8)
                self.att = part(4096, 2048).rearrange("p (a c) -> p a c", a=4)
                self.parts = part(0, 2304, BF16).rearrange("p (t a d) -> p t a d", t=12, a=6)
                self.x = part(2304, 768).rearrange("p (t d) -> p t d", t=12)
                self.normed12 = part(3072, 768).rearrange("p (t d) -> p t d", t=12)
                self.sq = part(4864, 768).rearrange("p (t d) -> p t d", t=12)
                self.cent = part(4096, 768).rearrange("p (t d) -> p t d", t=12)
                self.qm1 = part(5120, 512, BF16).rearrange("p (a c) -> p a c", a=2)
                self.qmc = part(0, 1024, BF16).rearrange("p (b a c) -> p b a c", b=2, a=2)
                self.v16 = part(4096, 512).rearrange("p (t h d) -> p t h d", t=NT, h=4)
                self.m3 = part(5120, NT * 65).rearrange("p (t d) -> p t d", t=NT)
                self.perm = prob_t[:, 1024 * n:1024 * n + NT * 160].rearrange("p (t r) -> p t r", t=NT)
                self.xt = [self.xt0[:, :, :]] + [rows[:, 768 * k:768 * k + 768].bitcast(BF16).rearrange("p (a c) -> p a c", a=3)
                                                 for k in range(2)]

        prob_t = sb("prob_t", [P, 3072])
        lanes = [Lane(n) for n in range(LANES)]
        kern = prob_t[0:NST, 0:SKEW]
        power = prob_t[0:NST, 512:512 + NST]
        power_t = prob_t[0:NST, 640:640 + NST]
        f_t = sb("f_t", [P, 2, 1024])
        pm_t = sb("pm_t", [P, 2, 1024], BF16)
        y_t = lanes[0].arena[:, 4096:6144].rearrange("p (a c) -> p a c", a=2)
        neg_t = sb("neg_t", [P, 2, 32])
        mc_t = sb("mc_t", [P, 2, 2, NT, P], BF16)
        m_t = mc_t[:, :, 0:1, :, :]
        m_left = sb("m_left", [P, 2, 8])
        qm_t = sb("qm_t", [P, 2, 2, 512], BF16)
        prob = [prob_t[:, 1024 * k:1024 * k + 1024] for k in range(3)]
        o_t = sb("o_t", [P, 2, 512])
        recip16 = sb("recip16", [P, NT, 4])
        prod = sb("prod", [P, 1024])
        red = sb("red", [P, 2, 64])

        def start_signal(name):
            return Signal(name, semaphore(name), known, noted)

        loaded = semaphore("loaded")
        staged = [semaphore("staged0"), semaphore("staged1")]
        set_v = start_signal("set_v")
        set_a = start_signal("set_a")
        set_p = start_signal("set_p")
        set_t = start_signal("set_t")
        skew_done = semaphore("skew_done")
        scan_loaded = semaphore("scan_loaded")
        stored = semaphore("stored")
        turn_done = semaphore("turn_done")
        go = {e: semaphore(f"go_{e}") for e in ("pe", "act", "dve", "pool")}
        clip_loaded = [turn_semaphore(f"clip_loaded{n}") for n in range(LANES)]

        def next_turn(eng, name):
            eng.nop().then_inc(turn_done, 1)
            eng.wait_ge(go[name], 1)
            eng.sem_clear(go[name])

        v_step = signal("v_step")
        a_step = signal("a_step")
        p_step = signal("p_step")
        var_ready = signal("var_ready")
        rstd_ready = signal("rstd_ready")
        part1_ready = signal("part1_ready")
        part1_copied = signal("part1_copied")
        parts_ready = signal("parts_ready")
        f_ready = signal("f_ready")
        p1_ready = signal("p1_ready")
        y1_ready = signal("y1_ready")
        p2_ready = signal("p2_ready")
        heads_ready = signal("heads_ready")
        early_ready = signal("early_ready")

        def split_done(st, n, what):
            return (early_ready if by_vector(st, n, what) else heads_ready).at(st, n, what)

        v_ready = signal("v_ready")
        maxima_ready = signal("maxima_ready")
        shift_ready = signal("shift_ready")
        prob_used = signal("prob_used")
        att_ready = signal("att_ready")
        act_req = signal("act_req")
        act_rsp = signal("act_rsp")
        pe_req = signal("pe_req")
        pool_rsp = signal("pool_rsp")
        hid_a = signal("hid_a")
        hid_v = signal("hid_v")
        out_ready = signal("out_ready")

        block = ctx.enter_context(nc.Block())

        def mm3(pe, o, w, xt, start=True, stop=True):
            ab, ca = w
            pe.matmul(o, ab, xt[:, 0, :], start=start, stop=False)
            pe.matmul(o, ab, xt[:, 1, :], start=False, stop=False)
            return pe.matmul(o, ca, xt[:, 2, :], start=False, stop=stop)

        def mm3t(pe, o, xt, t, w):
            ab, ca = w
            c = slice(t * P, (t + 1) * P)
            pe.matmul(o, xt[:, 0, c], ab, start=True, stop=False)
            pe.matmul(o, xt[:, 1, c], ab, start=False, stop=False)
            return pe.matmul(o, xt[:, 2, c], ca, start=False, stop=True)

        ATT = {
            "tok": dict(units=[(n, src, g) for n in range(LANES) for src in range(2) for g in range(4)],
                        qk=lambda L, src, g, j: (L.qs[:, 2 * g + j, :], L.ks[:, 4 * src + g, :]), mtiles=1, m=m_t,
                        needs=lambda src, g: [("q", 0, g // 2), ("k", src, g // 2)]),
            "l1": dict(units=[(n, 0, g) for n in range(LANES) for g in range(4)],
                       qk=lambda L, src, g, j: (L.qs[:, 2 * g + j, :], L.ks[:, g, :]), mtiles=1, m=m_t,
                       needs=lambda src, g: [("q", 0, g // 2), ("k", 0, g // 2)]),
            "causal": dict(units=[(n, 0, g) for n in range(LANES) for g in range(2)],
                           qk=lambda L, src, g, j: (L.ks[:, 4 + 2 * g + j, :], L.ks[:, 2 * g + j, :]), mtiles=2, m=mc_t,
                           needs=lambda src, g: [("q", g), ("k", g)]),
        }

        PIECES = {
            "tok": ([("q", 0, 0), ("k", 0, 0), ("v", 1), ("q", 0, 1), ("k", 0, 1), ("k", 1, 0), ("k", 1, 1), ("v", 2)], 5, 3),
            "l1": ([("q", 0, 0), ("k", 0, 0), ("v", 0), ("q", 0, 1), ("k", 0, 1)], 5, 3),
            "causal": ([("q", 0), ("k", 0), ("v", 0), ("q", 1), ("k", 1)], 5, 2),
        }

        def early_pieces(st):
            return PIECES[st][0][0:PIECES[st][1]]

        def by_vector(st, n, what):
            return st != "causal" and n == 0 and what in early_pieces(st)

        def late_pieces(st):
            pieces, early, every = PIECES[st]
            step, out = 0, []
            for L in lanes:
                for what in pieces[early if L.n == 0 else 0:]:
                    out.append((step, L, what))
                    step += 0 if what[0] == "v" else every
            return out

        def run_schedule(st, groups, do):
            late_split = 1 if st == "causal" else 4
            for step in range(4 * groups + 12):
                for at, L, what in late_pieces(st):
                    if at == step and "h" in do:
                        do["h"](L, what)
                for at, L, what in late_pieces(st):
                    if at + late_split == step and what[0] != "v" and "h2" in do:
                        do["h2"](L, what)
                for what, late in (("e", 7), ("w", 9), ("m", 0)):
                    k = step - late
                    if what in do and 0 <= k < 4 * groups:
                        do[what](k // 4, k % 4)
                for what, late in (("t", 5), ("o", 12), ("s", 14)):
                    k = step - late
                    if what in do and k >= 0 and k % 4 == 0 and k // 4 < groups and (what == "t" or k // 4 % 2 == 1):
                        do[what](k // 4)

        @block.tensor
        def _(pe):
            for k in range(8):
                T = 1 << k
                n = min(T, TOPK - T)
                pe.wait_ge(*set_v.at("power", k))
                pe.matmul(pair_t[0][0:NST, 0:n], power_t[:, :], kern[:, 0:n], start=True, stop=True)
                pe.matmul(pair_t[1][0:NST, 0:NST], power_t[:, :], power[:, :], start=True, stop=True)
                pe.matmul(pair_t[2][0:NST, 0:NST], power[:, :], power_t[:, :], start=True, stop=True).then_inc(*set_t.inc("power", k))
            pe.wait_ge(*set_v.at("all"))
            pe.wait_ge(scan_loaded, 16)

            def turn_features(st, L, src):
                n = L.n
                pe.wait_ge(*part1_copied.at(st, n))
                pe.wait_ge(*parts_ready.at(st, n))
                ps = pair.take(pe, st, n, "turn", src)[:].bitcast(BF16)
                for s in range(3):
                    for t in range(NT):
                        mm = pe.transpose(ps[:, s * 512 + t * P:s * 512 + (t + 1) * P],
                                          L.parts[:, src * NT + t, 2 * s:2 * s + 2, :].rearrange("p a d -> p (a d)"),
                                          identb[:, :])
                mm.then_inc(*pair.fill(st, n, "turn", src))

            def wait_xt(st, n, src):
                pe.wait_ge(*pair.read(st, n, "turn", src))

            def project(st, L, what, src, w, tiles=2):
                ps = pair.take(pe, st, L.n, what)
                for j in range(tiles):
                    mm = mm3(pe, ps[:, j * 512:(j + 1) * 512], SW(*w[j]), L.xt[src])
                mm.then_inc(*pair.fill(st, L.n, what))

            def values(st, L, src, w, cols):
                ps = pair.take(pe, st, L.n, "v", src)
                for t in range(NT):
                    mm = mm3t(pe, ps[:, t * cols:(t + 1) * cols], L.xt[src], t, SW(w))
                mm.then_inc(*pair.fill(st, L.n, "v", src))

            def piece(st, L, what):
                src = {"q": 0, "k": what[1] + 1, "v": what[1]}[what[0]] if st == "tok" else 0
                wait_xt(st, L.n, src)
                if what[0] == "v":
                    values(st, L, what[1], dict(tok="t_v", l1="l1_v", causal="c_v")[st], 32 if st == "causal" else 64)
                elif st == "causal":
                    for tile in (2 * what[1], 2 * what[1] + 1):
                        project(st, L, (what[0], tile), 0, [("c_" + what[0], 128 * tile, 128 * tile + 128),
                                                            ("c_" + what[0] + "s", 128 * tile, 128 * tile + 128)])
                else:
                    w, a = ("t_" if st == "tok" else "l1_") + what[0], what[2]
                    project(st, L, what, src, [(w, 256 * a + 128 * j, 256 * a + 128 * j + 128) for j in range(2)])

            def attention(st):
                cfg = ATT[st]
                units = cfg["units"]

                def scores(i, it):
                    n, src, g = units[i]
                    L = lanes[n]
                    if it == 0:
                        for what in cfg["needs"](src, g):
                            pe.wait_ge(*split_done(st, n, what))
                    cols = (it + 1) * P if st == "causal" else 512
                    ps = pair.take(pe, st, i, "m", it)
                    for j in range(2):
                        q, k = cfg["qk"](L, src, g, j)
                        mm = pe.matmul(ps[:, j * 512:j * 512 + cols], q[:, it * P:(it + 1) * P], k[:, 0:cols],
                                       start=True, stop=st == "tok")
                        d = ps[:, j * 512 + it * P:j * 512 + (it + 1) * P]
                        if st == "l1":
                            for a in range(3):
                                mm = pe.matmul(d, identb[:, :], diag3[:, a, :], start=False, stop=a == 2)
                        if st == "causal":
                            mm = pe.matmul(d, identb[:, :], causal_b[:, 0, :], start=False, stop=True)
                    mm.then_inc(*pair.fill(st, i, "m", it))

                def turn_maxima(i):
                    pe.wait_ge(*maxima_ready.at(st, i))
                    ps = turned_bank.take(pe, st, i, "t")[:].bitcast(BF16)
                    for j in range(cfg["mtiles"]):
                        for t in range(NT):
                            mm = pe.transpose(ps[:, j * 512 + t * P:j * 512 + (t + 1) * P], cfg["m"][:, i % 2, j, t, :],
                                              identb[:, :])
                    mm.then_inc(*turned_bank.fill(st, i, "t"))

                def shifted(i, jt):
                    n, src, g = units[i]
                    L = lanes[n]
                    if jt == 0:
                        pe.wait_ge(*shift_ready.at(st, i))
                    c0 = jt * P if st == "causal" else 0
                    ps = pair.take(pe, st, i, "e", jt)
                    for j in range(2):
                        q, k = cfg["qk"](L, src, g, j)
                        k = k[:, jt * P:(jt + 1) * P]
                        o = ps[:, j * 512 + c0:(j + 1) * 512]
                        d = ps[:, j * 512 + jt * P:j * 512 + (jt + 1) * P]
                        if st == "l1":
                            pe.matmul(o, k, q, start=True, stop=False)
                            for a in range(3):
                                pe.matmul(d, identb[:, :], diag3[:, a, :], start=False, stop=False)
                            mm = pe.matmul(o, monesb[:, j * P:(j + 1) * P], L.qm1[:, i % 2, :], start=False, stop=True)
                        else:
                            mm = pe.matmul(o, k, (L.qmc if st == "causal" else qm_t)[:, i % 2, j, c0:512], start=True, stop=st == "tok")
                        if st == "causal":
                            mm = pe.matmul(d, identb[:, :], causal_b[:, 1, :], start=False, stop=True)
                    mm.then_inc(*pair.fill(st, i, "e", jt))

                def weigh(i, jt):
                    n, src, g = units[i]
                    L = lanes[n]
                    pe.wait_ge(*pair.read(st, i, "e", jt))
                    if g % 2 == 0 and jt == 0:
                        pe.wait_ge(*v_ready.at(st, n, src))
                        heads_bank.take(pe, st, i + 1)
                    c0 = jt * P if st == "causal" else 0
                    for j in range(2):
                        h4 = (g % 2) * 2 + j
                        v = L.v16[:, jt, 2 * g + j, :] if st == "causal" else L.v[:, src, jt, 2 * g + j, :]
                        mm = pe.matmul(heads_t[32 * h4:32 * h4 + 32, c0:512], v,
                                       prob[(4 * i + jt) % 3][:, j * 512 + c0:(j + 1) * 512],
                                       start=jt == 0, stop=jt == NT - 1)
                    mm.then_inc(*prob_used.inc(st, i, jt))

                def turn_outputs(i):
                    pe.wait_ge(*heads_bank.read(st, i))
                    ps = turned_bank.take(pe, st, i, "s")
                    for t in range(NT):
                        mm = pe.transpose(ps[:, t * P:(t + 1) * P], o_t[:, (i // 2) % 2, t * P:(t + 1) * P], W("ident"))
                    mm.then_inc(*turned_bank.fill(st, i, "s"))

                for what in early_pieces(st):
                    piece(st, lanes[0], what)
                run_schedule(st, len(units), dict(h=lambda L, what: piece(st, L, what), m=scores, t=turn_maxima, e=shifted, w=weigh,
                                                  s=turn_outputs))

            def out_heads(st, L, w):
                n = L.n
                pe.wait_ge(*att_ready.at(st, n))
                ps = pair.take(pe, st, n, "at")
                for t in range(NT):
                    mm = pe.transpose(ps[0:64, t * P:(t + 1) * P], L.heads_out[:, t, :], W("ident"))
                mm.then_inc(*pair.fill(st, n, "at"))
                yield
                pe.wait_ge(*pair.read(st, n, "at"))
                ps = pair.take(pe, st, n, "wo")
                for t in range(NT):
                    mm = pe.matmul(ps[:, t * 64:(t + 1) * 64], L.att[0:64, 0, t * P:(t + 1) * P], W(w, 64), start=True, stop=True)
                mm.then_inc(*pair.fill(st, n, "wo"))

            def sparse(L):
                st, n = "sparse", L.n
                turn_features(st, L, 0)
                yield
                wait_xt(st, n, 0)
                ps = pair.take(pe, st, n, "xp")
                for t in range(NT):
                    mm = mm3t(pe, ps[:, t * P:(t + 1) * P], L.xt[0], t, SW("a_in"))
                mm.then_inc(*pair.fill(st, n, "xp"))
                yield
                pe.wait_ge(*pe_req.at(st, n, "kdiag"))
                ps = pair.take(pe, st, n, "kb")
                pe.matmul(ps[:, 0:512], W("ones"), L.att[:, 0, :], start=True, stop=True).then_inc(*pair.fill(st, n, "kb"))
                yield
                pe.wait_ge(*pe_req.at(st, n, "recip"))
                ps = pair.take(pe, st, n, "imp")
                for t in range(NT):
                    mm = pe.matmul(ps[:, 0:512], L.att[:, 1, t * P:(t + 1) * P], L.hid[:, t, :], start=t == 0, stop=t == NT - 1)
                mm.then_inc(*pair.fill(st, n, "imp"))
                yield
                pe.wait_ge(*pe_req.at(st, n, "perm"))
                ps = pair.take(pe, st, n, "xs")
                pv = L.perm
                for c, m in ((0, P), (1, TAIL)):
                    for t in range(NT):
                        mm = pe.matmul(ps[0:m, c * 512:c * 512 + EXP], pv[:, t, c * P:c * P + m], L.hid[:, 6, t * P:(t + 1) * P],
                                       start=t == 0, stop=t == NT - 1)
                mm.then_inc(*pair.fill(st, n, "xs"))
                ps = pair.take(pe, st, n, "pt")
                for c, m in ((0, P), (1, TAIL)):
                    for t in range(NT):
                        mm = pe.transpose(ps[0:m, c * 512 + t * P:c * 512 + (t + 1) * P], pv[:, t, c * P:c * P + m], W("ident"))
                mm.then_inc(*pair.fill(st, n, "pt"))
                pe.wait_ge(*pair.read(st, n, "xs"))
                for b in range(3):
                    ps = pair.take(pe, st, n, "scan", b)
                    for k in range(2):
                        s0, s1 = 6 * b + 3 * k, min(6 * b + 3 * k + 3, NST)
                        if s0 < s1:
                            o = ps[:, k * 512:k * 512 + (s1 - s0) * TOPK]
                            pe.matmul(o, L.hid[:, 7, 0:P], scan_t[:, s0:s1, :].rearrange("p n t -> p (n t)"), start=True, stop=False)
                            mm = pe.matmul(o.rearrange("p (n t) -> p n t", t=TOPK)[:, :, P:TOPK], L.hid[0:TAIL, 7, P:2 * P],
                                           scan_t[0:TAIL, s0:s1, 0:TAIL], start=False, stop=True)
                    mm.then_inc(*pair.fill(st, n, "scan", b))
                yield
                pe.wait_ge(*pe_req.at(st, n, "conv"))
                ps = pair.take(pe, st, n, "xo")
                y = L.att[:, 0, 160:160 + TOPK]
                pe.matmul(ps[:, 0:64], y[:, 0:P], W("a_wout"), start=True, stop=True)
                pe.matmul(ps[0:TAIL, 512:576], y[:, P:TOPK], W("a_wout"), start=True, stop=True).then_inc(*pair.fill(st, n, "xo"))
                yield
                pe.wait_ge(*pe_req.at(st, n, "xo"))
                pe.wait_ge(*pair.read(st, n, "pt"))
                ps = pair.take(pe, st, n, "back")
                for t in range(NT):
                    pe.matmul(ps[:, t * 64:(t + 1) * 64], L.hid[:, 4, t * P:(t + 1) * P], L.att[:, 1, 0:64], start=True, stop=False)
                    mm = pe.matmul(ps[:, t * 64:(t + 1) * 64], L.hid[0:TAIL, 5, t * P:(t + 1) * P], L.att[0:TAIL, 1, 64:128],
                                   start=False, stop=True)
                mm.then_inc(*pair.fill(st, n, "back"))

            def gates(st, L, w, E):
                ps = pair.take(pe, st, L.n, "gate")
                for t in range(NT):
                    mm = mm3t(pe, ps[:, t * E:(t + 1) * E], L.xt[0], t, SW(w))
                mm.then_inc(*pair.fill(st, L.n, "gate"))

            def experts_out(st, L, r, parts_of, E, bias=None):
                for tp in range(2):
                    ps = pair.take(pe, st, L.n, "out", r, tp)
                    for a in range(2):
                        t = 2 * tp + a
                        o = ps[:, a * 512:a * 512 + E * 64]
                        if bias is not None:
                            at, _ = BIAS_AT[bias]
                            pe.matmul(o, onesb[:, :], bias3[:, at + r * 512:at + r * 512 + E * 64], start=True, stop=False,
                                      skip_group_check=True)
                        for e in range(E):
                            ops = parts_of(e)
                            for k, (hid, w2, rows) in enumerate(ops):
                                mm = pe.matmul(o[:, e * 64:(e + 1) * 64], hid[0:rows, t * P:(t + 1) * P], w2,
                                               start=bias is None and e == 0 and k == 0, stop=True, skip_group_check=True)
                    mm.then_inc(*pair.fill(st, L.n, "out", r, tp))

            def ffn0(L):
                st, n = "ffn0", L.n
                turn_features(st, L, 0)
                yield
                wait_xt(st, n, 0)
                gates(st, L, "f0_g", 4)
                yield
                ps = pair.take(pe, st, n, "s1")
                mm3(pe, ps[0:64, 0:512], SW("f0_s1"), L.xt[0]).then_inc(*pair.fill(st, n, "s1"))
                for a in range(2):
                    project(st, L, ("e1", a), 0, [("f0_e1", 256 * a + 128 * j, 256 * a + 128 * j + 128) for j in range(2)])
                yield
                pe.wait_ge(*pair.read(st, n, "s1"))
                ps = pair.take(pe, st, n, "s2")
                pe.matmul(ps[:, 0:512], W("f0_s2", 64), L.hid[0:64, 5, :], start=True, stop=True).then_inc(*pair.fill(st, n, "s2"))
                for a in range(2):
                    pe.wait_ge(*pair.read(st, n, ("e1", a)))
                    ps = pair.take(pe, st, n, "e2", a)
                    for j in range(2):
                        e = 2 * a + j
                        mm = pe.matmul(ps[0:64, j * 512:(j + 1) * 512], W("f0_e2", P, e * 64, e * 64 + 64), L.hid[:, e, :],
                                       start=True, stop=True)
                    mm.then_inc(*pair.fill(st, n, "e2", a))
                yield
                pe.wait_ge(*pair.read(st, n, "s2"))
                pe.wait_ge(*pair.read(st, n, "e2", 0))
                pe.wait_ge(*pair.read(st, n, "e2", 1))

                def ops(e):
                    if e == 4:
                        return [(L.hid[:, 4, :], W("f0_w3", P, 256, 320), P)]
                    return [(L.att[:, e, :], W("f0_w3", 64, e * 64, e * 64 + 64), 64)]
                experts_out(st, L, 0, ops, 5, "f0_b3")

            def ffn_relu(st, L, g, E, w1, w2, bias, rounds):
                n = L.n
                turn_features(st, L, 0)
                yield
                wait_xt(st, n, 0)
                gates(st, L, g, E)
                yield
                for r in range(rounds):
                    for a in range(4):
                        e = 8 * r + 2 * a
                        project(st, L, ("h", r, a), 0, [(w1, (e + j) * 128, (e + j + 1) * 128) for j in range(2)])
                    yield
                    for a in range(4):
                        pe.wait_ge(*pair.read(st, n, ("h", r, a)))
                    experts_out(st, L, r, lambda e: [(L.hid[:, e, :], W(w2, P, (8 * r + e) * 64, (8 * r + e) * 64 + 64), P)], 8, bias)
                    yield

            def plain(st, L, w, k_rows):
                n = L.n
                turn_features(st, L, 0)
                yield
                wait_xt(st, n, 0)
                ps = pair.take(pe, st, n, "qk")
                mm3(pe, ps[0:64, 0:512], SW(w + "_q"), L.xt[0])
                mm3(pe, ps[0:64, 512:1024], SW(w + "_k"), L.xt[0]).then_inc(*pair.fill(st, n, "qk"))
                values(st, L, 0, w + "_v", 64)

            def l2_attn(L):
                st, n = "l2", L.n
                yield from plain(st, L, "l2", 64)
                yield
                pe.wait_ge(*pair.read(st, n, "qk"))
                for a in range(2):
                    ps = pair.take(pe, st, n, "s", a)
                    for j in range(2):
                        jt = 2 * a + j
                        mm = pe.matmul(ps[:, j * 512:(j + 1) * 512], L.att[0:64, 1, jt * P:(jt + 1) * P], L.att[0:64, 0, :],
                                       start=True, stop=True)
                    mm.then_inc(*pair.fill(st, n, "s", a))
                yield
                pe.wait_ge(*v_ready.at(st, n, "scaled"))
                ps = pair.take(pe, st, n, "wo")
                for t in range(NT):
                    for jt in range(NT):
                        mm = pe.matmul(ps[:, t * 64:(t + 1) * 64], L.hid[:, jt, t * P:(t + 1) * P], L.v64[:, jt, 0:64],
                                       start=jt == 0, stop=jt == NT - 1)
                mm.then_inc(*pair.fill(st, n, "wo"))

            def l3_attn(L):
                st, n = "l3", L.n
                yield from plain(st, L, "l3", 65)
                yield
                pe.wait_ge(*pair.read(st, n, "qk"))
                for a in range(2):
                    ps = pair.take(pe, st, n, "m", a)
                    for j in range(2):
                        it = 2 * a + j
                        mm = pe.matmul(ps[:, j * 512:(j + 1) * 512], L.att[0:64, 0, it * P:(it + 1) * P], L.att[0:64, 1, :],
                                       start=True, stop=True)
                    mm.then_inc(*pair.fill(st, n, "m", a))
                yield
                pe.wait_ge(*maxima_ready.at(st, n))
                ps = pair.take(pe, st, n, "turnm")
                for t in range(NT):
                    mm = pe.transpose(ps[0:65, t * P:(t + 1) * P], L.m3[:, t, 0:65],
                                      W("ident"))
                mm.then_inc(*pair.fill(st, n, "turnm"))
                yield
                pe.wait_ge(*pair.read(st, n, "turnm"))
                for a in range(2):
                    ps = pair.take(pe, st, n, "s", a)
                    for j in range(2):
                        jt = 2 * a + j
                        mm = pe.matmul(ps[:, j * 512:(j + 1) * 512], L.att[0:65, 1, jt * P:(jt + 1) * P], L.att[0:65, 0, :],
                                       start=True, stop=True)
                    mm.then_inc(*pair.fill(st, n, "s", a))
                yield
                pe.wait_ge(*pair.read(st, n, "s", 1))
                pe.wait_ge(*v_ready.at(st, n, 0))
                ps = pair.take(pe, st, n, "wo")
                for t in range(NT):
                    for jt in range(NT):
                        mm = pe.matmul(ps[:, t * 65:t * 65 + 65], L.hid[:, jt, t * P:(t + 1) * P], L.v64[:, jt, :],
                                       start=jt == 0, stop=jt == NT - 1)
                mm.then_inc(*pair.fill(st, n, "wo"))

            def turn_all(st, L):
                for src in range(3 if st == "tok" else 1):
                    turn_features(st, L, src)
                yield

            def ffn2(L):
                st, n = "ffn2", L.n
                turn_features(st, L, 0)
                yield
                wait_xt(st, n, 0)
                gates(st, L, "f2_g", 8)
                yield
                for r in range(2):
                    for c in range(8):
                        a = (8 * r + c) * ROWS2
                        ps = pair.take(pe, st, n, "h", r, c)
                        mm3(pe, ps[0:ROWS2, 0:512], SW("f2_w1", a, a + ROWS2), L.xt[0])
                        mm3(pe, ps[0:ROWS2, 512:1024], SW("f2_w3", a, a + ROWS2), L.xt[0]).then_inc(*pair.fill(st, n, "h", r, c))
                    yield
                    pe.wait_ge(*hid_v.at(st, n, r, 7))
                    experts_out(st, L, r, lambda e: [
                        (L.hid[:, 2 * e + c, :], W("f2_w2", ROWS2, (8 * r + 2 * e + c) * 64, (8 * r + 2 * e + c) * 64 + 64), ROWS2)
                        for c in range(2)], 4)
                    yield

            def ffn1(L):
                return ffn_relu("ffn1", L, "f1_g", 8, "f1_w1", "f1_w2", "f1_b2", 1)

            def ffn3(L):
                return ffn_relu("ffn3", L, "f3_g", 16, "f3_w1", "f3_w2", "f3_b2", 2)

            with pe.Fori(0, CLIPS // LANES) as turn:
                for st in STAGES:
                    if st not in ATT:
                        in_turn([dict(sparse=sparse, ffn0=ffn0, l2=l2_attn, ffn2=ffn2, l3=l3_attn, ffn1=ffn1, ffn3=ffn3)[st](L)
                                 for L in lanes])
                    else:
                        in_turn([turn_all(st, L) for L in lanes])
                        attention(st)
                        in_turn([out_heads(st, L, {"tok": "t_wo", "l1": "l1_wo", "causal": "c_wo"}[st]) for L in lanes])
                next_turn(pe, "pe")


        @block.scalar
        def _(act):
            def copy(o, i, scale=1.0):
                return act.activation(o, i, ACT.Copy, scale=scale)

            act.wait_ge(loaded, 64)
            act.activation(sig_c[:, :], W("a_Cp"), ACT.Sigmoid).then_inc(*set_a.inc("c"))
            act.activation(sig_b[:, :], W("a_BpT", NST), ACT.Sigmoid).then_inc(*set_a.inc("b"))
            act.wait_ge(*set_v.at("all"))
            units = [0]
            split_units = []

            def features(st, L, srcs=1):
                act.wait_ge(*part1_ready.at(st, L.n))
                T = srcs * NT
                act.activation(L.parts[:, 0:T, 1:5:3, :], L.parts[:, 0:T, 0:1, :].broadcast_to([P, T, 2, 64]), ACT.Copy)\
                    .then_inc(*part1_copied.inc(st, L.n))
                yield
                for src in range(srcs):
                    act.wait_ge(*pair.filled(st, L.n, "turn", src))
                    ps = pair.view(st, L.n, "turn", src)[:].bitcast(BF16)
                    copy(L.xt[src][:, 0:2, :].rearrange("p a b -> p (a b)"), ps[:, 0:1024]).then_inc(*pair.free(st, L.n, "turn", src))

            def heads_f(st, L, what, bias, scale):
                u = units[0]
                units[0] += 1
                act.wait_ge(*pair.filled(st, L.n, what))
                if u >= 2:
                    act.wait_ge(*split_done(*split_units[u - 2]))
                split_units.append((st, L.n, what))
                ps = pair.view(st, L.n, what)
                for j in range(2):
                    f = f_t[:, u % 2, j * 512:(j + 1) * 512]
                    if bias is None:
                        i = act.activation(f, ps[:, j * 512:(j + 1) * 512], ACT.Copy if isinstance(scale, float) else ACT.Identity, scale=scale)
                    else:
                        i = act.activation(f, ps[:, j * 512:(j + 1) * 512], ACT.Identity, bias=bias[j], scale=scale)
                finish(act, i, pair, st, L.n, what)
                first_parts(u, W(("q" if what[0] == "q" else "k") + "a1"))

            def first_parts(u, a1):
                act.activation(pm_t[:, u % 2, :], f_t[:, u % 2, :], ACT.Copy, scale=a1).then_inc(*p1_ready.inc(u))

            def attention(st):
                cfg = ATT[st]

                def exponentials(i, jt):
                    act.wait_ge(*pair.filled(st, i, "e", jt))
                    u = 4 * i + jt
                    if u >= 3:
                        act.wait_ge(*prob_used.at(st, (u - 3) // 4, (u - 3) % 4))
                    c0 = jt * P if st == "causal" else 0
                    ps = pair.view(st, i, "e", jt)[:].rearrange("p (j c) -> p j c", j=2)[:, :, c0:512]
                    pb = prob[u % 3].rearrange("p (j c) -> p j c", j=2)[:, :, c0:512]
                    act.activation(pb, ps, ACT.Exp, scale=0.25 if st == "causal" else 1.0).then_inc(*pair.free(st, i, "e", jt))

                def outputs(i):
                    act.wait_ge(*prob_used.at(st, i, 3))
                    if i >= 5:
                        act.wait_ge(*turned_bank.filled(st, i - 4, "s"))
                    copy(o_t[:, (i // 2) % 2, :], heads_t[:, :]).then_inc(*heads_bank.free(st, i))

                for what in early_pieces(st):
                    piece(st, lanes[0], what)
                run_schedule(st, len(cfg["units"]), dict(h=lambda L, what: piece(st, L, what), e=exponentials, o=outputs))
                for L in lanes:
                    act.wait_ge(*pair.filled(st, L.n, "at"))
                    copy(L.att[0:64, 0, :], pair.view(st, L.n, "at")[0:64, 0:512]).then_inc(*pair.free(st, L.n, "at"))

            def piece(st, L, what):
                if what[0] == "v":
                    return
                if st == "causal":
                    act.wait_ge(*f_ready.at(st, L.n, what))
                    first_parts(units[0], W({"q": "c", "k": "d"}[what[0]] + "a1"))
                    split_units.append((st, L.n, what))
                    units[0] += 1
                    return
                a = what[2]
                if what[0] == "k":
                    bias = W("t_bk" if st == "tok" else "l1_bk")
                    heads_f(st, L, what, [bias[:, 2 * a + j:2 * a + j + 1] for j in range(2)], 1.0)
                elif st == "tok":
                    heads_f(st, L, what, [t_bqs[:, 2 * a + j:2 * a + j + 1] for j in range(2)], 0.125)
                else:
                    heads_f(st, L, what, None, l1_qscale[:, 0:1])

            def sparse(L):
                st, n = "sparse", L.n
                act.wait_ge(*act_req.at(st, n, "tanh"))
                act.activation(L.normed[:, 0:NT, :], L.base[:, :, :], ACT.Tanh, scale=W("a_alpha")).then_inc(*act_rsp.inc(st, n, "tanh"))
                yield
                yield from features(st, L)
                yield
                act.wait_ge(*act_req.at(st, n, "soft"))
                for t in range(NT):
                    i = act.activation(L.hid[:, t, :], L.att[:, 2, :], ACT.Exp, bias=L.small[:, 3, t, 0:1], scale=L.small[:, 0, t, 0:1],
                                       accum_out=L.small[:, 4, t, 0:1])
                i.then_inc(*act_rsp.inc(st, n, "soft"))
                yield
                act.wait_ge(*pair.filled(st, n, "pt"))
                ps = pair.view(st, n, "pt")
                copy(L.hid[:, 4, :], ps[:, 0:512])
                copy(L.hid[0:TAIL, 5, :], ps[0:TAIL, 512:1024]).then_inc(*pair.free(st, n, "pt"))

            def small_exp(st, L, tag, o, i):
                act.wait_ge(*act_req.at(st, L.n, tag))
                act.activation(o, i, ACT.Exp).then_inc(*act_rsp.inc(st, L.n, tag))

            def top2_exp(st, L):
                small_exp(st, L, "top", L.small[:, 6, :, 1:2], L.small[:, 6, :, 0:1])

            def ffn0(L):
                st, n = "ffn0", L.n
                yield from features(st, L)
                yield
                small_exp(st, L, "probs", L.small[:, 3, :, 0:4], L.small[:, 2, :, 0:4])
                yield
                top2_exp(st, L)
                yield
                act.wait_ge(*pair.filled(st, n, "s1"))
                act.activation(L.hid[0:64, 5, :], pair.view(st, n, "s1")[0:64, 0:512], ACT.Relu, bias=W("f0_bs1", 64))\
                    .then_inc(*pair.free(st, n, "s1"))
                for a in range(2):
                    act.wait_ge(*pair.filled(st, n, ("e1", a)))
                    ps = pair.view(st, n, ("e1", a))
                    for j in range(2):
                        i = act.activation(L.hid[:, 2 * a + j, :], ps[:, j * 512:(j + 1) * 512], ACT.Relu,
                                           bias=W("f0_be1", P, 2 * a + j, 2 * a + j + 1))
                    i.then_inc(*pair.free(st, n, ("e1", a)))

            def ffn_h(st, L, rounds, b1, func):
                n = L.n
                yield from features(st, L)
                yield
                top2_exp(st, L)
                for r in range(rounds):
                    yield
                    if r:
                        act.wait_ge(*pair.filled(st, n, "out", r - 1, 1))
                    for a in range(4):
                        act.wait_ge(*pair.filled(st, n, ("h", r, a)))
                        ps = pair.view(st, n, ("h", r, a))
                        for j in range(2 if st == "ffn1" else 1):
                            e = 2 * a + j
                            last = j == 1 or st == "ffn3"
                            ins = act.activation(L.hid[:, e, :], ps[:, j * 512:(j + 1) * 512], func,
                                                 bias=W(b1, P, 8 * r + e, 8 * r + e + 1))
                            if last:
                                ins.then_inc(*pair.free(st, n, ("h", r, a)))

            def plain(st, L, bq, bk, qscale):
                n = L.n
                yield from features(st, L)
                yield
                act.wait_ge(*pair.filled(st, n, "qk"))
                ps = pair.view(st, n, "qk")
                if bq is None:
                    copy(L.att[0:64, 0, :], ps[0:64, 0:512], scale=0.125)
                    copy(L.att[0:64, 1, :], ps[0:64, 512:1024]).then_inc(*pair.free(st, n, "qk"))
                else:
                    act.activation(L.att[0:64, 0, :], ps[0:64, 0:512], ACT.Identity, bias=bq, scale=qscale)
                    act.activation(L.att[0:64, 1, :], ps[0:64, 512:1024], ACT.Identity, bias=bk)\
                        .then_inc(*pair.free(st, n, "qk"))

            def l2(L):
                st, n = "l2", L.n
                yield from plain(st, L, None, None, None)
                yield
                for a in range(2):
                    act.wait_ge(*maxima_ready.at(st, n, a))
                    ps = pair.view(st, n, "s", a)
                    for j in range(2):
                        jt = 2 * a + j
                        i = act.activation(L.hid[:, jt, :], ps[:, j * 512:(j + 1) * 512], ACT.Exp, bias=L.small[:, 10, jt, 0:1],
                                           accum_out=L.small[:, 11, jt, 0:1])
                    i.then_inc(*pair.free(st, n, "s", a))

            def l3(L):
                st, n = "l3", L.n
                yield from plain(st, L, l3_bqs[0:64, 0:1], W("l3_bk", 64), l3_qscale[0:64, 0:1])
                yield
                act.wait_ge(*pair.filled(st, n, "turnm"))
                copy(L.att[64:65, 0, :], pair.view(st, n, "turnm")[64:65, 0:512]).then_inc(*pair.free(st, n, "turnm"))
                yield
                for a in range(2):
                    act.wait_ge(*pair.filled(st, n, "s", a))
                    ps = pair.view(st, n, "s", a)
                    act.activation(L.hid[:, 2 * a:2 * a + 2, :].rearrange("p a b -> p (a b)"), ps[:, :], ACT.Exp)\
                        .then_inc(*pair.free(st, n, "s", a))

            def ffn2(L):
                st, n = "ffn2", L.n
                yield from features(st, L)
                yield
                small_exp(st, L, "probs", L.small[:, 3, :, 0:8], L.small[:, 2, :, 0:8])
                for r in range(2):
                    yield
                    for c in range(8):
                        k = 8 * r + c
                        act.wait_ge(*pair.filled(st, n, "h", r, c))
                        if k >= 2:
                            act.wait_ge(*hid_v.at(st, n, (k - 2) // 8, (k - 2) % 8))
                        act.activation(L.att[0:ROWS2, k % 2, :], pair.view(st, n, "h", r, c)[0:ROWS2, 0:512], ACT.Silu)\
                            .then_inc(*hid_a.inc(st, n, r, c))

            def ffn1(L):
                return ffn_h("ffn1", L, 1, "f1_b1", ACT.Gelu)

            def ffn3(L):
                return ffn_h("ffn3", L, 2, "f3_b1", ACT.Relu)

            with act.Fori(0, CLIPS // LANES) as turn:
                for st in STAGES:
                    if st not in ATT:
                        in_turn([dict(sparse=sparse, ffn0=ffn0, ffn1=ffn1, l2=l2, ffn2=ffn2, l3=l3, ffn3=ffn3)[st](L)
                                 for L in lanes])
                    else:
                        in_turn([features(st, L, 3 if st == "tok" else 1) for L in lanes])
                        attention(st)
                next_turn(act, "act")

        @block.gpsimd
        def _(pool):
            units = [0]

            def rstd(st, L, tag, T):
                pool.wait_ge(*var_ready.at(st, L.n, tag))
                pool.tensor_tensor(L.stat[:, 3, 0:T], L.stat[:, 2, 0:T], minus_half[:, 0:T], ALU.pow)\
                    .then_inc(*rstd_ready.inc(st, L.n, tag))

            def split_heads(st, L, what, dst):
                u = units[0]
                units[0] += 1
                b = u % 2
                pool.wait_ge(*p1_ready.at(u))
                pool.tensor_tensor(f_t[:, b, :], f_t[:, b, :], pm_t[:, b, :], ALU.subtract).then_inc(*y1_ready.inc(u))
                if by_vector(st, L.n, what):
                    return
                pool.wait_ge(*p2_ready.at(u))
                if isinstance(dst, int):
                    for j in range(2):
                        r = slice(64 * j, 64 * j + 64)
                        o = L.qs[r, 4 * dst + j:4 * dst + j + 3:2, :]
                        i, m = [t[r, b, :].rearrange("p (a c) -> p a c", a=2) for t in (f_t, pm_t)]
                        ins = pool.tensor_tensor(o, i, m, ALU.subtract)
                        if j == 0:
                            finish(pool, ins, p_step)
                        else:
                            finish(pool, ins, heads_ready, st, L.n, what)
                    return
                pool.tensor_tensor(dst, f_t[:, b, :], pm_t[:, b, :], ALU.subtract).then_inc(*heads_ready.inc(st, L.n, what))

            def two(t, a):
                return t[:, a:a + 2, :].rearrange("p a b -> p (a b)")

            def stage(st, L):
                for tag in {"sparse": ["ln", "norm"], "causal": ["ln", "rms"], "ffn2": ["rms"], "ffn1": ["ln", "ln2"],
                            "ffn3": ["ln", "ln2"]}.get(st, ["ln"]):
                    rstd(st, L, tag, 12 if st == "tok" else NT)
                    yield

            def piece(st, L, what):
                if what[0] == "v":
                    return
                if st == "causal":
                    split_heads(st, L, what, two(L.ks, (4 if what[0] == "q" else 0) + 2 * what[1]))
                elif what[0] == "q":
                    split_heads(st, L, what, what[2])
                else:
                    split_heads(st, L, what, two(L.ks, 4 * what[1] + 2 * what[2]))

            with pool.Fori(0, CLIPS // LANES) as turn:
                for st in STAGES:
                    in_turn([stage(st, L) for L in lanes])
                    if st in ATT:
                        for what in early_pieces(st):
                            piece(st, lanes[0], what)
                        for _, L, what in late_pieces(st):
                            piece(st, L, what)
                next_turn(pool, "pool")

        @block.sync
        def _(sp):
            sp.dma_start(whole[:, :], wwhole[:, 0:KEPT]).then_inc(loaded, 16)
            sp.dma_start(lanes[0].arena[:, 0:WHOLE_N - KEPT], wwhole[:, KEPT:WHOLE_N]).then_inc(loaded, 16)
            sp.dma_start(f_t[0:3, 0, 0:1024], wbias[:, 0:1024]).then_inc(loaded, 16)
            sp.dma_start(f_t[0:3, 1, 0:BIAS_N - 1024], wbias[:, 1024:BIAS_N]).then_inc(loaded, 16)
            for c in range(-(-SPLIT_N // CHUNK)):
                a, b = c * CHUNK, min((c + 1) * CHUNK, SPLIT_N)
                sp.wait_ge(*set_v.at("free", c))
                sp.dma_start(f_t[:, c % 2, 0:b - a], wsplit[:, a:b]).then_inc(staged[c % 2], 16)
            sp.wait_ge(*set_v.at("kernels"))
            sp.dma_start(skew.rearrange("n (s t) -> n s t", t=SKEW), kern[:, :].unsqueeze(1).broadcast_to([NST, P, SKEW]))\
                .then_inc(skew_done, 16)
            sp.wait_ge(skew_done, 16)
            sp.dma_start(scan_t[:, :, :], skew[:, 0:P * (SKEW - 1)].rearrange("n (s t) -> s n t", t=SKEW - 1)[:, :, 0:TOPK])\
                .then_inc(scan_loaded, 16)
            clip_in = x.rearrange("b (t p) d -> b p t d", p=P)
            clip_out = out.rearrange("b (t p) d -> b p t d", p=P)
            with sp.Fori(0, CLIPS // LANES) as turn:
                for L in lanes:
                    sp.dma_start(L.x, clip_in[turn * LANES + L.n]).then_inc(clip_loaded[L.n], 16)
                for L in lanes:
                    sp.wait_ge(*out_ready.at(L.n))
                    sp.dma_start(clip_out[turn * LANES + L.n], L.h[:, :, :]).then_inc(stored, 16)
                sp.wait_ge(stored, 16 * LANES)
                sp.wait_ge(turn_done, 4)
                for s in turn_sems + [stored, turn_done]:
                    sp.sem_clear(s)
                for e in go.values():
                    sp.sem_inc(e, 1)

        @block.vector
        def _(dve):
            def step(i):
                finish(dve, i, v_step)

            def stride(i):
                i.then_inc(*v_step.inc())
                count = v_step.count
                yield
                dve.wait_ge(v_step.sem, count)

            def bcast(a, shape, axis=2):
                return a.unsqueeze(axis).broadcast_to(shape)

            def start(i, *event):
                finish(dve, i, set_v, *(event or ("step", set_v.count)))

            dve.wait_ge(loaded, 64)
            start(dve.memset(kern[:, :], 0.0))
            start(dve.tensor_copy(power[:, :], W("a_A", NST)))
            start(dve.tensor_copy(power_t[:, :], W("a_AT", NST)))
            dve.wait_ge(*set_a.at("b"))
            start(dve.tensor_copy(kern[:, 0:1], sig_b[:, :]), "power", 0)
            for k in range(8):
                T = 1 << k
                n = min(T, TOPK - T)
                dve.wait_ge(*set_t.at("power", k))
                start(dve.tensor_copy(kern[:, T:T + n], pair_t[0][0:NST, 0:n]))
                start(dve.tensor_copy(power[:, :], pair_t[1][0:NST, 0:NST]))
                start(dve.tensor_copy(power_t[:, :], pair_t[2][0:NST, 0:NST]), *(("power", k + 1) if k < 7 else ("kernels",)))
            for a, b, s in ((0, 1024, 0), (1024, BIAS_N, 1)):
                f, pm, y = f_t[0:3, s, 0:b - a], pm_t[0:3, s, 0:b - a], y_t[0:3, s, 0:b - a]
                start(dve.tensor_scalar(pm, f, W("ra1", 3), None, ALU.mult))
                start(dve.tensor_tensor(y, f, pm, ALU.subtract))
                start(dve.tensor_scalar(pm, y, W("ra2", 3), None, ALU.mult))
                start(dve.tensor_tensor(bias3[:, a:b], y, pm, ALU.subtract), "free", s)
            for c in range(-(-SPLIT_N // CHUNK)):
                a, b = c * CHUNK, min((c + 1) * CHUNK, SPLIT_N)
                s, n = c % 2, b - a
                dve.wait_ge(staged[s], 16 * (c // 2 + 1))
                f, p1, p2, y = f_t[:, s, 0:n], pm_t[:, 0, 0:n], pm_t[:, 1, 0:n], y_t[:, 0, 0:n]
                start(dve.tensor_copy(p1, f))
                start(dve.tensor_tensor(y, f, p1, ALU.subtract), *(("free", c + 2) if c + 2 < -(-SPLIT_N // CHUNK) else ()))
                start(dve.tensor_copy(p2, y))
                start(dve.tensor_tensor(w_ca[0:64, a:b], y[0:64], p2[0:64], ALU.subtract))
                start(dve.tensor_copy(w_ca[64:P, a:b], p1[64:P]))
                start(dve.tensor_copy(w_ab[0:64, a:b], p1[0:64]))
                start(dve.tensor_copy(w_ab[64:P, a:b], p2[64:P]))
            for i in (
                dve.tensor_copy(identb[:, :], W("ident")),
                dve.tensor_copy(monesb[:, :], W("mones8")),
                dve.memset(onesb[:, :], 1.0),
                dve.memset(mc_t[:, :, :, :, :], 0.0),
                dve.memset(qm_t[:, :, :, :], 0.0),
                dve.tensor_copy(causal_b[:, 0, :], W("negmask")),
                dve.tensor_copy(causal_b[:, 1, :], W("negmaskT")),
                dve.tensor_scalar(t_bqs[:, :], W("t_bq"), 0.125, None, ALU.mult),
                dve.tensor_scalar(t_bo2[:, :], W("t_bo"), 2.0, None, ALU.mult),
                dve.reciprocal(l3_qscale[:, :], W("l3_scale")),
                dve.reciprocal(l1_qscale[:, :], W("l1_temp")),
            ):
                i.then_inc(*set_v.inc("const", set_v.count))
            for L in lanes:
                dve.memset(L.v64[:, :, 64:65], 1.0).then_inc(*set_v.inc("const", set_v.count))
            dve.wait_ge(set_v.sem, set_v.count)
            start(dve.tensor_scalar(y_t[:, 0, 0:P], W("ident"), l1_qscale[:, 0:1], DIAG, ALU.mult, ALU.mult))
            start(dve.tensor_copy(diag3[:, 0, :], y_t[:, 0, 0:P]))
            start(dve.tensor_tensor(y_t[:, 1, 0:P], y_t[:, 0, 0:P], diag3[:, 0, :], ALU.subtract))
            start(dve.tensor_copy(diag3[:, 1, :], y_t[:, 1, 0:P]))
            start(dve.tensor_tensor(diag3[:, 2, :], y_t[:, 1, 0:P], diag3[:, 1, :], ALU.subtract))
            start(dve.tensor_scalar(l1_qscale[:, :], l1_qscale[:, :], 0.125, None, ALU.mult))
            start(dve.tensor_tensor(l3_bqs[:, :], W("l3_bq"), l3_qscale[:, :], ALU.mult))
            start(dve.memset(minus_half[:, :], -0.5), "all")

            def layernorm(st, L, tag, src, T, dst, gamma=None, beta=None, eps=EPS, centre=True):
                if centre:
                    step(dve.tensor_reduce(L.stat[:, 0, 0:T], src, AX.X, ALU.add))
                    step(dve.tensor_scalar(L.stat[:, 1, 0:T], L.stat[:, 0, 0:T], 1.0 / DIM, None, ALU.mult))
                    step(dve.tensor_tensor(L.cent[:, 0:T, :], src, bcast(L.stat[:, 1, 0:T], [P, T, 64]), ALU.subtract))
                    src = L.cent[:, 0:T, :]
                step(dve.tensor_tensor(L.sq[:, 0:T, :], src, src, ALU.mult))
                step(dve.tensor_reduce(L.stat[:, 0, 0:T], L.sq[:, 0:T, :], AX.X, ALU.add))
                dve.tensor_scalar(L.stat[:, 2, 0:T], L.stat[:, 0, 0:T], 1.0 / DIM, eps, ALU.mult, ALU.add)\
                    .then_inc(*var_ready.inc(st, L.n, tag))
                yield
                dve.wait_ge(*rstd_ready.at(st, L.n, tag))
                step(dve.tensor_tensor(dst, src, bcast(L.stat[:, 3, 0:T], [P, T, 64]), ALU.mult))
                if gamma is not None:
                    step(dve.tensor_tensor(dst, dst, bcast(gamma, [P, T, 64], 1), ALU.mult))
                if beta is not None:
                    step(dve.tensor_tensor(dst, dst, bcast(beta, [P, T, 64], 1), ALU.add))

            def split_tokens(st, L, T=NT):
                x32 = L.normed12 if T == 12 else L.normed[:, :, :]
                finish(dve, dve.tensor_copy(L.parts[:, 0:T, 0, :], x32), part1_ready, st, L.n)
                step(dve.tensor_tensor(L.cent[:, 0:T, :], x32, L.parts[:, 0:T, 0, :], ALU.subtract))
                step(dve.tensor_copy(L.parts[:, 0:T, 2:4, :], bcast(L.cent[:, 0:T, :], [P, T, 2, 64])))
                dve.tensor_tensor(L.parts[:, 0:T, 5, :], L.cent[:, 0:T, :], L.parts[:, 0:T, 2, :], ALU.subtract)\
                    .then_inc(*parts_ready.inc(st, L.n))

            def turned(st, L, src=0):
                dve.wait_ge(*pair.filled(st, L.n, "turn", src))
                ps = pair.view(st, L.n, "turn", src)[:].bitcast(BF16)
                dve.tensor_copy(L.xt[src][:, 2, :], ps[:, 1024:1536]).then_inc(*pair.free(st, L.n, "turn", src))

            units = [0]
            split_units = []
            f_units = [0]

            def split2(a2, st, L, what):
                u = units[0]
                units[0] += 1
                split_units.append((st, L.n, what))
                dve.wait_ge(*y1_ready.at(u))
                f, m = f_t[:, u % 2, :], pm_t[:, u % 2, :]
                finish(dve, dve.tensor_scalar(m, f, a2, None, ALU.mult), p2_ready, u)
                if by_vector(st, L.n, what):
                    if what[0] == "q":
                        for j in range(2):
                            r = slice(64 * j, 64 * j + 64)
                            o = L.qs[r, 4 * what[2] + j:4 * what[2] + j + 3:2, :]
                            i2, m2 = [t[r].rearrange("p (a c) -> p a c", a=2) for t in (f, m)]
                            finish(dve, dve.tensor_tensor(o, i2, m2, ALU.subtract), *((v_step,) if j == 0 else (early_ready, st, L.n, what)))
                    else:
                        a = 4 * what[1] + 2 * what[2]
                        finish(dve, dve.tensor_tensor(L.ks[:, a:a + 2, :].rearrange("p a c -> p (a c)"), f, m, ALU.subtract),
                               early_ready, st, L.n, what)

            def values8(st, L, src, s, bias):
                dve.wait_ge(*pair.filled(st, L.n, "v", s))
                ps = pair.view(st, L.n, "v", s)
                for t in range(NT):
                    o, i = L.v[:, src, t, :, 0:8], ps[:, t * 64:(t + 1) * 64].rearrange("p (h d) -> p h d", h=8)
                    ins = dve.tensor_tensor(o, i, W(bias).rearrange("p (h d) -> p h d", h=8), ALU.add) if bias else dve.tensor_copy(o, i)
                finish(dve, ins, pair, st, L.n, "v", s)
                dve.nop().then_inc(*v_ready.inc(st, L.n, src))

            def attention(st):
                cfg = ATT[st]

                def maxima(i, it):
                    dve.wait_ge(*pair.filled(st, i, "m", it))
                    cols = (it + 1) * P if st == "causal" else 512
                    ps = pair.view(st, i, "m", it)[:].rearrange("p (j c) -> p j c", j=2)[:, :, 0:cols]
                    b = i % 2
                    finish(dve, dve.tensor_reduce(neg_t[:, b, 2 * it:2 * it + 2], ps, AX.X, ALU.max, negate=True), pair, st, i, "m", it)
                    if it < NT - 1:
                        return
                    neg = neg_t[:, b, 0:8].rearrange("p (t j) -> p t j", j=2)
                    left = m_left[:, b, :].rearrange("p (t j) -> p t j", j=2)
                    if st == "causal":
                        rows = [mc_t[:, b, :, :, 96 + k].rearrange("p j t -> p t j") for k in range(3)]
                    else:
                        rows = [m_t[:, b, 0, :, :].rearrange("p t (j c) -> p t j c", j=2)[:, :, :, 48 + k] for k in range(3)]
                    step(dve.tensor_copy(rows[0], neg))
                    step(dve.tensor_tensor(left, neg, rows[0], ALU.subtract))
                    step(dve.tensor_copy(rows[1], left))
                    dve.tensor_tensor(rows[2], left, rows[1], ALU.subtract).then_inc(*maxima_ready.inc(st, i))

                def shift(i):
                    n, src, g = cfg["units"][i]
                    L = lanes[n]
                    dve.wait_ge(*turned_bank.filled(st, i, "t"))
                    if i >= 2:
                        dve.wait_ge(*pair.filled(st, i - 2, "e", 3))
                    ps = turned_t[:].bitcast(BF16)
                    if st == "tok":
                        for j in range(2):
                            r = slice(64 * j, 64 * j + 64)
                            ins = dve.tensor_tensor(qm_t[r, i % 2, j, :], L.qs[r, 2 * g + j, :], ps[r, 0:512], ALU.add)
                            if j == 0:
                                step(ins)
                    elif st == "l1":
                        ins = dve.tensor_copy(L.qm1[:, i % 2, :], ps[:, 0:512])
                    else:
                        ins = dve.tensor_tensor(L.qmc[:, i % 2, :, :], L.ks[:, 4 + 2 * g:6 + 2 * g, :],
                                                ps[:, 0:1024].rearrange("p (j c) -> p j c", j=2), ALU.add)
                    finish(dve, ins, turned_bank, st, i, "t")
                    dve.nop().then_inc(*shift_ready.inc(st, i))

                def normalise(i):
                    n, src, g = cfg["units"][i]
                    L = lanes[n]
                    d = 16 if st == "causal" else 8
                    dve.wait_ge(*turned_bank.filled(st, i, "s"))
                    ps = turned_t[:].rearrange("p (t h c) -> p t h c", t=NT, h=4)
                    r = recip16[:, :, :].unsqueeze(3)
                    step(dve.reciprocal(r, ps[:, :, :, d:d + 1]))
                    og = g // 2
                    o = L.heads_out[:, :, 4 * d * og:4 * d * og + 4 * d].rearrange("p t (h c) -> p t h c", h=4)
                    if src == 0:
                        finish(dve, dve.tensor_tensor(o, ps[:, :, :, 0:d], r.broadcast_to([P, NT, 4, d]), ALU.mult), turned_bank, st, i, "s")
                    else:
                        x8 = red[:, :, :].rearrange("p a (t h c) -> p (a t) h c", h=4, t=2)
                        finish(dve, dve.tensor_tensor(x8, ps[:, :, :, 0:d], r.broadcast_to([P, NT, 4, d]), ALU.mult), turned_bank, st, i, "s")
                        step(dve.tensor_tensor(o, o, x8, ALU.add))
                    if i + 1 == len(cfg["units"]) or cfg["units"][i + 1][0] != n:
                        dve.nop().then_inc(*att_ready.inc(st, n))

                f_units[0] = units[0]
                last = None
                for what in early_pieces(st):
                    piece(st, lanes[0], what)
                    if what[0] != "v":
                        if last:
                            piece2(st, lanes[0], last)
                        last = what
                piece2(st, lanes[0], last)
                run_schedule(st, len(cfg["units"]), dict(h=lambda L, what: piece(st, L, what), h2=lambda L, what: piece2(st, L, what),
                                                         m=maxima, t=shift, s=normalise))

            def rows_add(st, L, first, bias=None):
                dve.wait_ge(*pair.filled(st, L.n, "wo"))
                ps = pair.view(st, L.n, "wo")[:, 0:NT * 64].rearrange("p (t d) -> p t d", t=NT)
                if bias is not None:
                    if not first:
                        step(dve.tensor_tensor(L.h[:, :, :], L.h[:, :, :], bcast(bias, [P, NT, 64], 1), ALU.add))
                        bias = None
                o = L.h[:, :, :]
                finish(dve, dve.tensor_tensor(o, ps, o if bias is None else bcast(bias, [P, NT, 64], 1), ALU.add), pair, st, L.n, "wo")

            def gating(st, L, E, bias=None, soft=False, renorm=False):
                n, S = L.n, L.small
                Ep = max(E, 8)
                dve.wait_ge(*pair.filled(st, n, "gate"))
                ps = pair.view(st, n, "gate")[:, 0:NT * E].rearrange("p (t e) -> p t e", t=NT)
                if E < 8:
                    yield from stride(dve.memset(S[:, 0, :, E:8], NEG))
                if bias is not None:
                    ins = dve.tensor_tensor(S[:, 0, :, 0:E], ps, bcast(bias, [P, NT, E], 1), ALU.add)
                else:
                    ins = dve.tensor_copy(S[:, 0, :, 0:E], ps)
                finish(dve, ins, pair, st, n, "gate")
                if soft:
                    yield from stride(dve.tensor_reduce(S[:, 1, :, 0:1], S[:, 0, :, 0:E], AX.X, ALU.max))
                    finish(dve, dve.tensor_tensor(S[:, 2, :, 0:E], S[:, 0, :, 0:E], S[:, 1, :, 0:1].broadcast_to([P, NT, E]), ALU.subtract),
                           act_req, st, n, "probs")
                    yield
                    dve.wait_ge(*act_rsp.at(st, n, "probs"))
                    yield from stride(dve.tensor_reduce(S[:, 1, :, 1:2], S[:, 3, :, 0:E], AX.X, ALU.add))
                    yield from stride(dve.reciprocal(S[:, 1, :, 2:3], S[:, 1, :, 1:2]))
                    yield from stride(dve.tensor_tensor(S[:, 0, :, 0:E], S[:, 3, :, 0:E], S[:, 1, :, 2:3].broadcast_to([P, NT, E]), ALU.mult))
                for t in range(NT):
                    ins = dve.max(out=S[:, 4, t, 0:8], in_=S[:, 0, t, 0:Ep])
                yield from stride(ins)
                for t in range(NT):
                    ins = dve.max_index(out=L.idx[:, t, :], in_max=S[:, 4, t, 0:8], in_values=S[:, 0, t, 0:Ep])
                yield from stride(ins)
                yield from stride(dve.tensor_copy(S[:, 5, :, 0:8], L.idx[:, :, :]))
                if renorm:
                    yield from stride(dve.tensor_tensor(S[:, 6, :, 0:1], S[:, 4, :, 0:1], S[:, 4, :, 1:2], ALU.add))
                    yield from stride(dve.tensor_scalar(S[:, 6, :, 0:1], S[:, 6, :, 0:1], 1e-9, None, ALU.add))
                    yield from stride(dve.reciprocal(S[:, 6, :, 1:2], S[:, 6, :, 0:1]))
                    yield from stride(dve.tensor_tensor(S[:, 7, :, 0:2], S[:, 4, :, 0:2], S[:, 6, :, 1:2].broadcast_to([P, NT, 2]), ALU.mult))
                else:
                    finish(dve, dve.tensor_tensor(S[:, 6, :, 0:1], S[:, 4, :, 1:2], S[:, 4, :, 0:1], ALU.subtract), act_req, st, n, "top")
                    yield
                    dve.wait_ge(*act_rsp.at(st, n, "top"))
                    yield from stride(dve.tensor_scalar(S[:, 6, :, 2:3], S[:, 6, :, 1:2], 1.0, None, ALU.add))
                    yield from stride(dve.reciprocal(S[:, 7, :, 0:1], S[:, 6, :, 2:3]))
                    yield from stride(dve.tensor_tensor(S[:, 7, :, 1:2], S[:, 7, :, 0:1], S[:, 6, :, 1:2], ALU.mult))
                number = bcast(W("iotae", P, 0, E), [P, NT, E], 1)
                for k in range(2):
                    yield from stride(dve.tensor_tensor(S[:, 8 + k, :, 0:E], number, S[:, 5, :, k:k + 1].broadcast_to([P, NT, E]), ALU.is_equal))
                    yield from stride(dve.tensor_tensor(S[:, 8 + k, :, 0:E], S[:, 8 + k, :, 0:E], S[:, 7, :, k:k + 1].broadcast_to([P, NT, E]), ALU.mult))
                yield from stride(dve.tensor_tensor(S[:, 8, :, 0:E], S[:, 8, :, 0:E], S[:, 9, :, 0:E], ALU.add))
                if st == "ffn0":
                    yield from stride(dve.memset(S[:, 8, :, 4:5], 1.0))

            def combine(st, L, r, E, acc):
                for tp in range(2):
                    dve.wait_ge(*pair.filled(st, L.n, "out", r, tp))
                    ps = pair.view(st, L.n, "out", r, tp)[:].rearrange("p (t c) -> p t c", t=2)[:, :, 0:E * 64]\
                        .rearrange("p t (e d) -> p t e d", e=E)
                    w = bcast(L.small[:, 8, 2 * tp:2 * tp + 2, r * E:(r + 1) * E], [P, 2, E, 64], 3)
                    o = prod[:, 0:2 * E * 64].rearrange("p (t e d) -> p t e d", t=2, e=E)
                    finish(dve, dve.tensor_tensor(o, ps, w, ALU.mult), pair, st, L.n, "out", r, tp)
                    step(dve.tensor_reduce(red[:, :, :], o.rearrange("p t e d -> p t d e"), AX.X, ALU.add))
                    step(dve.tensor_tensor(acc[:, 2 * tp:2 * tp + 2, :], acc[:, 2 * tp:2 * tp + 2, :], red[:, :, :], ALU.add))

            def zeros(L, sources):
                step(dve.memset(L.qs, 0.0))
                step(dve.memset(L.v[:, 0:sources], 0.0))
                step(dve.memset(L.v[:, 0:sources, :, :, 8:9], 1.0))

            def tok(L):
                n = L.n
                dve.wait_ge(clip_loaded[n], 16)
                yield from layernorm("tok", L, "ln", L.x, 12, L.normed12, W("t_g"), W("t_b"))
                split_tokens("tok", L, 12)
                yield
                for src in range(3):
                    turned("tok", L, src)
                yield
                zeros(L, 2)
                if L.n == 0:
                    step(dve.memset(mc_t[:, :, 0, :, 96:99], 0.0))

            def sparse(L):
                st, n, S = "sparse", L.n, L.small
                yield from layernorm(st, L, "ln", L.h[:, :, :], NT, L.base[:, :, :])
                finish(dve, dve.tensor_tensor(L.h[:, :, :], L.h[:, :, :], L.base[:, :, :], ALU.add), act_req, st, n, "tanh")
                yield
                dve.wait_ge(*act_rsp.at(st, n, "tanh"))
                xn = L.normed[:, 0:NT, :]
                yield from stride(dve.tensor_tensor(xn, xn, bcast(W("a_w"), [P, NT, 64], 1), ALU.mult))
                yield from stride(dve.tensor_tensor(xn, xn, bcast(W("a_b"), [P, NT, 64], 1), ALU.add))
                split_tokens(st, L)
                yield
                turned(st, L)
                yield
                dve.wait_ge(*pair.filled(st, n, "xp"))
                xp = L.hid[:, 6, :].rearrange("p (t e) -> p t e", t=NT)
                xq = L.hid[:, 7, :].rearrange("p (t e) -> p t e", t=NT)
                ps = pair.view(st, n, "xp")[:, 0:512].rearrange("p (t e) -> p t e", t=NT)
                finish(dve, dve.tensor_tensor(xp, ps, bcast(W("a_bin"), [P, NT, EXP], 1), ALU.add), pair, st, n, "xp")
                yield from stride(dve.tensor_tensor(xq, xp, xp, ALU.mult))
                yield from stride(dve.tensor_reduce(L.stat[:, 0, 0:NT], xq, AX.X, ALU.add))
                dve.tensor_scalar(L.stat[:, 2, 0:NT], L.stat[:, 0, 0:NT], 1e-24, None, ALU.max).then_inc(*var_ready.inc(st, n, "norm"))
                yield
                dve.wait_ge(*rstd_ready.at(st, n, "norm"))
                yield from stride(dve.tensor_tensor(xp, xp, bcast(L.stat[:, 3, 0:NT], [P, NT, EXP]), ALU.mult))
                for k, w in ((0, "a_wq"), (1, "a_wk")):
                    yield from stride(dve.tensor_tensor(xq, xp, bcast(W(w), [P, NT, EXP], 1), ALU.mult))
                    yield from stride(dve.tensor_reduce(S[:, k, :, 0:1], xq, AX.X, ALU.add))
                    yield from stride(dve.tensor_scalar(S[:, k, :, 0:1], S[:, k, :, 0:1], W("a_bq" if k == 0 else "a_bk"), None, ALU.add))
                diag = L.att[:, 0, :].rearrange("p (t e) -> p t e", t=NT)
                ident = bcast(W("ident"), [P, NT, P], 1)
                finish(dve, dve.tensor_tensor(diag, ident, S[:, 1, :, 0:1].broadcast_to([P, NT, P]), ALU.mult), pe_req, st, n, "kdiag")
                yield
                dve.wait_ge(*pair.filled(st, n, "kb"))
                finish(dve, dve.tensor_copy(L.att[:, 2, :], pair.view(st, n, "kb")[:, 0:512]), pair, st, n, "kb")
                yield from stride(dve.tensor_reduce(S[:, 2, 0, 0:1], L.att[:, 2, :], AX.X, ALU.max))
                yield from stride(dve.tensor_reduce(S[:, 2, 0, 1:2], L.att[:, 2, :], AX.X, ALU.min))
                yield from stride(dve.tensor_scalar(S[:, 3, :, 0:1], S[:, 0, :, 0:1], S[:, 2, 0, 0:1], None, ALU.mult))
                yield from stride(dve.tensor_scalar(S[:, 3, :, 1:2], S[:, 0, :, 0:1], S[:, 2, 0, 1:2], None, ALU.mult))
                yield from stride(dve.tensor_tensor(S[:, 3, :, 0:1], S[:, 3, :, 0:1], S[:, 3, :, 1:2], ALU.max))
                finish(dve, dve.tensor_scalar(S[:, 3, :, 0:1], S[:, 3, :, 0:1], -1.0, None, ALU.mult), act_req, st, n, "soft")
                yield
                dve.wait_ge(*act_rsp.at(st, n, "soft"))
                yield from stride(dve.reciprocal(S[:, 4, :, 1:2], S[:, 4, :, 0:1]))
                recip = L.att[:, 1, :].rearrange("p (t e) -> p t e", t=NT)
                finish(dve, dve.tensor_copy(recip, S[:, 4, :, 1:2].broadcast_to([P, NT, P])), pe_req, st, n, "recip")
                yield
                dve.wait_ge(*pair.filled(st, n, "imp"))
                imp = L.att[:, 3, :]
                finish(dve, dve.tensor_scalar(imp, pair.view(st, n, "imp")[:, 0:512], 1.0 / TOK, None, ALU.mult), pair, st, n, "imp")
                step(dve.tensor_tensor(diag, imp.rearrange("p (t e) -> p t e", t=NT), ident, ALU.mult))
                step(dve.tensor_reduce(S[:, 5, :, 0:1], diag, AX.X, ALU.add))
                for t in range(NT):
                    step(dve.tensor_scalar(prod[:, 0:512], imp, S[:, 5, t, 0:1], 0.0, ALU.is_gt, ALU.add, accum_out=S[:, 6, t, 0:1]))
                    c = (t + 1) * P
                    if t:
                        step(dve.tensor_scalar(prod[:, 0:t * P], imp[:, 0:t * P], S[:, 5, t, 0:1], 0.0, ALU.is_equal, ALU.add,
                                               accum_out=S[:, 6, t, 1:2]))
                    else:
                        step(dve.memset(S[:, 6, 0, 1:2], 0.0))
                    step(dve.scalar_tensor_tensor(out=prod[:, 0:P], in0=imp[:, t * P:c], scalar=S[:, 5, t, 0:1], in1=W("ltmask", P, 0, P),
                                                  op0=ALU.is_equal, op1=ALU.mult, accum_out=S[:, 6, t, 2:3]))
                step(dve.tensor_reduce(S[:, 7, :, 0:1], S[:, 6, :, 0:3], AX.X, ALU.add))
                finish(dve, dve.tensor_tensor(L.perm, bcast(W("iota"), [P, NT, 160], 1), S[:, 7, :, 0:1].broadcast_to([P, NT, 160]),
                                              ALU.is_equal), pe_req, st, n, "perm")
                yield
                dve.wait_ge(*pair.filled(st, n, "xs"))
                ps = pair.view(st, n, "xs")
                step(dve.tensor_copy(L.hid[0:TAIL, 7, P:2 * P], ps[0:TAIL, 512:512 + P]))
                finish(dve, dve.tensor_copy(L.hid[:, 7, 0:P], ps[:, 0:P]), pair, st, n, "xs")
                step(dve.memset(L.att[:, 0, 0:DCONV - 1], 0.0))
                acc = L.att[:, 0, DCONV - 1:DCONV - 1 + TOPK]
                for k in range(NST):
                    b, c = k // 6, 512 * (k % 6 // 3) + TOPK * (k % 3)
                    if k % 6 == 0:
                        dve.wait_ge(*pair.filled(st, n, "scan", b))
                    ps = pair.view(st, n, "scan", b)[:, c:c + TOPK]
                    if k == 0:
                        i = dve.tensor_scalar(acc, ps, sig_c[:, 0:1], None, ALU.mult)
                    else:
                        i = dve.scalar_tensor_tensor(out=acc, in0=ps, scalar=sig_c[:, k:k + 1], in1=acc, op0=ALU.mult, op1=ALU.add)
                    if k % 6 == 5 or k == NST - 1:
                        finish(dve, i, pair, st, n, "scan", b)
                    else:
                        step(i)
                y = L.att[:, 0, 160:160 + TOPK]
                step(dve.tensor_scalar(y, L.att[:, 0, 0:TOPK], W("a_conv", P, 0, 1), None, ALU.mult))
                for j in range(1, DCONV):
                    i = dve.scalar_tensor_tensor(out=y, in0=L.att[:, 0, j:j + TOPK], scalar=W("a_conv", P, j, j + 1), in1=y,
                                                 op0=ALU.mult, op1=ALU.add)
                    finish(dve, i, pe_req, st, n, "conv" if j == DCONV - 1 else ("conv", j))
                yield
                dve.wait_ge(*pair.filled(st, n, "xo"))
                ps = pair.view(st, n, "xo")
                step(dve.tensor_tensor(L.att[:, 1, 0:64], ps[:, 0:64], W("a_bout"), ALU.add))
                finish(dve, dve.tensor_tensor(L.att[0:TAIL, 1, 64:128], ps[0:TAIL, 512:576], W("a_bout", TAIL), ALU.add), pair, st, n, "xo")
                dve.nop().then_inc(*pe_req.inc(st, n, "xo"))
                yield
                dve.wait_ge(*pair.filled(st, n, "back"))
                ps = pair.view(st, n, "back")[:, 0:NT * 64].rearrange("p (t d) -> p t d", t=NT)
                finish(dve, dve.tensor_tensor(L.h[:, :, :], ps, L.h[:, :, :], ALU.add), pair, st, n, "back")

            def ffn0(L):
                st, n = "ffn0", L.n
                yield from layernorm(st, L, "ln", L.h[:, :, :], NT, L.normed[:, 0:NT, :])
                split_tokens(st, L)
                yield
                turned(st, L)
                yield
                yield from gating(st, L, 4, W("f0_gb"), soft=True)
                yield
                dve.wait_ge(*pair.filled(st, n, "s2"))
                dve.tensor_scalar(L.hid[:, 4, :], pair.view(st, n, "s2")[:, 0:512], W("f0_bs2"), 0.0, ALU.add, ALU.max)\
                    .then_inc(*pair.free(st, n, "s2"))
                for a in range(2):
                    dve.wait_ge(*pair.filled(st, n, "e2", a))
                    ps = pair.view(st, n, "e2", a)
                    for j in range(2):
                        e = 2 * a + j
                        i = dve.tensor_scalar(L.att[0:64, e, :], ps[0:64, j * 512:(j + 1) * 512], W("f0_be2", 64, e, e + 1), 0.0, ALU.add, ALU.max)
                    i.then_inc(*pair.free(st, n, "e2", a))
                yield
                combine(st, L, 0, 5, L.h)

            def l1(L):
                yield from layernorm("l1", L, "ln", L.h[:, :, :], NT, L.normed[:, 0:NT, :])
                split_tokens("l1", L)
                yield
                turned("l1", L)
                yield
                zeros(L, 1)

            def ffn1(L):
                st = "ffn1"
                yield from layernorm(st, L, "ln", L.h[:, :, :], NT, L.base[:, :, :])
                yield from layernorm(st, L, "ln2", L.base[:, :, :], NT, L.normed[:, 0:NT, :], W("f1_gam"), W("f1_bet"))
                split_tokens(st, L)
                yield
                turned(st, L)
                yield
                yield from gating(st, L, 8, W("f1_gb"))
                yield
                combine(st, L, 0, 8, L.h)

            def values64(st, L, bias=None):
                dve.wait_ge(*pair.filled(st, L.n, "v", 0))
                ps = pair.view(st, L.n, "v", 0)[:, 0:NT * 64].rearrange("p (t d) -> p t d", t=NT)
                v = L.v64[:, :, 0:64]
                ins = dve.tensor_copy(v, ps) if bias is None else dve.tensor_tensor(v, ps, bcast(bias, [P, NT, 64], 1), ALU.add)
                finish(dve, ins, pair, st, L.n, "v", 0)

            def l2(L):
                st, n, S = "l2", L.n, L.small
                yield from layernorm(st, L, "ln", L.h[:, :, :], NT, L.normed[:, 0:NT, :])
                split_tokens(st, L)
                yield
                turned(st, L)
                yield
                values64(st, L)
                yield
                for a in range(2):
                    dve.wait_ge(*pair.filled(st, n, "s", a))
                    ps = pair.view(st, n, "s", a)[:].rearrange("p (j c) -> p j c", j=2)
                    dve.tensor_reduce(S[:, 10, 2 * a:2 * a + 2, 0:1], ps, AX.X, ALU.max, negate=True).then_inc(*maxima_ready.inc(st, n, a))
                yield
                for a in range(2):
                    dve.wait_ge(*pair.read(st, n, "s", a))
                step(dve.reciprocal(S[:, 11, :, 1:2], S[:, 11, :, 0:1]))
                finish(dve, dve.tensor_tensor(L.v64[:, :, 0:64], L.v64[:, :, 0:64], S[:, 11, :, 1:2].broadcast_to([P, NT, 64]), ALU.mult),
                       v_ready, st, n, "scaled")
                yield
                rows_add(st, L, False)

            def causal(L):
                st, n = "causal", L.n
                yield from layernorm(st, L, "ln", L.h[:, :, :], NT, L.base[:, :, :])
                yield from layernorm(st, L, "rms", L.base[:, :, :], NT, L.normed[:, 0:NT, :], W("c_ln1"), eps=EPS_RMS, centre=False)
                split_tokens(st, L)
                yield
                turned(st, L)
                yield
                step(dve.memset(L.v16, 0.0))
                step(dve.memset(L.v16[:, :, :, 16:17], 1.0))
                if n == 0:
                    step(dve.memset(mc_t[:, :, 0, :, 48:51], 0.0))
                    step(dve.memset(mc_t[:, :, 0, :, 112:115], 0.0))

            def rotate(L, w, g):
                st, n = "causal", L.n
                u = f_units[0]
                f_units[0] += 1
                dve.wait_ge(*split_done(*split_units[u - 2]))
                for j in range(2):
                    key = (st, n, (w, 2 * g + j))
                    f = f_t[:, u % 2, j * 512:(j + 1) * 512]
                    dve.wait_ge(*pair.filled(*key))
                    ps = pair.view(*key)
                    dve.tensor_tensor(prod[:, 0:512], ps[:, 0:512], W("cos"), ALU.mult)
                    finish(dve, dve.tensor_tensor(prod[:, 512:1024], ps[:, 512:1024], W("sin"), ALU.mult), pair, *key)
                    if w == "q":
                        step(dve.tensor_tensor(f, prod[:, 0:512], prod[:, 512:1024], ALU.add))
                    else:
                        step(dve.scalar_tensor_tensor(out=f, in0=prod[:, 0:512], scalar=W("c_bk"), in1=prod[:, 512:1024],
                                                      op0=ALU.add, op1=ALU.add))
                dve.nop().then_inc(*f_ready.inc(st, n, (w, g)))

            def piece(st, L, what):
                if st == "causal" and what[0] == "v":
                    dve.wait_ge(*pair.filled(st, L.n, "v", 0))
                    ps = pair.view(st, L.n, "v", 0)[:, 0:NT * 32].rearrange("p (t h d) -> p t h d", t=NT, h=2)
                    step(dve.tensor_copy(L.v16[:, :, 0:4:2, 0:16], ps))
                    finish(dve, dve.tensor_copy(L.v16[:, :, 1:4:2, 0:16], ps), pair, st, L.n, "v", 0)
                    dve.nop().then_inc(*v_ready.inc(st, L.n, 0))
                elif what[0] == "v":
                    values8(st, L, max(what[1] - 1, 0), what[1], "t_bv" if st == "tok" else None)
                elif st == "causal":
                    rotate(L, *what)

            def piece2(st, L, what):
                split2(W({"q": "c", "k": "d"}[what[0]] + "a2" if st == "causal" else what[0] + "a2"), st, L, what)

            def causal_out(L):
                st, n = "causal", L.n
                dve.wait_ge(*pair.filled(st, n, "wo"))
                ps = pair.view(st, n, "wo")[:, 0:NT * 64].rearrange("p (t d) -> p t d", t=NT)
                finish(dve, dve.tensor_tensor(L.base[:, :, :], ps, L.base[:, :, :], ALU.add), pair, st, n, "wo")
                step(dve.tensor_tensor(L.h[:, :, :], L.h[:, :, :], L.base[:, :, :], ALU.add))

            def ffn2(L):
                st, n = "ffn2", L.n
                yield from layernorm(st, L, "rms", L.base[:, :, :], NT, L.normed[:, 0:NT, :], W("c_ln2"), eps=EPS_RMS, centre=False)
                split_tokens(st, L)
                yield
                turned(st, L)
                yield
                yield from gating(st, L, 8, soft=True, renorm=True)
                yield
                for r in range(2):
                    if r:
                        yield
                        combine(st, L, 0, 4, L.h)
                        yield
                    for c in range(8):
                        dve.wait_ge(*hid_a.at(st, n, r, c))
                        k = 8 * r + c
                        ps = pair.view(st, n, "h", r, c)
                        finish(dve, dve.tensor_tensor(L.hid[0:ROWS2, c, :], ps[0:ROWS2, 512:1024], L.att[0:ROWS2, k % 2, :], ALU.mult),
                               pair, st, n, "h", r, c)
                        dve.nop().then_inc(*hid_v.inc(st, n, r, c))
                yield
                combine(st, L, 1, 4, L.h)

            def l3(L):
                st, n, S = "l3", L.n, L.small
                yield from layernorm(st, L, "ln", L.h[:, :, :], NT, L.normed[:, 0:NT, :])
                split_tokens(st, L)
                yield
                turned(st, L)
                yield
                step(dve.memset(L.m3, 0.0))
                values64(st, L, W("l3_bv"))
                step(dve.memset(L.att[64:65, 1, :], 1.0))
                dve.nop().then_inc(*v_ready.inc(st, n, 0))
                yield
                for a in range(2):
                    dve.wait_ge(*pair.filled(st, n, "m", a))
                    ps = pair.view(st, n, "m", a)[:].rearrange("p (j c) -> p j c", j=2)
                    i = dve.tensor_reduce(L.m3[:, 2 * a:2 * a + 2, 64:65], ps, AX.X, ALU.max, negate=True)
                    finish(dve, i, pair, st, n, "m", a)
                dve.nop().then_inc(*maxima_ready.inc(st, n))
                yield
                dve.wait_ge(*pair.filled(st, n, "wo"))
                ps = pair.view(st, n, "wo")[:, 0:NT * 65].rearrange("p (t d) -> p t d", t=NT)
                step(dve.reciprocal(S[:, 11, :, 1:2], ps[:, :, 64:65]))
                finish(dve, dve.tensor_tensor(L.cent[:, 0:NT, :], ps[:, :, 0:64], S[:, 11, :, 1:2].broadcast_to([P, NT, 64]), ALU.mult),
                       pair, st, n, "wo")
                step(dve.tensor_tensor(L.h[:, :, :], L.h[:, :, :], L.cent[:, 0:NT, :], ALU.add))

            def ffn3(L):
                st, n = "ffn3", L.n
                yield from layernorm(st, L, "ln", L.h[:, :, :], NT, L.normed[:, 0:NT, :])
                step(dve.tensor_copy(L.base[:, :, :], L.normed[:, 0:NT, :]))
                split_tokens(st, L)
                yield
                turned(st, L)
                yield
                yield from gating(st, L, 16, W("f3_gb"))
                yield
                for r in range(2):
                    for a in range(4):
                        e = 2 * a + 1
                        dve.wait_ge(*pair.filled(st, n, ("h", r, a)))
                        if r and a == 0:
                            dve.wait_ge(*pair.filled(st, n, "out", 0, 1))
                        ps = pair.view(st, n, ("h", r, a))
                        dve.tensor_scalar(L.hid[:, e, :], ps[:, 512:1024], W("f3_b1", P, 8 * r + e, 8 * r + e + 1), 0.0, ALU.add, ALU.max)\
                            .then_inc(*pair.free(st, n, ("h", r, a)))
                    yield
                    combine(st, L, r, 8, L.base)
                    yield
                yield from layernorm(st, L, "ln2", L.base[:, :, :], NT, L.normed[:, 0:NT, :], W("f3_gam"), W("f3_bet"))
                finish(dve, dve.tensor_tensor(L.h[:, :, :], L.h[:, :, :], L.normed[:, 0:NT, :], ALU.add), out_ready, n)

            with dve.Fori(0, CLIPS // LANES) as turn:
                for st in STAGES:
                    in_turn([dict(tok=tok, sparse=sparse, ffn0=ffn0, l1=l1, ffn1=ffn1, l2=l2, causal=causal, ffn2=ffn2, l3=l3,
                                  ffn3=ffn3)[st](L) for L in lanes])
                    if st in ATT:
                        attention(st)
                        for L in lanes:
                            if st == "tok":
                                rows_add(st, L, True, t_bo2[:, :])
                            elif st == "l1":
                                rows_add(st, L, False, W("l1_bo"))
                            else:
                                causal_out(L)
                next_turn(dve, "dve")


def whole_array(w):
    import numpy as np
    a = np.zeros((P, WHOLE_N), np.float32)

    def put(name, v, rows=None):
        at, n = WHOLE_AT[name]
        v = np.asarray(v)
        a[0:v.shape[0], at:at + v.shape[1]] = v

    def rows(name, v):
        at, n = WHOLE_AT[name]
        a[:, at:at + n] = np.asarray(v).reshape(1, -1)

    p, c = np.arange(P)[:, None], np.arange(P)[None, :]
    put("ident", (p == c).astype(np.float32))
    rows("ones", np.ones(P, np.float32))
    put("ltmask", (c < p).astype(np.float32))
    rows("iota", np.arange(160, dtype=np.float32))
    rows("iotae", np.arange(16, dtype=np.float32))
    put("negmask", np.where(c > p, np.float32(CAUSAL), np.float32(0)))
    put("negmaskT", np.where(p > c, np.float32(CAUSAL), np.float32(0)))
    inv_freq = 1.0 / 10000.0 ** (np.arange(0, 16, 2, dtype=np.float32) / 16)
    freqs = np.outer(np.arange(TOK, dtype=np.float32), inv_freq)
    emb = np.concatenate([freqs, freqs], axis=-1)
    cos, sin = np.cos(emb).T, np.sin(emb).T
    sin = np.concatenate([-sin[0:8], sin[8:16]])
    for k in range(6):
        for name, t in (("cos", cos), ("sin", sin)):
            at, _ = WHOLE_AT[name]
            a[16 * k:16 * k + 16, at:at + TOK] = t
        for j in range(2):
            r = slice(64 * j + 8 * k, 64 * j + 8 * k + 8)
            a[r, WHOLE_AT["qa1"][0]] = Q_PART[k] >= 2
            a[r, WHOLE_AT["qa2"][0]] = Q_PART[k] == 3
            a[r, WHOLE_AT["ka1"][0]] = K_PART[k] >= 2
            a[r, WHOLE_AT["ka2"][0]] = K_PART[k] == 3
            for g in range(4):
                head = slice((2 * g + j) * 8, (2 * g + j) * 8 + 8)
                a[r, WHOLE_AT["t_bq"][0] + g] = w["L0_tok_bq"][head]
                a[r, WHOLE_AT["t_bk"][0] + g] = w["L0_tok_bk"][head]
        r = slice(16 * k, 16 * k + 16)
        a[r, WHOLE_AT["ca1"][0]] = Q_PART[k] >= 2
        a[r, WHOLE_AT["ca2"][0]] = Q_PART[k] == 3
        a[r, WHOLE_AT["da1"][0]] = K_PART[k] >= 2
        a[r, WHOLE_AT["da2"][0]] = K_PART[k] == 3
    a[1:3, WHOLE_AT["ra1"][0]] = 1
    a[2:3, WHOLE_AT["ra2"][0]] = 1
    for j in range(2):
        r = slice(64 * j + 48, 64 * j + 51)
        a[r, WHOLE_AT["mones8"][0] + j * P:WHOLE_AT["mones8"][0] + (j + 1) * P] = 1
        a[r, WHOLE_AT["t_bk"][0]:WHOLE_AT["t_bk"][0] + 4] = 1
        a[r, WHOLE_AT["l1_bk"][0]:WHOLE_AT["l1_bk"][0] + 4] = 1
    a[96:99, WHOLE_AT["c_bk"][0]] = 1
    for name, v in (("t_g", "L0_tok_ln_g"), ("t_b", "L0_tok_ln_b"), ("t_bv", "L0_tok_bv"), ("t_bo", "L0_tok_bo"),
                    ("a_alpha", "L0_attn_alpha"), ("a_w", "L0_attn_dyt_w"), ("a_b", "L0_attn_dyt_b"), ("a_bin", "L0_attn_b_in"),
                    ("a_wq", "L0_attn_w_q"), ("a_wk", "L0_attn_w_k"), ("a_bq", "L0_attn_b_q"), ("a_bk", "L0_attn_b_k"),
                    ("a_bout", "L0_attn_b_out"), ("f0_gb", "L0_ffn_gb"), ("l1_bo", "L1_attn_b_proj"), ("l1_temp", "L1_attn_temperature"),
                    ("f1_gam", "L1_ffn_gamma"), ("f1_bet", "L1_ffn_beta"), ("f1_gb", "L1_ffn_br"), ("c_ln1", "L2_ffn_ln1_w"),
                    ("c_ln2", "L2_ffn_ln2_w"), ("l3_bv", "L3_attn_bv"), ("l3_scale", "L3_attn_scale"), ("f3_gb", "L3_ffn_gate_b"),
                    ("f3_gam", "L3_ffn_gamma"), ("f3_bet", "L3_ffn_beta")):
        rows(name, w[v])
    put("a_Cp", w["L0_attn_Cp"])
    put("a_A", w["L0_attn_A"])
    put("a_AT", w["L0_attn_A"].T)
    put("a_BpT", w["L0_attn_Bp"].reshape(NST, 1))
    put("a_conv", w["L0_attn_conv_w"][:, 0, :])
    put("a_wout", w["L0_attn_w_out"].T)
    put("f0_bs1", w["L0_ffn_sb1"][:, None])
    put("f0_s2", w["L0_ffn_sW2"])
    put("f0_bs2", w["L0_ffn_sb2"][:, None])
    put("f0_be1", w["L0_ffn_eb1"].T)
    put("f0_e2", w["L0_ffn_eW2"].transpose(1, 0, 2).reshape(P, 256))
    put("f0_be2", w["L0_ffn_eb2"].T)
    put("f0_w3", w["L0_ffn_eW3"].transpose(1, 0, 2).reshape(64, 256))
    a[:, WHOLE_AT["f0_w3"][0] + 256:WHOLE_AT["f0_w3"][0] + 320] = w["L0_ffn_sW3"]
    put("f1_b1", w["L1_ffn_b1"].T)
    put("f1_w2", w["L1_ffn_W2"].transpose(1, 0, 2).reshape(P, 512))
    put("f2_w2", w["L2_ffn_w2"].reshape(8, 64, 2, HALF).transpose(3, 0, 2, 1).reshape(HALF, 1024))
    put("t_wo", w["L0_tok_Wo"].T)
    put("l1_wo", w["L1_attn_w_proj"].T)
    put("c_wo", w["L2_ffn_wo"].T)
    put("l3_bq", w["L3_attn_bq"][:, None])
    put("l3_bk", w["L3_attn_bk"][:, None])
    put("f3_b1", w["L3_ffn_b1"].T)
    put("f3_w2", w["L3_ffn_w2"].transpose(1, 0, 2).reshape(P, 1024))
    return a


def split_array(w):
    import numpy as np
    a = np.zeros((P, SPLIT_N), np.float32)

    def put(name, v):
        at, n = SPLIT_AT[name]
        a[0:64, at:at + n] = v
        a[64:P, at:at + n] = v

    def heads8(name, v):
        t = np.zeros((64, 4, 2, 64), np.float32)
        for k in range(6):
            t[:, :, :, 8 * k:8 * k + 8] = v.T.reshape(64, 4, 2, 8)
        put(name, t.reshape(64, 512))

    def heads16(name, v, repeat, swap):
        t = np.zeros((64, 4, P), np.float32)
        u = v.T.reshape(64, 4 // repeat, 16)
        if swap:
            u = np.concatenate([u[:, :, 8:16], u[:, :, 0:8]], axis=2)
        for k in range(6):
            t[:, :, 16 * k:16 * k + 16] = np.repeat(u, repeat, axis=1)
        put(name, t.reshape(64, 512))

    def experts(name, v):
        put(name, v.transpose(1, 0, 2).reshape(64, -1))

    heads8("t_q", w["L0_tok_Wq"])
    heads8("t_k", w["L0_tok_Wk"])
    put("t_v", w["L0_tok_Wv"].T)
    put("a_in", w["L0_attn_w_in"].T)
    put("f0_s1", w["L0_ffn_sW1"])
    experts("f0_e1", w["L0_ffn_eW1"])
    put("f0_g", w["L0_ffn_gW"])
    heads8("l1_q", w["L1_attn_w_qkv"][0:64])
    heads8("l1_k", w["L1_attn_w_qkv"][64:128])
    put("l1_v", w["L1_attn_w_qkv"][128:192].T)
    put("f1_g", w["L1_ffn_Wr"])
    experts("f1_w1", w["L1_ffn_W1"])
    for k, name in (("q", "Wq"), ("k", "Wk"), ("v", "Wv")):
        put("l2_" + k, w["L2_attn_" + name].T)
        put("l3_" + k, w["L3_attn_" + name].T)
    heads16("c_q", w["L2_ffn_wq"], 1, False)
    heads16("c_qs", w["L2_ffn_wq"], 1, True)
    heads16("c_k", w["L2_ffn_wk"], 2, False)
    heads16("c_ks", w["L2_ffn_wk"], 2, True)
    put("c_v", w["L2_ffn_wv"].T)
    put("f2_g", w["L2_ffn_router_w"].T)
    for name, v in (("f2_w1", w["L2_ffn_w1"]), ("f2_w3", w["L2_ffn_w3"])):
        t = np.zeros((64, 16, ROWS2), np.float32)
        t[:, :, 0:HALF] = v.reshape(16, HALF, 64).transpose(2, 0, 1)
        put(name, t.reshape(64, -1))
    put("f3_g", w["L3_ffn_gate_w"])
    experts("f3_w1", w["L3_ffn_w1"])
    return a


def bias_array(w):
    import numpy as np
    a = np.zeros((3, BIAS_N), np.float32)
    at = BIAS_AT["f0_b3"][0]
    a[:, at:at + 256] = w["L0_ffn_eb3"].reshape(1, 256)
    a[:, at + 256:at + 320] = w["L0_ffn_sb3"].reshape(1, 64)
    for name, v in (("f1_b2", w["L1_ffn_b2"]), ("f3_b2", w["L3_ffn_b2"])):
        at, n = BIAS_AT[name]
        a[:, at:at + n] = v.reshape(1, n)
    return a


def kernel(**inputs):
    import numpy as np
    import concourse.bacc as bacc
    from concourse.bass_utils import run_bass_kernel_spmd as run

    w = {k: np.asarray(v) for k, v in inputs.items()}
    arrays = {"in_x": np.ascontiguousarray(w["x"]), "in_split": split_array(w), "in_whole": whole_array(w), "in_bias": bias_array(w)}
    known = {}
    for _ in range(2):
        nc = bacc.Bacc("TRN2", target_bir_lowering=False, num_devices=1)
        noted = {}
        args = [nc.dram_tensor(n, a.shape, F32, kind="ExternalInput").ap() for n, a in arrays.items()]
        skew = nc.dram_tensor("skew", (NST, P * SKEW), F32, kind="Internal").ap()
        out = nc.dram_tensor("out", (CLIPS, TOK, DIM), F32, kind="ExternalOutput").ap()
        audio_tower(nc, args[0], args[1], args[2], args[3], skew, out, known, noted)
        known = noted
    r = run(nc, [arrays], core_ids=[0])
    return r.results[0]["out"]
```
